# Optimizing a Trainium2 kernel written in Bass

```python
import numpy as np
import jax
import jax.numpy as jnp

def _softmax(x, axis=-1):
    return jax.nn.softmax(x, axis=axis)

def _gelu(x):
    return jax.nn.gelu(x, approximate=True)

def _silu(x):
    return jax.nn.silu(x)

def _sigmoid(x):
    return jax.nn.sigmoid(x)

def _layernorm(x, axis=-1, eps=1e-05):
    m = jnp.mean(x, axis=axis, keepdims=True)
    v = jnp.var(x, axis=axis, keepdims=True)
    return (x - m) / jnp.sqrt(v + eps)

def _scatter_add(tgt, idx, src, axis=0):
    return tgt.at[idx].add(src)

def _segment_sum(src, seg, n):
    return jax.ops.segment_sum(src, seg, n)
kernel_name = 'mk_adaln_d2_jaxref_r4_2d0556'

def setup_inputs(seed: int=0):
    np.random.seed(seed)
    _w = jnp.asarray

    def _L0_attn_setup():
        import jax, jax.numpy as jnp
        import numpy as np
        EMBED_DIM = 256
        NUM_HEADS = 16
        HEAD_DIM = EMBED_DIM // NUM_HEADS
        LORA_R = 8
        ALPHA = 1.0
        B, S = (2, 512)

        def lora_linear(x, W, b, A, Bm):
            return x @ W.T + b + x @ A.T @ Bm.T * (ALPHA / LORA_R)
        key = jax.random.key(seed)
        ks = jax.random.split(key, 20)
        d = {'x': jax.random.normal(ks[0], (B, S, EMBED_DIM), dtype=jnp.float32)}
        names = ['q', 'k', 'v', 'o']
        i = 1
        for n in names:
            d['W' + n] = jax.random.normal(ks[i], (EMBED_DIM, EMBED_DIM), jnp.float32) * 0.02
            i += 1
            d['b' + n] = jnp.zeros((EMBED_DIM,), jnp.float32)
            d['A' + n] = jax.random.normal(ks[i], (LORA_R, EMBED_DIM), jnp.float32) * 0.02
            i += 1
            d['B' + n] = jax.random.normal(ks[i], (EMBED_DIM, LORA_R), jnp.float32) * 0.02
            i += 1
        d['rezero'] = jnp.zeros((1,), jnp.float32) + 0.1
        return d
    _L0_attn_in = _L0_attn_setup()

    def _L0_ffn_setup():
        import jax, jax.numpy as jnp
        import numpy as np
        D_MODEL = 256
        D_FF = 1024
        N_EXPERTS = 8
        TOP_K = 2
        D_FF_PER = D_FF // N_EXPERTS
        B, T = (4, 512)
        key = jax.random.key(seed)
        ks = jax.random.split(key, 7)
        b1_bound = 1.0 / np.sqrt(D_MODEL)
        b2_bound = 1.0 / np.sqrt(D_FF_PER)
        return {'x': jax.random.normal(ks[0], (B, T, D_MODEL), dtype=jnp.float32), 'router_w': jax.random.uniform(ks[1], (D_MODEL, N_EXPERTS), minval=-b1_bound, maxval=b1_bound, dtype=jnp.float32), 'router_b': jax.random.uniform(ks[2], (N_EXPERTS,), minval=-b1_bound, maxval=b1_bound, dtype=jnp.float32), 'W1': jax.random.uniform(ks[3], (N_EXPERTS, D_MODEL, D_FF_PER), minval=-b1_bound, maxval=b1_bound, dtype=jnp.float32), 'b1': jax.random.uniform(ks[4], (N_EXPERTS, D_FF_PER), minval=-b1_bound, maxval=b1_bound, dtype=jnp.float32), 'W2': jax.random.uniform(ks[5], (N_EXPERTS, D_FF_PER, D_MODEL), minval=-b2_bound, maxval=b2_bound, dtype=jnp.float32), 'b2': jax.random.uniform(ks[6], (N_EXPERTS, D_MODEL), minval=-b2_bound, maxval=b2_bound, dtype=jnp.float32)}
    _L0_ffn_in = _L0_ffn_setup()
    _L0_c = _w((lambda *s: np.random.randn(*s).astype(np.float32) * 0.05)(4, 256))
    _L0_wmod = _w((lambda *s: np.random.randn(*s).astype(np.float32) * 0.05)(256, 6 * 256) * 256 ** (-0.5))

    def _L1_attn_setup():
        import jax, jax.numpy as jnp
        import numpy as np
        DIM = 256
        D_STATE = 64
        D_CONV = 4
        EXPAND = 2
        HEADDIM = 128
        NGROUPS = 1
        D_INNER = EXPAND * DIM
        NHEADS = D_INNER // HEADDIM
        CONV_DIM = D_INNER + 2 * NGROUPS * D_STATE
        D_IN_PROJ = 2 * D_INNER + 2 * NGROUPS * D_STATE + NHEADS
        CHUNK = 64
        BATCH = 2
        SEQLEN = 1024
        LN_EPS = 1e-05
        RMS_EPS = 1e-05

        def l2norm(w, eps=1e-06):
            n = jnp.linalg.norm(w, axis=-1, keepdims=True)
            return w / jnp.maximum(n, eps)

        def layernorm(x, w, b, eps=LN_EPS):
            mu = jnp.mean(x, axis=-1, keepdims=True)
            var = jnp.mean(jnp.square(x - mu), axis=-1, keepdims=True)
            return (x - mu) * jax.lax.rsqrt(var + eps) * w + b

        def _ssd_chunk_scan(x, dt, A, B, C):
            b, l, h, p = x.shape
            n = B.shape[-1]
            c = l // CHUNK
            xc = x.reshape(b, c, CHUNK, h, p)
            Bc = B.reshape(b, c, CHUNK, n)
            Cc = C.reshape(b, c, CHUNK, n)
            dtc = dt.reshape(b, c, CHUNK, h)
            dA = dtc * A
            cum = jnp.cumsum(dA, axis=2)
            seg = cum[:, :, :, None, :] - cum[:, :, None, :, :]
            tri = jnp.tril(jnp.ones((CHUNK, CHUNK), dtype=bool))
            decay = jnp.where(tri[None, None, :, :, None], jnp.exp(seg), 0.0)
            scores = jnp.einsum('bcin,bcjn->bcij', Cc, Bc)
            att = scores[..., None] * decay * dtc[:, :, None, :, :]
            y_intra = jnp.einsum('bcijh,bcjhp->bcihp', att, xc)
            decay_to_end = jnp.exp(cum[:, :, -1:, :] - cum)
            states = jnp.einsum('bcln,bclh,bclhp->bchpn', Bc, dtc * decay_to_end, xc)
            chunk_decay = jnp.exp(cum[:, :, -1, :])

            def step(carry, inp):
                st, dec = inp
                new = carry * dec[:, :, None, None] + st
                return (new, carry)
            init = jnp.zeros((b, h, p, n), dtype=x.dtype)
            _, prev = jax.lax.scan(step, init, (jnp.moveaxis(states, 1, 0), jnp.moveaxis(chunk_decay, 1, 0)))
            prev_states = jnp.moveaxis(prev, 0, 1)
            y_inter = jnp.einsum('bcln,bclh,bchpn->bclhp', Cc, jnp.exp(cum), prev_states)
            return (y_intra + y_inter).reshape(b, l, h, p)
        key = jax.random.key(seed)
        ks = jax.random.split(key, 8)
        u = jax.random.normal(ks[0], (BATCH, SEQLEN, DIM), dtype=jnp.float32)
        in_proj_w = jax.random.normal(ks[1], (D_IN_PROJ, DIM), dtype=jnp.float32)
        conv_w = jax.random.normal(ks[2], (CONV_DIM, D_CONV), dtype=jnp.float32) * 0.2
        conv_b = jnp.zeros((CONV_DIM,), dtype=jnp.float32)
        dt = jnp.exp(jax.random.uniform(ks[3], (NHEADS,)) * (np.log(0.1) - np.log(0.001)) + np.log(0.001))
        dt_bias = dt + jnp.log(-jnp.expm1(-dt))
        A_log = jnp.log(jax.random.uniform(ks[4], (NHEADS,), minval=1.0, maxval=16.0))
        D = jnp.ones((NHEADS,), dtype=jnp.float32)
        x_norm_w = jnp.ones((DIM,), dtype=jnp.float32)
        x_norm_b = jnp.zeros((DIM,), dtype=jnp.float32)
        rms_w = jnp.ones((D_INNER,), dtype=jnp.float32)
        out_proj_w = jax.random.normal(ks[5], (DIM, D_INNER), dtype=jnp.float32)
        return {'u': u, 'in_proj_w': in_proj_w, 'conv_w': conv_w, 'conv_b': conv_b, 'dt_bias': dt_bias, 'A_log': A_log, 'D': D, 'x_norm_w': x_norm_w, 'x_norm_b': x_norm_b, 'rms_w': rms_w, 'out_proj_w': out_proj_w}
    _L1_attn_in = _L1_attn_setup()

    def _L1_ffn_setup():
        import jax, jax.numpy as jnp
        import numpy as np
        B, S, D, H, E = (8, 512, 256, 1024, 16)
        key = jax.random.key(seed)
        ks = jax.random.split(key, 4)
        sd = 1.0 / np.sqrt(D).astype(np.float32)
        sh = 1.0 / np.sqrt(H).astype(np.float32)
        return {'x': jax.random.normal(ks[0], (B, S, D), jnp.float32), 'Wg': jax.random.normal(ks[1], (D, E), jnp.float32) * sd, 'bg': jnp.zeros((E,), jnp.float32), 'W1': jax.random.normal(ks[2], (E, D, H), jnp.float32) * sd, 'b1': jnp.zeros((E, H), jnp.float32), 'W2': jax.random.normal(ks[3], (E, H, D), jnp.float32) * sh, 'b2': jnp.zeros((E, D), jnp.float32)}
    _L1_ffn_in = _L1_ffn_setup()
    _L1_c = _w((lambda *s: np.random.randn(*s).astype(np.float32) * 0.05)(4, 256))
    _L1_wmod = _w((lambda *s: np.random.randn(*s).astype(np.float32) * 0.05)(256, 6 * 256) * 256 ** (-0.5))
    _d = {'L0_attn_x': _L0_attn_in['x'], 'L0_attn_Wq': _L0_attn_in['Wq'], 'L0_attn_bq': _L0_attn_in['bq'], 'L0_attn_Aq': _L0_attn_in['Aq'], 'L0_attn_Bq': _L0_attn_in['Bq'], 'L0_attn_Wk': _L0_attn_in['Wk'], 'L0_attn_bk': _L0_attn_in['bk'], 'L0_attn_Ak': _L0_attn_in['Ak'], 'L0_attn_Bk': _L0_attn_in['Bk'], 'L0_attn_Wv': _L0_attn_in['Wv'], 'L0_attn_bv': _L0_attn_in['bv'], 'L0_attn_Av': _L0_attn_in['Av'], 'L0_attn_Bv': _L0_attn_in['Bv'], 'L0_attn_Wo': _L0_attn_in['Wo'], 'L0_attn_bo': _L0_attn_in['bo'], 'L0_attn_Ao': _L0_attn_in['Ao'], 'L0_attn_Bo': _L0_attn_in['Bo'], 'L0_attn_rezero': _L0_attn_in['rezero'], 'L0_ffn_router_w': _L0_ffn_in['router_w'], 'L0_ffn_router_b': _L0_ffn_in['router_b'], 'L0_ffn_W1': _L0_ffn_in['W1'], 'L0_ffn_b1': _L0_ffn_in['b1'], 'L0_ffn_W2': _L0_ffn_in['W2'], 'L0_ffn_b2': _L0_ffn_in['b2'], 'L0_c': _L0_c, 'L0_wmod': _L0_wmod, 'L1_attn_in_proj_w': _L1_attn_in['in_proj_w'], 'L1_attn_conv_w': _L1_attn_in['conv_w'], 'L1_attn_conv_b': _L1_attn_in['conv_b'], 'L1_attn_dt_bias': _L1_attn_in['dt_bias'], 'L1_attn_A_log': _L1_attn_in['A_log'], 'L1_attn_D': _L1_attn_in['D'], 'L1_attn_x_norm_w': _L1_attn_in['x_norm_w'], 'L1_attn_x_norm_b': _L1_attn_in['x_norm_b'], 'L1_attn_rms_w': _L1_attn_in['rms_w'], 'L1_attn_out_proj_w': _L1_attn_in['out_proj_w'], 'L1_ffn_Wg': _L1_ffn_in['Wg'], 'L1_ffn_bg': _L1_ffn_in['bg'], 'L1_ffn_W1': _L1_ffn_in['W1'], 'L1_ffn_b1': _L1_ffn_in['b1'], 'L1_ffn_W2': _L1_ffn_in['W2'], 'L1_ffn_b2': _L1_ffn_in['b2'], 'L1_c': _L1_c, 'L1_wmod': _L1_wmod}
    _x0 = _d['L0_attn_x']
    _d['L0_attn_x'] = jax.random.normal(jax.random.fold_in(jax.random.key(seed), 1), (4, 2048, 256), dtype=_x0.dtype)
    del _x0
    return _d

def reference(L0_attn_x, L0_attn_Wq, L0_attn_bq, L0_attn_Aq, L0_attn_Bq, L0_attn_Wk, L0_attn_bk, L0_attn_Ak, L0_attn_Bk, L0_attn_Wv, L0_attn_bv, L0_attn_Av, L0_attn_Bv, L0_attn_Wo, L0_attn_bo, L0_attn_Ao, L0_attn_Bo, L0_attn_rezero, L0_ffn_router_w, L0_ffn_router_b, L0_ffn_W1, L0_ffn_b1, L0_ffn_W2, L0_ffn_b2, L0_c, L0_wmod, L1_attn_in_proj_w, L1_attn_conv_w, L1_attn_conv_b, L1_attn_dt_bias, L1_attn_A_log, L1_attn_D, L1_attn_x_norm_w, L1_attn_x_norm_b, L1_attn_rms_w, L1_attn_out_proj_w, L1_ffn_Wg, L1_ffn_bg, L1_ffn_W1, L1_ffn_b1, L1_ffn_W2, L1_ffn_b2, L1_c, L1_wmod):

    def _L0_attn_ref(x, Wq, bq, Aq, Bq, Wk, bk, Ak, Bk, Wv, bv, Av, Bv, Wo, bo, Ao, Bo, rezero):
        import jax, jax.numpy as jnp
        import numpy as np
        EMBED_DIM = 256
        NUM_HEADS = 16
        HEAD_DIM = EMBED_DIM // NUM_HEADS
        LORA_R = 8
        ALPHA = 1.0
        B, S = (2, 512)

        def lora_linear(x, W, b, A, Bm):
            return x @ W.T + b + x @ A.T @ Bm.T * (ALPHA / LORA_R)
        bsz, seq_len, _ = x.shape
        Q = lora_linear(x, Wq, bq, Aq, Bq).reshape(bsz, seq_len, NUM_HEADS, HEAD_DIM)
        K = lora_linear(x, Wk, bk, Ak, Bk).reshape(bsz, seq_len, NUM_HEADS, HEAD_DIM)
        V = lora_linear(x, Wv, bv, Av, Bv).reshape(bsz, seq_len, NUM_HEADS, HEAD_DIM)
        scores = jnp.einsum('bqhd,bkhd->bhqk', Q, K) / np.sqrt(HEAD_DIM).astype(np.float32)
        slopes = 0.5 ** jnp.arange(NUM_HEADS, dtype=jnp.float32)
        pos = jnp.arange(seq_len, dtype=jnp.float32)
        rel = pos[None, :] - pos[:, None]
        scores = scores + slopes[None, :, None, None] * rel[None, None, :, :]
        attn = jax.nn.softmax(scores, axis=-1)
        out = jnp.einsum('bhqk,bkhd->bqhd', attn, V).reshape(bsz, seq_len, EMBED_DIM)
        out = lora_linear(out, Wo, bo, Ao, Bo)
        return x + rezero * out

    def _L0_ffn_ref(x, router_w, router_b, W1, b1, W2, b2):
        import jax, jax.numpy as jnp
        import numpy as np
        D_MODEL = 256
        D_FF = 1024
        N_EXPERTS = 8
        TOP_K = 2
        D_FF_PER = D_FF // N_EXPERTS
        B, T = (4, 512)
        router_logits = x @ router_w + router_b
        routing_weights = jax.nn.softmax(router_logits, axis=-1)
        top_k_weights, top_k_indices = jax.lax.top_k(routing_weights, TOP_K)
        top_k_weights = top_k_weights / jnp.sum(top_k_weights, axis=-1, keepdims=True)
        routing_mask = jnp.zeros_like(routing_weights)
        routing_mask = jnp.take_along_axis(routing_mask, top_k_indices, axis=-1)
        b_idx = jnp.arange(x.shape[0])[:, None, None]
        t_idx = jnp.arange(x.shape[1])[None, :, None]
        routing_mask = jnp.zeros_like(routing_weights).at[b_idx, t_idx, top_k_indices].set(top_k_weights)
        h1 = jnp.einsum('btd,nde->btne', x, W1) + b1
        h1 = jax.nn.gelu(h1, approximate=False)
        out_per_expert = jnp.einsum('btne,nef->btnf', h1, W2) + b2
        output = jnp.sum(out_per_expert * routing_mask[..., None], axis=-2)
        return output

    def _L1_attn_ref(u, in_proj_w, conv_w, conv_b, dt_bias, A_log, D, x_norm_w, x_norm_b, rms_w, out_proj_w):
        import jax, jax.numpy as jnp
        import numpy as np
        DIM = 256
        D_STATE = 64
        D_CONV = 4
        EXPAND = 2
        HEADDIM = 128
        NGROUPS = 1
        D_INNER = EXPAND * DIM
        NHEADS = D_INNER // HEADDIM
        CONV_DIM = D_INNER + 2 * NGROUPS * D_STATE
        D_IN_PROJ = 2 * D_INNER + 2 * NGROUPS * D_STATE + NHEADS
        CHUNK = 64
        BATCH = 2
        SEQLEN = 1024
        LN_EPS = 1e-05
        RMS_EPS = 1e-05

        def l2norm(w, eps=1e-06):
            n = jnp.linalg.norm(w, axis=-1, keepdims=True)
            return w / jnp.maximum(n, eps)

        def layernorm(x, w, b, eps=LN_EPS):
            mu = jnp.mean(x, axis=-1, keepdims=True)
            var = jnp.mean(jnp.square(x - mu), axis=-1, keepdims=True)
            return (x - mu) * jax.lax.rsqrt(var + eps) * w + b

        def _ssd_chunk_scan(x, dt, A, B, C):
            b, l, h, p = x.shape
            n = B.shape[-1]
            c = l // CHUNK
            xc = x.reshape(b, c, CHUNK, h, p)
            Bc = B.reshape(b, c, CHUNK, n)
            Cc = C.reshape(b, c, CHUNK, n)
            dtc = dt.reshape(b, c, CHUNK, h)
            dA = dtc * A
            cum = jnp.cumsum(dA, axis=2)
            seg = cum[:, :, :, None, :] - cum[:, :, None, :, :]
            tri = jnp.tril(jnp.ones((CHUNK, CHUNK), dtype=bool))
            decay = jnp.where(tri[None, None, :, :, None], jnp.exp(seg), 0.0)
            scores = jnp.einsum('bcin,bcjn->bcij', Cc, Bc)
            att = scores[..., None] * decay * dtc[:, :, None, :, :]
            y_intra = jnp.einsum('bcijh,bcjhp->bcihp', att, xc)
            decay_to_end = jnp.exp(cum[:, :, -1:, :] - cum)
            states = jnp.einsum('bcln,bclh,bclhp->bchpn', Bc, dtc * decay_to_end, xc)
            chunk_decay = jnp.exp(cum[:, :, -1, :])

            def step(carry, inp):
                st, dec = inp
                new = carry * dec[:, :, None, None] + st
                return (new, carry)
            init = jnp.zeros((b, h, p, n), dtype=x.dtype)
            _, prev = jax.lax.scan(step, init, (jnp.moveaxis(states, 1, 0), jnp.moveaxis(chunk_decay, 1, 0)))
            prev_states = jnp.moveaxis(prev, 0, 1)
            y_inter = jnp.einsum('bcln,bclh,bchpn->bclhp', Cc, jnp.exp(cum), prev_states)
            return (y_intra + y_inter).reshape(b, l, h, p)
        b, l, _ = u.shape
        u = layernorm(u, x_norm_w, x_norm_b)
        zxbcdt = jnp.einsum('bld,od->blo', u, l2norm(in_proj_w)) * DIM ** (-0.5)
        z = zxbcdt[..., :D_INNER]
        xBC = zxbcdt[..., D_INNER:D_INNER + CONV_DIM]
        dt_raw = zxbcdt[..., D_INNER + CONV_DIM:]
        xt = jnp.transpose(xBC, (0, 2, 1))
        xt = jax.lax.conv_general_dilated(xt, conv_w[:, None, :], window_strides=(1,), padding=[(D_CONV - 1, 0)], feature_group_count=CONV_DIM, dimension_numbers=('NCH', 'OIH', 'NCH'))
        xt = xt + conv_b[None, :, None]
        xBC = jnp.transpose(jax.nn.silu(xt), (0, 2, 1))
        x = xBC[..., :D_INNER].reshape(b, l, NHEADS, HEADDIM)
        B = xBC[..., D_INNER:D_INNER + NGROUPS * D_STATE]
        C = xBC[..., D_INNER + NGROUPS * D_STATE:]
        dt = jax.nn.softplus(dt_raw + dt_bias)
        A = -jnp.exp(A_log)
        y = _ssd_chunk_scan(x, dt, A, B, C)
        y = y + D[None, None, :, None] * x
        y = y.reshape(b, l, D_INNER)
        g = y * jax.nn.silu(z)
        g = g * jax.lax.rsqrt(jnp.mean(jnp.square(g), axis=-1, keepdims=True) + RMS_EPS) * rms_w
        out = jnp.einsum('bld,od->blo', g, l2norm(out_proj_w))
        return out

    def _L1_ffn_ref(x, Wg, bg, W1, b1, W2, b2):
        import jax, jax.numpy as jnp
        import numpy as np
        B, S, D, H, E = (8, 512, 256, 1024, 16)
        d = x.shape[-1]
        xf = x.reshape(-1, d)
        n_tok = xf.shape[0]
        n_exp = Wg.shape[1]
        cap = -(-n_tok // n_exp)
        score = jax.nn.softmax(xf @ Wg + bg, axis=-1)
        gate = jnp.max(score, axis=-1)
        idx = jnp.argmax(score, axis=-1)
        onehot = jax.nn.one_hot(idx, n_exp, dtype=jnp.int32)
        pos = jnp.sum((jnp.cumsum(onehot, axis=0) - 1) * onehot, axis=-1)
        keep = pos < cap
        safe_pos = jnp.where(keep, pos, cap - 1)
        buf = jnp.zeros((n_exp, cap, d), x.dtype).at[idx, safe_pos].add(jnp.where(keep[:, None], xf, 0.0))
        h = jax.nn.relu(jnp.einsum('ecd,edh->ech', buf, W1) + b1[:, None, :])
        y = jnp.einsum('ech,ehd->ecd', h, W2) + b2[:, None, :]
        out = y[idx, safe_pos] * gate[:, None]
        out = jnp.where(keep[:, None], out, 0.0)
        return out.reshape(x.shape)
    x = L0_attn_x
    mod = (_silu(L0_c) @ L0_wmod).reshape(L0_c.shape[0], 6, 1, -1)
    sa, ca, ga, sb, cb, gb = (mod[:, 0], mod[:, 1], mod[:, 2], mod[:, 3], mod[:, 4], mod[:, 5])
    ga = (2 * (ga >= 0) - 1) * jnp.maximum(jnp.abs(ga), 0.25)
    gb = (2 * (gb >= 0) - 1) * jnp.maximum(jnp.abs(gb), 0.25)
    h = _layernorm(x, axis=-1) * (1 + ca) + sa
    x = x + ga * _L0_attn_ref(h, L0_attn_Wq, L0_attn_bq, L0_attn_Aq, L0_attn_Bq, L0_attn_Wk, L0_attn_bk, L0_attn_Ak, L0_attn_Bk, L0_attn_Wv, L0_attn_bv, L0_attn_Av, L0_attn_Bv, L0_attn_Wo, L0_attn_bo, L0_attn_Ao, L0_attn_Bo, L0_attn_rezero)
    h = _layernorm(x, axis=-1) * (1 + cb) + sb
    x = x + gb * _L0_ffn_ref(h, L0_ffn_router_w, L0_ffn_router_b, L0_ffn_W1, L0_ffn_b1, L0_ffn_W2, L0_ffn_b2)
    mod = (_silu(L1_c) @ L1_wmod).reshape(L1_c.shape[0], 6, 1, -1)
    sa, ca, ga, sb, cb, gb = (mod[:, 0], mod[:, 1], mod[:, 2], mod[:, 3], mod[:, 4], mod[:, 5])
    ga = (2 * (ga >= 0) - 1) * jnp.maximum(jnp.abs(ga), 0.25)
    gb = (2 * (gb >= 0) - 1) * jnp.maximum(jnp.abs(gb), 0.25)
    h = _layernorm(x, axis=-1) * (1 + ca) + sa
    x = x + ga * _L1_attn_ref(h, L1_attn_in_proj_w, L1_attn_conv_w, L1_attn_conv_b, L1_attn_dt_bias, L1_attn_A_log, L1_attn_D, L1_attn_x_norm_w, L1_attn_x_norm_b, L1_attn_rms_w, L1_attn_out_proj_w)
    h = _layernorm(x, axis=-1) * (1 + cb) + sb
    x = x + gb * _L1_ffn_ref(h, L1_ffn_Wg, L1_ffn_bg, L1_ffn_W1, L1_ffn_b1, L1_ffn_W2, L1_ffn_b2)
    return x

_drawn_inputs = setup_inputs


def setup_inputs(seed=0):
    import zlib

    import numpy as np

    out = dict(_drawn_inputs(seed))
    spreads = {'L0_attn_bq': (0.0, 0.8),
     'L0_attn_bk': (0.0, 0.8),
     'L0_attn_bv': (0.0, 0.8),
     'L0_attn_bo': (0.0, 0.8),
     'L1_attn_conv_b': (0.0, 0.1),
     'L1_attn_D': (1.0, 0.6),
     'L1_attn_x_norm_w': (1.0, 0.6),
     'L1_attn_x_norm_b': (0.0, 0.566),
     'L1_attn_rms_w': (1.0, 0.572),
     'L1_ffn_bg': (0.0, 0.408),
     'L1_ffn_b1': (0.0, 0.8),
     'L1_ffn_b2': (0.0, 0.8)}
    factors = {'L0_attn_Wq': 8.0,
     'L0_attn_Aq': 8.0,
     'L0_attn_Bq': 8.0,
     'L0_attn_Wk': 8.0,
     'L0_attn_Ak': 8.0,
     'L0_attn_Bk': 8.0,
     'L0_attn_Wv': 8.0,
     'L0_attn_Av': 8.0,
     'L0_attn_Bv': 8.0,
     'L0_attn_Wo': 8.0,
     'L0_attn_Ao': 8.0,
     'L0_attn_Bo': 8.0,
     'L0_ffn_router_b': 7.854,
     'L0_ffn_b1': 8.0,
     'L0_ffn_b2': 5.729,
     'L1_attn_dt_bias': 8.0,
     'L1_attn_A_log': 8.0}
    for name, (base, spread) in spreads.items():
        noise = np.random.default_rng([zlib.crc32(name.encode()), seed]).standard_normal(out[name].shape)
        drawn = base * np.exp(spread * noise) if base else spread * noise
        out[name] = jnp.asarray(drawn.astype(out[name].dtype))
    for name, factor in factors.items():
        out[name] = (out[name] * factor).astype(out[name].dtype)
    return out
```

```python
from contextlib import ExitStack

import numpy as np

import concourse.bass as bass
from concourse import mybir

F32 = mybir.dt.float32
BF16 = mybir.dt.bfloat16
U32 = mybir.dt.uint32
I32 = mybir.dt.int32
ALU = mybir.AluOpType
ACT = mybir.ActivationFunctionType
AX = mybir.AxisListType
ds = bass.ds

P = 128
B, S, D = 4, 2048, 256
N = B * S
KD = D // P
T = 512
SUB = T // P
CPB = S // T
NCH = N // T
EPS = 1e-5

H, HD = 16, 16
HPG = 4
G = H // HPG
UNITS = B * G
KT = S // P
LORA = 8
BANDS = [(0, 0), (0, 1), (1, 0), (1, 1), (0, 2), (2, 0)]
SROWS = 16 * len(BANDS)
ALI = SROWS
MXR = SROWS + 2
QROWS = SROWS + 4

E0, F0 = 8, 128
NH, HP, NS = 4, 128, 64
DI = NH * HP
CONV = DI + 2 * NS
CTL = CONV // P
TAPS = 4
E1, F1 = 16, 1024
CAP = N // E1

R_GCA, R_GSA, R_GRZ, R_GB0, R_CA1, R_SA1, R_GA1, R_CB1, R_SB1, R_GB1 = range(10)
NROWS = 10


def wait_alone(eng, sem, value, always):
    eng.wait_ge(always, 1)
    eng.wait_ge(sem, value)


def phase_semaphores(nc, ctx, prefix):
    mine = []

    def sem(name):
        mine.append(nc.alloc_semaphore(prefix + name))
        return mine[-1]

    def give_back():
        nc.clear_and_free_semaphores(mine)
        nc.all_engine_barrier()

    ctx.callback(give_back)
    return sem


def setup_phase(nc, x, d, keep):
    ctx = ExitStack()
    with ctx:
        sb = lambda name, shape, dt=F32: ctx.enter_context(nc.sbuf_tensor("su_" + name, shape, dt))
        cT = sb("cT", [P, KD, 2, B])
        silu_c = sb("silu_c", [P, KD, 2, B])
        wmod = sb("wmod", [P, 2, KD, 6 * D])
        lora_a = sb("lora_a", [LORA, 4, D])
        lora_b = sb("lora_b", [LORA, 4, D])
        wT = sb("wT", [P, 4, KD, D])
        modr = sb("modr", [B, 2, 6, D])
        rows = sb("rows", [B, NROWS, D])
        sgn = sb("sgn", [B, 4, D])
        mag = sb("mag", [B, 4, D])
        bo = sb("bo", [B, D])
        rz = sb("rz", [B, 1])
        bqk = sb("bqk", [P, G])
        ps = [ctx.enter_context(nc.psum_tensor(f"su_ps{i}", [P, 512], F32)) for i in range(8)]
        sem = phase_semaphores(nc, ctx, "su_")
        loaded, c_loaded = sem("loaded"), sem("c_loaded")
        silu_done, lora_done, mod0_done, mod1_done = sem("silu_done"), sem("lora_done"), sem("mod0_done"), sem("mod1_done")
        lora_read, rows_done, stored = sem("lora_read"), sem("rows_done"), sem("stored")
        nload = 0

        with nc.Block() as block:
            @block.sync
            def _(sp):
                sp.dma_start(cT[:, :, 0, :], x["c0T"].rearrange("(k p) b -> p k b", p=P)).then_inc(c_loaded, 16)
                sp.dma_start(cT[:, :, 1, :], x["c1T"].rearrange("(k p) b -> p k b", p=P)).then_inc(c_loaded, 16)
                for n, w in enumerate("qkvo"):
                    sp.dma_start(lora_a[:, n, :], x["A" + w]).then_inc(loaded, 16)
                    sp.dma_start(lora_b[:, n, :], x["B" + w + "T"]).then_inc(loaded, 16)
                    sp.dma_start(wT[:, n, :, :], x["W" + w + "T"].rearrange("(k p) n -> p k n", p=P)).then_inc(loaded, 16)
                for l in range(2):
                    sp.dma_start(wmod[:, l, :, :], x[f"wmod{l}"].rearrange("(k p) n -> p k n", p=P)).then_inc(loaded, 16)
                sp.dma_start(bo[:, :], x["bo"].partition_broadcast(B)).then_inc(loaded, 16)
                sp.dma_start(rz[:, :], x["rezero"].partition_broadcast(B)).then_inc(loaded, 16)
                sp.dma_start(bqk[:, :], x["bqk"]).then_inc(loaded, 16)
                sp.dma_start(keep["qscale"][:, :], x["qscale"]).then_inc(loaded, 16)
                sp.dma_start(keep["ident"][:, :], x["ident"]).then_inc(loaded, 16)
                sp.dma_start(keep["bvT"][:, :], x["bvT"]).then_inc(loaded, 16)
                sp.wait_ge(rows_done, 1)
                sp.dma_start(d["rows"].rearrange("r b f -> b r f"), rows[:, :, :]).then_inc(stored, 16)
                sp.wait_ge(stored, 16)

            NLOAD = 16 * (4 * 3 + 2 + 6)

            @block.scalar
            def _(act):
                act.wait_ge(c_loaded, 32)
                nc.scalar.activation(silu_c[:, :, :, :], cT[:, :, :, :], ACT.Silu).then_inc(silu_done, 1)

            @block.tensor
            def _(pe):
                pe.wait_ge(loaded, NLOAD)
                for n in range(4):
                    for k in range(KD):
                        last = nc.tensor.matmul(ps[n][:, k * D:(k + 1) * D], lora_a[:, n, k * P:(k + 1) * P],
                                                lora_b[:, n, :], start=True, stop=True)
                last.then_inc(lora_done, 1)
                pe.wait_ge(silu_done, 1)
                for j in range(3):
                    for k in range(KD):
                        nc.tensor.matmul(ps[4 + j][0:B, :], silu_c[:, k, 0, :], wmod[:, 0, k, j * 512:(j + 1) * 512],
                                         start=(k == 0), stop=(k == KD - 1))
                for w, part in enumerate((1, 0, 4, 3)):
                    for k2 in range(KD):
                        for k in range(KD):
                            col = part * D + k2 * P
                            last = nc.tensor.matmul(ps[7][:, (w * KD + k2) * B:(w * KD + k2 + 1) * B],
                                                    wmod[:, 0, k, col:col + P], silu_c[:, k, 0, :],
                                                    start=(k == 0), stop=(k == KD - 1))
                last.then_inc(mod0_done, 1)
                pe.wait_ge(lora_read, 1)
                for j in range(3):
                    for k in range(KD):
                        last = nc.tensor.matmul(ps[j][0:B, :], silu_c[:, k, 1, :], wmod[:, 1, k, j * 512:(j + 1) * 512],
                                                start=(k == 0), stop=(k == KD - 1))
                last.then_inc(mod1_done, 1)

            @block.vector
            def _(dve):
                dve.wait_ge(loaded, NLOAD)
                nc.vector.tensor_scalar(keep["bqk"][:, :], bqk[:, :], keep["qscale"][:, 0:1], None, ALU.mult)
                dve.wait_ge(lora_done, 1)
                for n in range(4):
                    for k in range(KD):
                        low = ps[n][:, k * D:(k + 1) * D]
                        if n < 2:
                            out = keep["wqk"][:, k, :, n * 64:(n + 1) * 64]
                            low, full = low.rearrange("p (g c) -> p g c", g=G), wT[:, n, k, :].rearrange("p (g c) -> p g c", g=G)
                        else:
                            out, full = keep["wv" if n == 2 else "wo"][:, k, :], wT[:, n, k, :]
                        last = nc.vector.scalar_tensor_tensor(out, low, 1.0 / LORA, full, ALU.mult, ALU.add)
                last.then_inc(lora_read, 1)
                dve.wait_ge(mod0_done, 1)
                for j in range(3):
                    nc.vector.tensor_copy(modr[:, 0, :, :].rearrange("b m f -> b (m f)")[:, j * 512:(j + 1) * 512], ps[4 + j][0:B, :])
                for w, add in enumerate((1.0, 0.0, 1.0, 0.0)):
                    src = ps[7][:, w * KD * B:(w + 1) * KD * B].rearrange("p (k b) -> p k b", b=B)
                    nc.vector.tensor_scalar(keep["mfm"][:, w * KD:(w + 1) * KD, 0:B], src, add, None, ALU.add)
                    nc.vector.tensor_scalar(keep["mfm"][:, w * KD:(w + 1) * KD, B:B + 1], src[:, :, B - 1:B], add, None, ALU.add)
                dve.wait_ge(mod1_done, 1)
                for j in range(3):
                    nc.vector.tensor_copy(modr[:, 1, :, :].rearrange("b m f -> b (m f)")[:, j * 512:(j + 1) * 512], ps[j][0:B, :])
                dve.drain()
                for l in range(2):
                    for n, m in enumerate((2, 5)):
                        nc.vector.tensor_scalar(sgn[:, 2 * l + n, :], modr[:, l, m, :], 0.0, 2.0, ALU.is_ge, ALU.mult)
                        nc.vector.tensor_scalar(mag[:, 2 * l + n, :], modr[:, l, m, :], -1.0, None, ALU.mult)
                dve.drain()
                for l in range(2):
                    for n, m in enumerate((2, 5)):
                        nc.vector.tensor_tensor(mag[:, 2 * l + n, :], mag[:, 2 * l + n, :], modr[:, l, m, :], ALU.max)
                dve.drain()
                nc.vector.tensor_scalar(mag[:, :, :], mag[:, :, :], 0.25, None, ALU.max)
                dve.drain()
                GA0, GB0, GA1, GB1 = range(4)
                for n in range(4):
                    nc.vector.scalar_tensor_tensor(sgn[:, n, :], sgn[:, n, :], -1.0, mag[:, n, :], ALU.add, ALU.mult)
                dve.drain()
                for r, n in ((R_GB0, GB0), (R_GA1, GA1), (R_GB1, GB1)):
                    nc.vector.tensor_copy(rows[:, r, :], sgn[:, n, :])
                for r, m, add in ((R_CA1, 1, 1.0), (R_SA1, 0, 0.0), (R_CB1, 4, 1.0), (R_SB1, 3, 0.0)):
                    nc.vector.tensor_scalar(rows[:, r, :], modr[:, 1, m, :], add, None, ALU.add)
                nc.vector.scalar_tensor_tensor(rows[:, R_GCA, :], modr[:, 0, 1, :], 1.0, sgn[:, GA0, :], ALU.add, ALU.mult)
                nc.vector.tensor_scalar(rows[:, R_GRZ, :], sgn[:, GA0, :], rz[:, 0:1], None, ALU.mult)
                nc.vector.tensor_tensor(rows[:, R_GSA, :], modr[:, 0, 0, :], sgn[:, GA0, :], ALU.mult)
                dve.drain()
                nc.vector.tensor_tensor(mag[:, 0, :], rows[:, R_GRZ, :], bo[:, :], ALU.mult)
                dve.drain()
                nc.vector.tensor_tensor(rows[:, R_GSA, :], rows[:, R_GSA, :], mag[:, 0, :], ALU.add).then_inc(rows_done, 1)


def project_phase(nc, x, d, keep):
    ctx = ExitStack()
    with ctx:
        sb = lambda name, shape, dt=F32: ctx.enter_context(nc.sbuf_tensor("pr_" + name, shape, dt))
        xin = [sb(f"xin{h}", [P, SUB, D]) for h in range(2)]
        xh = [sb(f"xh{h}", [P, SUB, D]) for h in range(2)]
        hT = [sb(f"hT{h}", [P, KD, T]) for h in range(2)]
        mcur = sb("mcur", [P, 2 * KD])
        st, mv = sb("st", [P, SUB, 6]), sb("mv", [P, SUB, 2])
        ve, rstd, mhalf = sb("ve", [P, SUB]), sb("rstd", [P, SUB]), sb("mhalf", [P, SUB])
        qk = [sb(f"qk{g}", [P, T]) for g in range(G)]
        rest = [sb(f"rest{g}", [P, T]) for g in range(G)]
        parts = [sb(f"parts{g}", [P, 3, T], BF16) for g in range(G)]
        vaug = [sb(f"vaug{h}", [P, SUB, H, 32]) for h in range(2)]
        ps_t = [ctx.enter_context(nc.psum_tensor(f"pr_pst{k}", [P, T], F32)) for k in range(KD)]
        ps_qk = [ctx.enter_context(nc.psum_tensor(f"pr_psqk{k}", [P, T], F32)) for k in range(4)]
        ps_v = [ctx.enter_context(nc.psum_tensor(f"pr_psv{k}", [P, 2, D], F32)) for k in range(2)]
        sem = phase_semaphores(nc, ctx, "pr_")
        x_in = [sem(f"x_in{h}") for h in range(2)]
        var_done, rstd_done, xh_done = sem("var_done"), sem("rstd_done"), sem("xh_done")
        tr_done, hT_done, qk_done, qk_out = sem("tr_done"), sem("hT_done"), sem("qk_done"), sem("qk_out")
        rest_done, p2_done, p3_done = sem("rest_done"), sem("p2_done"), sem("p3_done")
        v_done, v_out, always, const_done = sem("v_done"), sem("v_out"), sem("always"), sem("const_done")
        parts_stored = [sem(f"parts_stored{g}") for g in range(G)]
        v_stored = [sem(f"v_stored{h}") for h in range(2)]

        with nc.Block() as block:
            @block.sync
            def _(sp):
                with sp.Fori(0, B) as b:
                    for c in range(CPB):
                        i = b * CPB + c
                        for g in range(G):
                            sp.wait_ge(p3_done, i * G + g + 1)
                            sp.wait_ge(p2_done, i * G + g + 1)
                            sp.dma_start(d["parts"][g, :, :, ds(i * T, T)].rearrange("c p t -> p c t"), parts[g][:, :, :]).then_inc(parts_stored[g], 16)
                        sp.wait_ge(v_out, 2 * i + 2)
                        for g in range(G):
                            sp.dma_start(d["v"][ds(b * G + g, 1), :, c * SUB:(c + 1) * SUB, :].rearrange("u p s c -> p (u s) c"),
                                         vaug[c % 2][:, :, g * HPG:(g + 1) * HPG, :].rearrange("p s h c -> p s (h c)")).then_inc(v_stored[c % 2], 16)
                for g in range(G):
                    sp.wait_ge(parts_stored[g], 16 * NCH)
                for h in range(2):
                    sp.wait_ge(v_stored[h], 16 * G * NCH // 2)

            @block.gpsimd
            def _(pool):
                nc.gpsimd.memset(mhalf[:, :], -0.5)
                for h in range(2):
                    nc.gpsimd.memset(vaug[h][:, :, :, HD:32], 0.0)
                pool.drain()
                for h in range(2):
                    last = nc.gpsimd.memset(vaug[h][:, :, :, HD:HD + 1], 1.0)
                last.then_inc(const_done, 1)
                pool.sem_inc(always, 1)
                pool.drain()

                def load(chunk, h):
                    nc.gpsimd.dma_start(xin[h][:, :, :], x["x"][ds(chunk * T, T), :].rearrange("(s p) f -> p s f", p=P)).then_inc(x_in[h], 16)

                def rsqrt(n):
                    pool.wait_ge(var_done, n + 1)
                    nc.gpsimd.tensor_tensor(rstd[:, :], ve[:, :], mhalf[:, :], ALU.pow).then_inc(rstd_done, 1)

                for n in range(2):
                    load(n, n)
                for n in range(2):
                    rsqrt(n)
                    wait_alone(pool, xh_done, n + 1, always)
                    load(n + 2, n)
                with pool.Fori(0, B) as b:
                    for c in range(CPB):
                        i = b * CPB + c
                        rsqrt(i + 2)
                        wait_alone(pool, xh_done, i + 3, always)
                        load((i + 4) % NCH, c % 2)
                        for g in range(G):
                            pool.wait_ge(p2_done, i * G + g + 1)
                            nc.gpsimd.tensor_tensor(parts[g][:, 2, :], rest[g][:, :], parts[g][:, 1, :], ALU.subtract).then_inc(p3_done, 1)
                for h in range(2):
                    pool.wait_ge(x_in[h], 16 * (NCH // 2 + 2))

            @block.vector
            def _(dve):
                def normalise(n, m, h):
                    dve.wait_ge(x_in[h], 16 * m + 16)
                    for s in range(SUB):
                        nc.vector.bn_stats(st[:, s, :], xin[h][:, s, :])
                    dve.drain()
                    for s in range(SUB):
                        nc.vector.bn_aggr(mv[:, s, :], st[:, s, :])
                    dve.drain()
                    nc.vector.tensor_scalar(ve[:, :], mv[:, :, 1], EPS, None, ALU.add).then_inc(var_done, 1)
                    dve.wait_ge(rstd_done, n + 1)
                    if not isinstance(n, int):
                        dve.wait_ge(tr_done, n - 1)
                    for s in range(SUB):
                        last = nc.vector.tensor_scalar(xh[h][:, s, :], xin[h][:, s, :], mv[:, s, 0:1], rstd[:, s:s + 1], ALU.subtract, ALU.mult)
                    last.then_inc(xh_done, 1)

                normalise(0, 0, 0)
                normalise(1, 0, 1)
                dve.wait_ge(const_done, 1)
                with dve.Fori(0, B) as b:
                    for c in range(CPB):
                        i = b * CPB + c
                        normalise(i + 2, b * 2 + (c + 2) // 2, c % 2)
                        for half in range(2):
                            dve.wait_ge(v_done, 2 * i + half + 1)
                            if half == 0:
                                dve.wait_ge(v_stored[c % 2], (b * 2 + c // 2) * G * 16)
                            nc.vector.tensor_copy(vaug[c % 2][:, 2 * half:2 * half + 2, :, 0:HD],
                                                  ps_v[half][:, :, :].rearrange("p s (h e) -> p s h e", e=HD)).then_inc(v_out, 1)
                        for g in range(G):
                            dve.wait_ge(qk_out, i * G + g + 1)
                            dve.wait_ge(p3_done, i * G)
                            nc.vector.tensor_tensor(rest[g][:, :], qk[g][:, :], parts[g][:, 0, :], ALU.subtract).then_inc(rest_done, 1)
                            dve.drain()
                            nc.vector.tensor_copy(parts[g][:, 1, :], rest[g][:, :]).then_inc(p2_done, 1)

            @block.scalar
            def _(act):
                def modulate(n, h):
                    act.wait_ge(tr_done, n + 1)
                    for k in range(KD):
                        last = nc.scalar.activation(hT[h][:, k, :], ps_t[k][:, :], ACT.Identity,
                                                    scale=mcur[:, k:k + 1], bias=mcur[:, KD + k:KD + k + 1])
                    last.then_inc(hT_done, 1)

                def batch_vectors(b):
                    act.drain()
                    nc.scalar.copy(mcur[:, :], keep["mfm"][:, 0:2 * KD, ds(b, 1)].rearrange("p m b -> p (m b)"))
                    act.drain()

                batch_vectors(0)
                modulate(0, 0)
                with act.Fori(0, B) as b:
                    for c in range(CPB):
                        i = b * CPB + c
                        for g in range(G):
                            act.wait_ge(qk_done, i * G + g + 1)
                            act.wait_ge(rest_done, i * G)
                            act.wait_ge(parts_stored[g], 16 * i)
                            nc.scalar.activation(qk[g][:, :], ps_qk[g][:, :], ACT.Identity, scale=keep["qscale"][:, 0:1], bias=keep["bqk"][:, g:g + 1])
                            nc.scalar.activation(parts[g][:, 0, :], ps_qk[g][:, :], ACT.Identity, scale=keep["qscale"][:, 0:1],
                                                 bias=keep["bqk"][:, g:g + 1]).then_inc(qk_out, 1)
                            if g == 1:
                                if c == CPB - 1:
                                    batch_vectors(b + 1)
                                modulate(i + 1, (c + 1) % 2)

            @block.tensor
            def _(pe):
                def transposes(n, h):
                    pe.wait_ge(xh_done, n + 1)
                    pe.wait_ge(hT_done, n)
                    for k in range(KD):
                        for s in range(SUB):
                            last = nc.tensor.transpose(ps_t[k][:, s * P:(s + 1) * P], xh[h][:, s, k * P:(k + 1) * P], keep["ident"][:, :])
                    last.then_inc(tr_done, 1)

                def qk_products(i, c, g):
                    if g == 0:
                        pe.wait_ge(hT_done, i + 1)
                    pe.wait_ge(qk_out, i * G)
                    for k in range(KD):
                        last = nc.tensor.matmul(ps_qk[g][:, :], keep["wqk"][:, k, g, :], hT[c % 2][:, k, :], start=(k == 0), stop=(k == KD - 1))
                    last.then_inc(qk_done, 1)

                def v_products(i, c, half):
                    pe.wait_ge(v_out, 2 * i)
                    for s in range(2):
                        for k in range(KD):
                            last = nc.tensor.matmul(ps_v[half][:, s, :], hT[c % 2][:, k, (2 * half + s) * P:(2 * half + s + 1) * P],
                                                    keep["wv"][:, k, :], start=(k == 0), stop=(k == KD - 1))
                    last.then_inc(v_done, 1)

                transposes(0, 0)
                with pe.Fori(0, B) as b:
                    for c in range(CPB):
                        i = b * CPB + c
                        qk_products(i, c, 0)
                        qk_products(i, c, 1)
                        v_products(i, c, 0)
                        transposes(i + 1, (c + 1) % 2)
                        qk_products(i, c, 2)
                        qk_products(i, c, 3)
                        v_products(i, c, 1)


def attend_phase(nc, x, d, keep):
    ctx = ExitStack()
    with ctx:
        sb = lambda name, shape, dt=F32: ctx.enter_context(nc.sbuf_tensor("at_" + name, shape, dt))
        qs = [sb(f"qs{s}", [QROWS, HPG, S], BF16) for s in range(2)]
        ks = [sb(f"ks{s}", [QROWS, HPG, S], BF16) for s in range(2)]
        vs = [sb(f"vs{s}", [P, KT, HPG * 32]) for s in range(2)]
        prob = [[sb(f"prob{r}{a}", [P, 2, T]) for a in range(2)] for r in range(2)]
        mxp = sb("mxp", [P, SUB * HPG, S // T])
        nmax = sb("nmax", [P, SUB * HPG])
        nparts = sb("nparts", [P, SUB, HPG, 2], BF16)
        nrows = sb("nrows", [2 * HPG, T], BF16)
        osum = sb("osum", [P, T])
        rec = sb("rec", [P, SUB, HPG])
        onorm = [sb(f"onorm{r}", [P, SUB, HPG * HD]) for r in range(2)]
        identb = sb("identb", [P, P], BF16)
        ps_s = [ctx.enter_context(nc.psum_tensor(f"at_ps_s{a}", [P, 2, T], F32)) for a in range(2)]
        ps_m = [ctx.enter_context(nc.psum_tensor(f"at_ps_m{a}", [P, T], F32)) for a in range(2)]
        ps_o = ctx.enter_context(nc.psum_tensor("at_ps_o", [P, T], F32))
        ps_x = ctx.enter_context(nc.psum_tensor("at_ps_x", [P, T], F32))
        x_bf = ps_x[:, :].bitcast(BF16)
        sem = phase_semaphores(nc, ctx, "at_")
        kq_in = [sem(f"kq_in{s}") for s in range(2)]
        s_done, p_done, o_done, o_out = sem("s_done"), sem("p_done"), sem("o_done"), sem("o_out")
        mx_done, mx_read, neg_done = sem("mx_done"), sem("mx_read"), sem("neg_done")
        xt_done, ot_done, x_read = sem("xt_done"), sem("ot_done"), sem("x_read")
        max_in, always = sem("max_in"), sem("always")
        o_stored = [sem(f"o_stored{r}") for r in range(2)]
        QC = S // T
        STEP = 2 * KT
        MXN = SUB * HPG * (S // T)
        NLD = 2 * len(BANDS) + 2

        with nc.Block() as block:
            @block.sync
            def _(sp):
                def load(u, s):
                    b, g = u // G, u % G
                    for r, (qp, kp) in enumerate(BANDS):
                        for dst, part, row in ((qs, qp, 0), (ks, kp, HPG * HD)):
                            src = d["parts"][ds(g, 1), part, row:row + HPG * HD, ds(b * S, S)]
                            sp.dma_start(dst[s][r * HD:(r + 1) * HD, :, :], src.rearrange("g (j e) t -> e (g j) t", e=HD)).then_inc(kq_in[s], 16)
                    sp.dma_start(ks[s][ALI:ALI + 2, :, :], x["alibi"].bitcast(BF16)[:, ds(g * HPG, HPG), :]).then_inc(kq_in[s], 16)
                    sp.dma_start(vs[s][:, :, :], d["v"][ds(u, 1), :, :, :].rearrange("u p k c -> p (u k) c")).then_inc(kq_in[s], 16)

                for s in range(2):
                    sp.dma_start(qs[s][ALI:ALI + 2, :, :], x["ones"].bitcast(BF16)).then_inc(max_in, 16)
                    sp.dma_start(ks[s][MXR:MXR + 2, :, :], x["ones"].bitcast(BF16)).then_inc(max_in, 16)

                def store_max(s, c):
                    for j in range(HPG):
                        sp.dma_start(qs[s][MXR:MXR + 2, j, c * T:(c + 1) * T], nrows[2 * j:2 * j + 2, :]).then_inc(max_in, 16)

                load(0, 0)
                sp.wait_ge(x_read, 1)
                store_max(0, 0)
                with sp.Fori(0, UNITS // 2) as up:
                    for s in range(2):
                        u = up * 2 + s
                        wait_alone(sp, o_done, u * QC, always)
                        load((u + 1) % UNITS, 1 - s)
                        for c in range(QC):
                            n = u * QC + c
                            sp.wait_ge(x_read, 2 * n + 2)
                            store_max(s if c < QC - 1 else 1 - s, (c + 1) % QC)
                            wait_alone(sp, x_read, 2 * n + 3, always)
                            sp.dma_start(d["o"][ds(n, 1), :, :, :].rearrange("n p s c -> p (n s) c"), onorm[c % 2][:, :, :]).then_inc(o_stored[c % 2], 16)
                sp.wait_ge(x_read, 2 * UNITS * QC + 2)
                sp.dma_start(d["o"][UNITS * QC, :, :, :], onorm[0][:, :, :]).then_inc(o_stored[0], 16)
                sp.wait_ge(o_stored[0], 16 * (UNITS * QC // 2 + 1))
                sp.wait_ge(o_stored[1], 16 * (UNITS * QC // 2))
                sp.wait_ge(max_in, 64 + 64 * (UNITS * QC + 1))

            @block.scalar
            def _(act):
                def take_sums(n):
                    act.wait_ge(o_done, n)
                    act.wait_ge(ot_done, n)
                    nc.scalar.copy(osum[:, :], ps_o[:, :]).then_inc(o_out, 1)

                act.wait_ge(always, 1)
                with act.Fori(0, UNITS * QC) as n:
                    for t in range(KT):
                        for a in range(2):
                            act.wait_ge(s_done, n * STEP + 2 * t + a + 1)
                            nc.scalar.activation(prob[t % 2][a][:, :, :], ps_s[a][:, :, :], ACT.Exp).then_inc(p_done, 1)
                            if t == 0 and a == 0:
                                take_sums(n)
                take_sums(UNITS * QC)

            @block.vector
            def _(dve):
                def maxima(n, t):
                    for k in range(S // T):
                        dve.wait_ge(mx_done, n * MXN + t * (S // T) + k + 1)
                        nc.vector.tensor_reduce(mxp[:, t, k:k + 1], ps_m[k % 2][:, :], AX.X, ALU.max).then_inc(mx_read, 1)

                def negate():
                    dve.drain()
                    nc.vector.tensor_reduce(nmax[:, :], mxp[:, :, :], AX.X, ALU.max, negate=True)
                    dve.drain()
                    flat = nparts[:, :, :, :].rearrange("p s j c -> p (s j) c")
                    nc.vector.tensor_copy(flat[:, :, 0], nmax[:, :])
                    dve.drain()
                    nc.vector.tensor_tensor(flat[:, :, 1], nmax[:, :], flat[:, :, 0], ALU.subtract).then_inc(neg_done, 1)

                def take_rows(n):
                    dve.wait_ge(xt_done, n + 1)
                    dve.wait_ge(max_in, 64 + 64 * n)
                    nc.vector.tensor_copy(nrows[:, :], x_bf[0:2 * HPG, 0:T]).then_inc(x_read, 1)

                def normalise(n, r, m):
                    dve.wait_ge(ot_done, n + 1)
                    view = ps_x[:, :].rearrange("p (s j c) -> p s j c", s=SUB, j=HPG)
                    nc.vector.reciprocal(rec[:, :, :], view[:, :, :, HD])
                    dve.drain()
                    dve.wait_ge(o_stored[r], 16 * m)
                    nc.vector.tensor_tensor(onorm[r][:, :, :].rearrange("p s (j c) -> p s j c", j=HPG), view[:, :, :, 0:HD],
                                            rec[:, :, :].unsqueeze(3).to_broadcast([P, SUB, HPG, HD]), ALU.mult).then_inc(x_read, 1)

                nc.vector.memset(ps_o[:, :], 1.0)
                nc.vector.tensor_copy(identb[:, :], keep["ident"][:, :])
                dve.drain()
                dve.sem_inc(always, 1)
                for n in range(2):
                    for t in range(SUB * HPG):
                        maxima(n, t)
                    if n == 1:
                        dve.wait_ge(xt_done, 1)
                    negate()
                    if n == 0:
                        take_rows(0)
                with dve.Fori(0, UNITS * QC // 2) as m:
                    for r in range(2):
                        n = m * 2 + r
                        for t in range(SUB * HPG):
                            maxima(n + 2, t)
                            if t == 3:
                                take_rows(n + 1)
                            if t == 7:
                                normalise(n, r, m)
                        negate()
                normalise(UNITS * QC, 0, UNITS * QC // 2)

            @block.tensor
            def _(pe):
                def scores(s, c, t, a):
                    for j in range(2):
                        head = 2 * a + j
                        last = nc.tensor.matmul(ps_s[a][:, j, :], ks[s][0:QROWS, head, t * P:(t + 1) * P],
                                                qs[s][0:QROWS, head, c * T:(c + 1) * T], start=True, stop=True)
                    last.then_inc(s_done, 1)

                def max_scores(n, s, c, t, k):
                    if not (isinstance(n, int) and n * MXN + t * (S // T) + k < 2):
                        pe.wait_ge(mx_read, n * MXN + t * (S // T) + k - 1)
                    q0 = c * T + (t // HPG) * P
                    nc.tensor.matmul(ps_m[k % 2][:, :], qs[s][0:MXR, t % HPG, q0:q0 + P], ks[s][0:MXR, t % HPG, k * T:(k + 1) * T],
                                     start=True, stop=True).then_inc(mx_done, 1)

                def weighted(s, t, half):
                    cols = slice(half * (T // 2), (half + 1) * (T // 2))
                    for j in range(HPG):
                        last = nc.tensor.matmul(ps_o[32 * j:32 * j + 32, cols], vs[s][:, t, 32 * j:32 * j + 32], prob[t % 2][j // 2][:, j % 2, cols],
                                                start=(t == 0 and half == 0), stop=(t == KT - 1 and half == 1),
                                                tile_position=(0, 32 * j), skip_group_check=True)
                    return last

                def max_rows(n):
                    wait_alone(pe, neg_done, n + 1, always)
                    for s in range(SUB):
                        last = nc.tensor.transpose(x_bf[0:2 * HPG, s * P:(s + 1) * P], nparts[:, s, :, :].rearrange("p j c -> p (j c)"), identb[:, :])
                    last.then_inc(xt_done, 1)

                def sums_by_token(n):
                    pe.wait_ge(o_out, n + 1)
                    for s in range(SUB):
                        last = nc.tensor.transpose(ps_x[:, s * P:(s + 1) * P], osum[:, s * P:(s + 1) * P], keep["ident"][:, :])
                    last.then_inc(ot_done, 1)

                pe.wait_ge(max_in, 64)
                pe.wait_ge(kq_in[0], 16 * NLD)
                for t in range(SUB * HPG):
                    for k in range(S // T):
                        max_scores(0, 0, 0, t, k)
                max_rows(0)
                for t in range(SUB * HPG):
                    for k in range(S // T):
                        max_scores(1, 0, 1, t, k)
                pe.wait_ge(max_in, 128)
                for a in range(2):
                    scores(0, 0, 0, a)
                with pe.Fori(0, UNITS // 2) as up:
                    for s in range(2):
                        for c in range(QC):
                            n = (up * 2 + s) * QC + c
                            ms, mc = (s, c + 2) if c + 2 < QC else (1 - s, c + 2 - QC)
                            if c + 2 == QC:
                                pe.wait_ge(kq_in[1 - s], 16 * NLD * (up + 1 + s))
                            for t in range(KT):
                                nxt = (s, c, t + 1) if t + 1 < KT else ((s, c + 1, 0) if c + 1 < QC else (1 - s, 0, 0))
                                if t + 1 == KT:
                                    pe.wait_ge(max_in, 64 + 64 * (n + 2))
                                pe.wait_ge(p_done, n * STEP + 2 * t + 1)
                                scores(*nxt, 0)
                                max_scores(n + 2, ms, mc, t, 0)
                                if t == 0:
                                    pe.wait_ge(o_out, n + 1)
                                pe.wait_ge(p_done, n * STEP + 2 * t + 2)
                                weighted(s, t, 0)
                                max_scores(n + 2, ms, mc, t, 1)
                                scores(*nxt, 1)
                                max_scores(n + 2, ms, mc, t, 2)
                                last = weighted(s, t, 1)
                                if t + 1 == KT:
                                    last.then_inc(o_done, 1)
                                max_scores(n + 2, ms, mc, t, 3)
                                if t == 3:
                                    wait_alone(pe, x_read, 2 * n + 1, always)
                                    max_rows(n + 1)
                                if t == 7:
                                    pe.wait_ge(x_read, 2 * n + 2)
                                    sums_by_token(n)
                pe.wait_ge(x_read, 2 * UNITS * QC + 1)
                sums_by_token(UNITS * QC)


def mix_phase(nc, x, d, keep):
    ctx = ExitStack()
    with ctx:
        sb = lambda name, shape, dt=F32: ctx.enter_context(nc.sbuf_tensor("mi_" + name, shape, dt))
        w1 = sb("w1", [P, E0, KD, F0])
        w2 = sb("w2", [P, E0, D])
        b1 = sb("b1", [F0, E0])
        b2 = sb("b2", [E0, D])
        rw = sb("rw", [P, KD, E0])
        rb = sb("rb", [P, E0])
        gvec = sb("gvec", [P, 4, B + 1, D])
        g_front = sb("g_front", [P, 2, D])
        g_back = sb("g_back", [P, D])
        wob = sb("wob", [P, KD, D])
        iota = sb("iota", [P, E0])
        xin = [sb(f"xin{h}", [P, SUB, D]) for h in range(2)]
        oin = [sb(f"oin{h}", [P, SUB, G, HPG * HD]) for h in range(2)]
        st, mv = sb("st", [P, SUB, 6]), sb("mv", [P, SUB, 2])
        ve, rstd, mhalf = sb("ve", [P, SUB]), sb("rstd", [P, SUB]), sb("mhalf", [P, SUB])
        xh1, base = sb("xh1", [P, SUB, D]), sb("base", [P, SUB, D])
        x1 = [sb(f"x1{h}", [P, SUB, D]) for h in range(2)]
        xh2 = sb("xh2", [P, SUB, D])
        oT = sb("oT", [P, KD, T])
        hT = [sb(f"hT{h}", [P, KD, T]) for h in range(2)]
        mcur = sb("mcur", [P, 2 * KD])
        act_e = [sb(f"act{e}", [F0, T]) for e in range(E0)]
        acc = sb("acc", [P, SUB, D])
        scaled = sb("scaled", [P, SUB, D])
        x2 = [sb(f"x2{h}", [P, SUB, D]) for h in range(2)]
        lg, mx8, ix = sb("lg", [P, SUB, E0]), sb("mx8", [P, SUB, 8]), sb("ix", [P, SUB, 8], U32)
        ixf, gap, e2 = sb("ixf", [P, SUB, 2]), sb("gap", [P, SUB]), sb("e2", [P, SUB])
        den, wt = sb("den", [P, SUB]), sb("wt", [P, 2, SUB])
        pick = sb("pick", [P, 2, SUB, E0])
        mask = [sb(f"mask{h}", [P, SUB, E0]) for h in range(2)]
        maskT = sb("maskT", [E0, T])
        pb = lambda name, shape: ctx.enter_context(nc.psum_tensor("mi_" + name, shape, F32))
        ps_t = [pb(f"ps_t{k}", [P, T]) for k in range(KD)]
        ps_a = [pb(f"ps_a{k}", [P, 2, D]) for k in range(2)]
        ps_h = [pb(f"ps_h{k}", [P, T]) for k in range(2)]
        ps_f = [pb(f"ps_f{k}", [P, 2, D]) for k in range(2)]
        sem = phase_semaphores(nc, ctx, "mi_")
        const_in, always = sem("const_in"), sem("always")
        xo_in = [sem(f"xo_in{h}") for h in range(2)]
        var_done, rstd_done, xh1_done, base_done = sem("var_done"), sem("rstd_done"), sem("xh1_done"), sem("base_done")
        wob_done, x1_done, xh2_done, mask_done = sem("wob_done"), sem("x1_done"), sem("xh2_done"), sem("mask_done")
        tro_done, oT_done, proj_done, trx_done = sem("tro_done"), sem("oT_done"), sem("proj_done"), sem("trx_done")
        hT_done, lg_done, lg_read, gap_done, e2_done = sem("hT_done"), sem("lg_done"), sem("lg_read"), sem("gap_done"), sem("e2_done")
        mT_done, mT_out, b2_done, acc_set = sem("mT_done"), sem("mT_out"), sem("b2_done"), sem("acc_set")
        h_done, act_done, f_done, f_read = sem("h_done"), sem("act_done"), sem("f_done"), sem("f_read")
        scaled_done, x2_done = sem("scaled_done"), sem("x2_done")
        x2_stored = [sem(f"x2_stored{h}") for h in range(2)]
        NCONST = 16 * (6 + 4 * B + 4 + 1)

        with nc.Block() as block:
            @block.sync
            def _(sp):
                sp.dma_start(iota[:, :], x["iota"][:, 0:E0]).then_inc(const_in, 16)
                sp.dma_start(rb[:, :], x["rb"].partition_broadcast(P)).then_inc(const_in, 16)
                sp.dma_start(rw[:, :, :], x["rw"].rearrange("(k p) e -> p k e", p=P)).then_inc(const_in, 16)
                sp.dma_start(b1[:, :], x["b1T"]).then_inc(const_in, 16)
                sp.dma_start(b2[:, :], x["b2"]).then_inc(const_in, 16)
                for n, r in enumerate((R_GCA, R_GSA, R_GRZ, R_GB0)):
                    for b in range(B + 1):
                        sp.dma_start(gvec[:, n, b, :], d["rows"][r, min(b, B - 1), :].partition_broadcast(P)).then_inc(const_in, 16)

                def load(n, b, c, h):
                    sp.dma_start(xin[h][:, :, :], x["x"][ds(n * T, T), :].rearrange("(s p) f -> p s f", p=P)).then_inc(xo_in[h], 16)
                    for g in range(G):
                        sp.dma_start(oin[h][:, :, g, :], d["o"][ds((b * G + g) * CPB + c + 1, 1), :, :, :].rearrange("n p s f -> p (n s) f")).then_inc(xo_in[h], 16)

                load(0, 0, 0, 0)
                sp.dma_start(w1[:, :, :, :], x["w1"].rearrange("e (k p) f -> p e k f", p=P)).then_inc(const_in, 16)
                load(1, 0, 1, 1)
                sp.dma_start(w2[:, :, :], x["w2"].rearrange("e f n -> f e n")).then_inc(const_in, 16)
                with sp.Fori(0, B) as b:
                    for c in range(CPB):
                        i = b * CPB + c
                        sp.wait_ge(base_done, i + 1)
                        wait_alone(sp, tro_done, i + 1, always)
                        load((i + 2) % NCH, (b + (c + 2) // CPB) % B, (c + 2) % CPB, c % 2)
                        wait_alone(sp, x2_done, i + 1, always)
                        sp.dma_start(d["x2"][ds(i * T, T), :].rearrange("(s p) f -> p s f", p=P), x2[c % 2][:, :, :]).then_inc(x2_stored[c % 2], 16)
                for h in range(2):
                    sp.wait_ge(x2_stored[h], 16 * NCH // 2)
                    sp.wait_ge(xo_in[h], 80 * (NCH // 2 + 1))

            @block.gpsimd
            def _(pool):
                def rsqrt(k):
                    pool.wait_ge(var_done, k + 1)
                    nc.gpsimd.tensor_tensor(rstd[:, :], ve[:, :], mhalf[:, :], ALU.pow).then_inc(rstd_done, 1)

                def residual_base(n, m, h):
                    over = lambda v: v.unsqueeze(1).to_broadcast([P, SUB, D])
                    pool.wait_ge(xh1_done, n + 1)
                    pool.wait_ge(x1_done, n)
                    nc.gpsimd.tensor_tensor(base[:, :, :], xh1[:, :, :], over(g_front[:, 0, :]), ALU.mult)
                    pool.drain()
                    nc.gpsimd.tensor_tensor(base[:, :, :], base[:, :, :], over(g_front[:, 1, :]), ALU.add)
                    pool.drain()
                    nc.gpsimd.tensor_tensor(base[:, :, :], base[:, :, :], xin[h][:, :, :], ALU.add).then_inc(base_done, 1)

                def front_vectors(b):
                    pool.drain()
                    nc.gpsimd.tensor_copy(g_front[:, :, :], gvec[:, 0:2, ds(b, 1), :].rearrange("p n b f -> p (n b) f"))
                    pool.drain()

                nc.gpsimd.memset(mhalf[:, :], -0.5)
                pool.sem_inc(always, 1)
                pool.wait_ge(const_in, NCONST)
                front_vectors(0)
                rsqrt(0)
                residual_base(0, 0, 0)
                rsqrt(1)
                rsqrt(2)
                residual_base(1, 0, 1)
                with pool.Fori(0, B) as b:
                    for c in range(CPB):
                        i = b * CPB + c
                        rsqrt(2 * i + 3)
                        if c == CPB - 2:
                            front_vectors(b + 1)
                        rsqrt(2 * i + 4)
                        residual_base(i + 2, b * 2 + (c + 2) // 2, c % 2)
                        pool.wait_ge(scaled_done, i + 1)
                        pool.wait_ge(x2_stored[c % 2], 16 * (b * 2 + c // 2))
                        nc.gpsimd.tensor_tensor(x2[c % 2][:, :, :], scaled[:, :, :], x1[c % 2][:, :, :], ALU.add).then_inc(x2_done, 1)

            @block.vector
            def _(dve):
                def variance(src):
                    for s in range(SUB):
                        nc.vector.bn_stats(st[:, s, :], src[:, s, :])
                    dve.drain()
                    for s in range(SUB):
                        nc.vector.bn_aggr(mv[:, s, :], st[:, s, :])
                    dve.drain()
                    nc.vector.tensor_scalar(ve[:, :], mv[:, :, 1], EPS, None, ALU.add).then_inc(var_done, 1)

                def scale_rows(dst, src, k):
                    dve.wait_ge(rstd_done, k + 1)
                    for s in range(SUB):
                        last = nc.vector.tensor_scalar(dst[:, s, :], src[:, s, :], mv[:, s, 0:1], rstd[:, s:s + 1], ALU.subtract, ALU.mult)
                    return last

                def first_variance(m, h):
                    dve.wait_ge(xo_in[h], 80 * m + 80)
                    variance(xin[h])

                def first_norm(n, h):
                    dve.wait_ge(base_done, n)
                    scale_rows(xh1, xin[h], 2 * n).then_inc(xh1_done, 1)

                def output_weights(b):
                    dve.drain()
                    nc.vector.tensor_tensor(wob[:, :, :], keep["wo"][:, :, :], gvec[:, 2, ds(b, 1), :].to_broadcast([P, KD, D]), ALU.mult).then_inc(wob_done, 1)

                def first_residual(n, h):
                    dve.wait_ge(base_done, n + 1)
                    dve.wait_ge(proj_done, n + 1)
                    for k in range(2):
                        last = nc.vector.tensor_tensor(x1[h][:, 2 * k:2 * k + 2, :], base[:, 2 * k:2 * k + 2, :], ps_a[k][:, :, :], ALU.add)
                    last.then_inc(x1_done, 1)
                    dve.drain()
                    variance(x1[h])

                def second_norm(n, h):
                    dve.wait_ge(trx_done, n)
                    scale_rows(xh2, x1[h], 2 * n + 1).then_inc(xh2_done, 1)

                def best_two(n):
                    dve.wait_ge(lg_done, n + 1)
                    nc.vector.tensor_tensor(lg[:, :, :], ps_a[0][:, 0, 0:SUB * E0].rearrange("p (s e) -> p s e", s=SUB),
                                            rb[:, :].unsqueeze(1).to_broadcast([P, SUB, E0]), ALU.add).then_inc(lg_read, 1)
                    dve.drain()
                    for s in range(SUB):
                        nc.vector.max(mx8[:, s, :], lg[:, s, :])
                    dve.drain()
                    for s in range(SUB):
                        nc.vector.max_index(ix[:, s, :], mx8[:, s, :], lg[:, s, :])
                    nc.vector.tensor_tensor(gap[:, :], mx8[:, :, 1], mx8[:, :, 0], ALU.subtract).then_inc(gap_done, 1)
                    dve.drain()
                    nc.vector.tensor_copy(ixf[:, :, :], ix[:, :, 0:2])

                def routing(n, h):
                    dve.wait_ge(e2_done, n + 1)
                    nc.vector.tensor_scalar(den[:, :], e2[:, :], 1.0, None, ALU.add)
                    dve.drain()
                    nc.vector.reciprocal(wt[:, 0, :], den[:, :])
                    dve.drain()
                    nc.vector.tensor_tensor(wt[:, 1, :], e2[:, :], wt[:, 0, :], ALU.mult)
                    dve.drain()
                    for k in range(2):
                        for s in range(SUB):
                            nc.vector.tensor_scalar(pick[:, k, s, :], iota[:, :], ixf[:, s, k:k + 1], wt[:, k, s:s + 1], ALU.is_equal, ALU.mult)
                    dve.drain()
                    nc.vector.tensor_tensor(mask[h][:, :, :], pick[:, 0, :, :], pick[:, 1, :, :], ALU.add).then_inc(mask_done, 1)

                def add_expert(i, h, e):
                    for pair in range(2):
                        dve.wait_ge(f_done, (i * E0 + e) * 2 + pair + 1)
                        for j in range(2):
                            s = 2 * pair + j
                            last = nc.vector.scalar_tensor_tensor(acc[:, s, :], ps_f[pair][:, j, :], mask[h][:, s, e:e + 1], acc[:, s, :], ALU.mult, ALU.add)
                        last.then_inc(f_read, 1)
                    dve.drain()

                dve.wait_ge(const_in, NCONST)
                output_weights(0)
                first_variance(0, 0)
                first_norm(0, 0)
                first_residual(0, 0)
                second_norm(0, 0)
                best_two(0)
                routing(0, 0)
                first_variance(0, 1)
                first_norm(1, 1)
                with dve.Fori(0, B) as b:
                    dve.drain()
                    nc.vector.tensor_copy(g_back[:, :], gvec[:, 3, ds(b, 1), :].rearrange("p b f -> p (b f)"))
                    for c in range(CPB):
                        i = b * CPB + c
                        h, h1 = c % 2, (c + 1) % 2
                        if c == CPB - 1:
                            output_weights(b + 1)
                        dve.wait_ge(acc_set, i + 1)
                        add_expert(i, h, 0)
                        first_residual(i + 1, h1)
                        add_expert(i, h, 1)
                        second_norm(i + 1, h1)
                        add_expert(i, h, 2)
                        add_expert(i, h, 3)
                        first_variance(b * 2 + (c + 2) // 2, h)
                        add_expert(i, h, 4)
                        first_norm(i + 2, h)
                        add_expert(i, h, 5)
                        best_two(i + 1)
                        add_expert(i, h, 6)
                        routing(i + 1, h1)
                        add_expert(i, h, 7)
                        dve.wait_ge(x2_done, i)
                        nc.vector.tensor_tensor(scaled[:, :, :], acc[:, :, :], g_back[:, :].unsqueeze(1).to_broadcast([P, SUB, D]), ALU.mult).then_inc(scaled_done, 1)

            @block.scalar
            def _(act):
                def attention_rows(n):
                    act.wait_ge(tro_done, n + 1)
                    for k in range(KD):
                        last = nc.scalar.activation(oT[:, k, :], ps_t[k][:, :], ACT.Identity, bias=keep["bvT"][:, k:k + 1])
                    last.then_inc(oT_done, 1)

                def modulate(n, h):
                    act.wait_ge(trx_done, n + 1)
                    for k in range(KD):
                        last = nc.scalar.activation(hT[h][:, k, :], ps_t[k][:, :], ACT.Identity, scale=mcur[:, k:k + 1], bias=mcur[:, KD + k:KD + k + 1])
                    last.then_inc(hT_done, 1)

                def batch_vectors(b):
                    act.drain()
                    nc.scalar.copy(mcur[:, :], keep["mfm"][:, 2 * KD:4 * KD, ds(b, 1)].rearrange("p m b -> p (m b)"))
                    act.drain()

                def second_weight(n):
                    act.wait_ge(gap_done, n + 1)
                    nc.scalar.activation(e2[:, :], gap[:, :], ACT.Exp).then_inc(e2_done, 1)

                def hidden(i, e):
                    act.wait_ge(h_done, i * E0 + e + 1)
                    nc.scalar.activation(act_e[e][:, :], ps_h[e % 2][:, :], ACT.Gelu, bias=b1[:, e:e + 1]).then_inc(act_done, 1)

                act.wait_ge(const_in, NCONST)
                batch_vectors(0)
                attention_rows(0)
                modulate(0, 0)
                second_weight(0)
                hidden(0, 0)
                hidden(0, 1)
                with act.Fori(0, B) as b:
                    for c in range(CPB):
                        i = b * CPB + c
                        act.wait_ge(mT_done, i + 1)
                        nc.scalar.copy(maskT[:, :], ps_a[1][0:E0, :, :].rearrange("p a f -> p (a f)")).then_inc(mT_out, 1)
                        attention_rows(i + 1)
                        act.wait_ge(x2_done, i)
                        act.wait_ge(b2_done, i + 1)
                        for k in range(2):
                            last = nc.scalar.copy(acc[:, 2 * k:2 * k + 2, :], ps_a[k][:, :, :])
                        last.then_inc(acc_set, 1)
                        for e in range(2, 6):
                            hidden(i, e)
                        if c == CPB - 1:
                            batch_vectors(b + 1)
                        modulate(i + 1, (c + 1) % 2)
                        hidden(i, 6)
                        hidden(i, 7)
                        second_weight(i + 1)
                        hidden(i + 1, 0)
                        hidden(i + 1, 1)

            @block.tensor
            def _(pe):
                def attention_rows(n, m, h):
                    pe.wait_ge(xo_in[h], 80 * m + 80)
                    pe.wait_ge(hT_done, n)
                    for k in range(KD):
                        for s in range(SUB):
                            o_tok = oin[h][:, s, :, :].rearrange("p g c -> p (g c)")[:, k * P:(k + 1) * P]
                            last = nc.tensor.transpose(ps_t[k][:, s * P:(s + 1) * P], o_tok, keep["ident"][:, :])
                    last.then_inc(tro_done, 1)

                def project(n, b1st):
                    pe.wait_ge(oT_done, n + 1)
                    pe.wait_ge(wob_done, b1st + 1)
                    pe.wait_ge(acc_set, n)
                    for s in range(SUB):
                        for k in range(KD):
                            last = nc.tensor.matmul(ps_a[s // 2][:, s % 2, :], oT[:, k, s * P:(s + 1) * P], wob[:, k, :], start=(k == 0), stop=(k == KD - 1))
                    last.then_inc(proj_done, 1)

                def normed_rows(n):
                    pe.wait_ge(xh2_done, n + 1)
                    for k in range(KD):
                        for s in range(SUB):
                            last = nc.tensor.transpose(ps_t[k][:, s * P:(s + 1) * P], xh2[:, s, k * P:(k + 1) * P], keep["ident"][:, :])
                    last.then_inc(trx_done, 1)

                def router(n, h):
                    pe.wait_ge(hT_done, n + 1)
                    for s in range(SUB):
                        for k in range(KD):
                            last = nc.tensor.matmul(ps_a[0][:, 0, s * E0:(s + 1) * E0], hT[h][:, k, s * P:(s + 1) * P], rw[:, k, :], start=(k == 0), stop=(k == KD - 1))
                    last.then_inc(lg_done, 1)

                def up(i, h, e):
                    if e > 0:
                        pe.wait_ge(act_done, i * E0 + e - 1)
                    elif not isinstance(i, int):
                        pe.wait_ge(act_done, i * E0 - 1)
                    for k in range(KD):
                        last = nc.tensor.matmul(ps_h[e % 2][:, :], w1[:, e, k, :], hT[h][:, k, :], start=(k == 0), stop=(k == KD - 1))
                    last.then_inc(h_done, 1)

                def down(i, e):
                    pe.wait_ge(act_done, i * E0 + e + 1)
                    for pair in range(2):
                        pe.wait_ge(f_read, (i * E0 + e) * 2 + (pair - 1 if e else 0))
                        for j in range(2):
                            s = 2 * pair + j
                            last = nc.tensor.matmul(ps_f[pair][:, j, :], act_e[e][:, s * P:(s + 1) * P], w2[:, e, :], start=True, stop=True)
                        last.then_inc(f_done, 1)

                pe.wait_ge(const_in, NCONST)
                attention_rows(0, 0, 0)
                project(0, 0)
                normed_rows(0)
                router(0, 0)
                up(0, 0, 0)
                up(0, 0, 1)
                with pe.Fori(0, B) as b:
                    for c in range(CPB):
                        i = b * CPB + c
                        h, h1, m1 = c % 2, (c + 1) % 2, b * 2 + (c + 1) // 2
                        pe.wait_ge(mask_done, i + 1)
                        for s in range(SUB):
                            last = nc.tensor.transpose(ps_a[1][0:E0, s // 2, (s % 2) * P:(s % 2 + 1) * P], mask[h][:, s, :], keep["ident"][:, :])
                        last.then_inc(mT_done, 1)
                        attention_rows(i + 1, m1, h1)
                        pe.wait_ge(mT_out, i + 1)
                        for s in range(SUB):
                            last = nc.tensor.matmul(ps_a[s // 2][:, s % 2, :], maskT[:, s * P:(s + 1) * P], b2[:, :], start=True, stop=True)
                        last.then_inc(b2_done, 1)
                        up(i, h, 2)
                        down(i, 0)
                        up(i, h, 3)
                        project(i + 1, b + (c + 1) // CPB)
                        down(i, 1)
                        up(i, h, 4)
                        down(i, 2)
                        up(i, h, 5)
                        normed_rows(i + 1)
                        down(i, 3)
                        up(i, h, 6)
                        down(i, 4)
                        up(i, h, 7)
                        pe.wait_ge(x1_done, i + 2)
                        router(i + 1, h1)
                        down(i, 5)
                        up(i + 1, h1, 0)
                        down(i, 6)
                        up(i + 1, h1, 1)
                        down(i, 7)


A_TURN = (["cum1", "seg1", "xT1", "ct4", "ct0", "ct1"]
          + ["gT0", "cum2", "seg2", "xT2", "out0", "ct2", "ct3", "dt"]
          + ["gT1", "cum3", "seg3", "xT3", "out1", "z0", "z1"]
          + ["gT2", "cum0", "seg0", "xT0", "out2", "z2", "z3", "gT3", "uT0", "uT1", "out3"])
A_FIRST = ["uT0", "uT1", "ct4", "ct0", "ct1", "ct2", "ct3", "dt", "z0", "z1", "z2", "z3", "vT0", "vT1", "cum0", "seg0", "xT0"]
A_BANKS = 4
A_POS = {n: len(A_FIRST) + k for k, n in enumerate(A_TURN)}
A_PRE = {n: k for k, n in enumerate(A_FIRST)}
CONV_GROUPS = [(4, 0), (1, 2), (3,)]


def scan_phase(nc, x, d, keep):
    ctx = ExitStack()
    with ctx:
        sb = lambda name, shape, dt=F32: ctx.enter_context(nc.sbuf_tensor("sc_" + name, shape, dt))
        ZX = 2 * DI + 2 * NS + NH
        RT = (2 * DI + 2 * NS) // P
        KO = DI // P
        win = sb("win", [P, KD, ZX])
        wout = sb("wout", [P, KO, D])
        upper, lower, ones = sb("upper", [P, P]), sb("lower", [P, P]), sb("ones", [P, P])
        dtb, a_neg, dvec = sb("dtb", [P, NH]), sb("a_neg", [P, NH]), sb("dvec", [P, NH])
        conv_w, conv_b = sb("conv_w", [P, CTL, TAPS]), sb("conv_b", [P, CTL])
        nw, nb, rms = sb("nw", [P, KD]), sb("nb", [P, KD]), sb("rms", [P, KO])
        gvec = sb("gvec", [P, 3, B + 1, D])
        g_front, g_back = sb("g_front", [P, 2, D]), sb("g_back", [P, D])
        ss, rs = sb("ss", [P, 16]), sb("rs", [P, 16])
        mhalf = sb("mhalf", [P, 16])
        xin = [sb(f"xin{h}", [P, SUB, D]) for h in range(4)]
        xh, uh = sb("xh", [P, SUB, D]), sb("uh", [P, SUB, D])
        st, mv = sb("st", [P, SUB, 6]), sb("mv", [P, SUB, 2])
        ve, rstd = sb("ve", [P, SUB]), sb("rstd", [P, SUB])
        uT = [sb(f"uT{h}", [P, KD, T]) for h in range(2)]
        CW = T + TAPS - 1
        xc_flat = [sb(f"xc{h}", [P, CTL * CW]) for h in range(2)]
        xc = [t[:, :].rearrange("p (c w) -> p c w", w=CW) for t in xc_flat]
        cv = sb("cv", [P, CTL, T])
        xs = [sb(f"xs{h}", [P, CTL, T]) for h in range(2)]
        cT = [sb(f"cT{h}", [NS, T]) for h in range(2)]
        sz = [sb(f"sz{h}", [P, SUB, DI]) for h in range(2)]
        dtr = sb("dtr", [P, SUB, NH])
        vraw, nabs, ez = sb("vraw", [P, SUB, NH]), sb("nabs", [P, SUB, NH]), sb("ez", [P, SUB, NH])
        zq, zw, zp = sb("zq", [P, SUB, NH]), sb("zw", [P, SUB, NH]), sb("zp", [P, SUB, NH])
        dts = [sb(f"dts{h}", [P, SUB, NH]) for h in range(2)]
        dA = [sb(f"dA{h}", [P, SUB, NH]) for h in range(2)]
        two = lambda name, shape: [sb(f"{name}{h}", shape) for h in range(2)]
        segm, decay, att = two("segm", [P, NH, P]), two("decay", [P, NH, P]), two("att", [P, NH, P])
        sm, btok, ex = two("sm", [P, P]), two("btok", [P, NS]), two("ex", [P, 3, NH])
        xtok, xdt, xde, xd = two("xtok", [P, NH, HP]), two("xdt", [P, NH, HP]), two("xde", [P, NH, HP]), two("xd", [P, NH, HP])
        ysum, g, gT = two("ysum", [P, NH, HP]), two("g", [P, DI]), two("gT", [P, KO, P])
        junk, ssq, osb = sb("junk", [P, DI]), sb("ssq", [P, SUB]), sb("osb", [P, SUB, D])
        state = sb("state", [NS, NH, HP])
        pb = lambda name: ctx.enter_context(nc.psum_tensor("sc_" + name, [P, 512], F32))
        ps_a = [pb(f"ps_a{k}") for k in range(A_BANKS)]
        ps_sc, ps_in, ps_y, ps_st = pb("ps_sc"), pb("ps_in"), pb("ps_y"), pb("ps_st")
        wbank = [ps_sc, ps_in, ps_y, ps_st]
        raw = xc_flat[0][:, 0:RT * D].rearrange("p (t f) -> p t f", f=D)
        raw_sq = xc_flat[1][:, 0:RT * D].rearrange("p (t f) -> p t f", f=D)
        cvf = cv[:, :, :].rearrange("p c t -> p (c t)")
        raw_o = cvf[:, 0:KD * DI].rearrange("p (o f) -> p o f", f=DI)
        raw_dt = cvf[0:NH, KD * DI:KD * DI + D]
        uhf = uh[:, :, :].rearrange("p s f -> p (s f)")
        raw_o_sq = uhf[:, 0:KD * DI].rearrange("p (o f) -> p o f", f=DI)
        raw_dt_sq = xh[0:NH, 0, :]

        sem = phase_semaphores(nc, ctx, "sc_")
        const_in, always, setup_v, setup_p, setup_a = sem("const_in"), sem("always"), sem("setup_v"), sem("setup_p"), sem("setup_a")
        w_done, w_read = sem("w_done"), sem("w_read")
        x_in = [sem(f"x_in{h}") for h in range(4)]
        x_stored = [sem(f"x_stored{h}") for h in range(4)]
        cT_in = [sem(f"cT_in{h}") for h in range(2)]
        a_done, a_out = sem("a_done"), sem("a_out")
        var_done, rstd_done, xh_done, h_done, uh_done = sem("var_done"), sem("rstd_done"), sem("xh_done"), sem("h_done"), sem("uh_done")
        conv_done, silu_done, nabs_done, ez_done, dA_done = sem("conv_done"), sem("silu_done"), sem("nabs_done"), sem("ez_done"), sem("dA_done")
        seg_set, xdt_done, att_done, xde_done, g_done = sem("seg_set"), sem("xdt_done"), sem("att_done"), sem("xde_done"), sem("g_done")
        sc_done, sc_read, in_done, in_read = sem("sc_done"), sem("sc_read"), sem("in_done"), sem("in_read")
        y_done, y_read, st_done, state_set = sem("y_done"), sem("y_read"), sem("st_done"), sem("state_set")
        ssq_done, osc_done, x3_done = sem("ssq_done"), sem("osc_done"), sem("x3_done")

        NCONST = 16 * (15 + 3 * (B + 1))
        TURN = len(A_TURN)
        RND = 7
        over_h = lambda v: v.unsqueeze(2).to_broadcast([P, NH, P])
        over_s = lambda v: v.unsqueeze(1).to_broadcast([P, SUB, D])

        def place(i, name):
            pos = A_PRE[name] if i is None else A_POS[name]
            return (pos if i is None else i * TURN + pos), pos % A_BANKS

        with nc.Block() as block:
            @block.sync
            def _(sp):
                sp.dma_start(raw, x["inw"][0:RT * P, :].rearrange("(t p) f -> p t f", p=P)).then_inc(const_in, 16)
                sp.dma_start(raw_dt, x["inw"][RT * P:ZX, :]).then_inc(const_in, 16)
                sp.dma_start(raw_o, x["outw"].rearrange("(o p) f -> p o f", p=P)).then_inc(const_in, 16)
                for t, name in ((upper, "upper"), (lower, "lower"), (ones, "ones_f"), (conv_b, "conv_b"), (nw, "xnw"), (nb, "xnb"), (rms, "rmsw")):
                    sp.dma_start(t[:, :], x[name]).then_inc(const_in, 16)
                sp.dma_start(conv_w[:, :, :], x["conv_w"]).then_inc(const_in, 16)
                for t, name in ((dtb, "dt_bias"), (a_neg, "A_log"), (dvec, "Dskip")):
                    sp.dma_start(t[:, :], x[name].partition_broadcast(P)).then_inc(const_in, 16)
                sp.dma_start(mhalf[:, :], x["mhalf"]).then_inc(const_in, 16)
                for n, r in enumerate((R_CA1, R_SA1, R_GA1)):
                    for b in range(B + 1):
                        sp.dma_start(gvec[:, n, b, :], d["rows"][r, min(b, B - 1), :].partition_broadcast(P)).then_inc(const_in, 16)

                def load(n, h):
                    sp.dma_start(xin[h][:, :, :], d["x2"][ds(n * T, T), :].rearrange("(s p) f -> p s f", p=P)).then_inc(x_in[h], 16)

                def move_c(n, m, h):
                    wait_alone(sp, silu_done, 3 * n + 1, always)
                    sp.dma_start(cT[h][:, :], xs[h][NS:2 * NS, CTL - 1, :]).then_inc(cT_in[h], 16)

                for n in range(3):
                    load(n, n)
                move_c(0, 0, 0)
                with sp.Fori(0, B) as b:
                    for c in range(CPB):
                        i = b * CPB + c
                        if c == 0:
                            wait_alone(sp, x_stored[3], 16 * b, always)
                        else:
                            wait_alone(sp, x_stored[c - 1], 16 * (b + 1), always)
                        load((i + 3) % NCH, (c + 3) % 4)
                        move_c(i + 1, b * 2 + (c + 1) // 2, (c + 1) % 2)
                        wait_alone(sp, x3_done, i + 1, always)
                        sp.dma_start(d["x3"][ds(i * T, T), :].rearrange("(s p) f -> p s f", p=P), xin[c][:, :, :]).then_inc(x_stored[c], 16)
                for h in range(4):
                    sp.wait_ge(x_stored[h], 16 * B)
                    sp.wait_ge(x_in[h], 16 * (B + (h < 3)))
                sp.wait_ge(cT_in[0], 16 * (NCH // 2 + 1))
                sp.wait_ge(cT_in[1], 16 * NCH // 2)

            @block.gpsimd
            def _(pool):
                def rsqrt(k):
                    pool.wait_ge(var_done, k + 1)
                    nc.gpsimd.tensor_tensor(rstd[:, :], ve[:, :], mhalf[:, 0:SUB], ALU.pow).then_inc(rstd_done, 1)

                def scale_shift(n):
                    pool.wait_ge(xh_done, n + 1)
                    nc.gpsimd.tensor_tensor(xh[:, :, :], xh[:, :, :], over_s(g_front[:, 0, :]), ALU.mult)
                    pool.drain()
                    nc.gpsimd.tensor_tensor(xh[:, :, :], xh[:, :, :], over_s(g_front[:, 1, :]), ALU.add).then_inc(h_done, 1)

                def front_vectors(b):
                    pool.drain()
                    nc.gpsimd.tensor_copy(g_front[:, :, :], gvec[:, 0:2, ds(b, 1), :].rearrange("p n b f -> p (n b) f"))
                    pool.drain()

                def segment_mask(n, h, s):
                    pool.wait_ge(dA_done, n + 1)
                    nc.gpsimd.tensor_tensor(segm[s % 2][:, :, :], lower[:, :].unsqueeze(1).to_broadcast([P, NH, P]),
                                            over_h(dA[h][:, s, :]), ALU.mult).then_inc(seg_set, 1)

                def weigh_inputs(i, s):
                    pool.wait_ge(xdt_done, i * SUB + s + 1)
                    nc.gpsimd.tensor_tensor(xde[s % 2][:, :, :], xdt[s % 2][:, :, :], over_h(ex[s % 2][:, 1, :]), ALU.mult).then_inc(xde_done, 1)
                    nc.gpsimd.tensor_tensor(xd[s % 2][:, :, :], xtok[s % 2][:, :, :], over_h(dvec[:, :]), ALU.mult)

                def gate(i, h, s):
                    pool.drain()
                    pool.wait_ge(y_read, i * SUB + s + 1)
                    nc.gpsimd.tensor_tensor(xd[s % 2][:, :, :], xd[s % 2][:, :, :], ysum[s % 2][:, :, :], ALU.add)
                    pool.drain()
                    nc.gpsimd.tensor_tensor(g[s % 2][:, :], xd[s % 2][:, :, :].rearrange("p h c -> p (h c)"), sz[h][:, s, :], ALU.mult).then_inc(g_done, 1)

                pool.sem_inc(always, 1)
                pool.wait_ge(const_in, NCONST)
                pool.wait_ge(setup_v, 1)
                nc.gpsimd.tensor_tensor(rs[:, :], ss[:, :], mhalf[:, :], ALU.pow).then_inc(setup_p, 1)
                front_vectors(0)
                for n in range(2):
                    rsqrt(2 * n)
                    scale_shift(n)
                    rsqrt(2 * n + 1)
                segment_mask(0, 0, 0)
                segment_mask(0, 0, 1)
                weigh_inputs(0, 0)
                with pool.Fori(0, B) as b:
                    pool.drain()
                    nc.gpsimd.tensor_copy(g_back[:, :], gvec[:, 2, ds(b, 1), :].rearrange("p b f -> p (b f)"))
                    pool.drain()
                    for c in range(CPB):
                        i = b * CPB + c
                        h = c % 2
                        for s in range(SUB):
                            gate(i, h, s)
                            if s < 2:
                                segment_mask(i, h, s + 2)
                            elif s == 3:
                                segment_mask(i + 1, 1 - h, 1)
                            weigh_inputs(i + (s + 1) // SUB, (s + 1) % SUB)
                            if s == 0:
                                if c == 2:
                                    front_vectors(b + 1)
                                rsqrt(4 + 3 * i)
                                scale_shift(i + 2)
                            if s == 2:
                                segment_mask(i + 1, 1 - h, 0)
                                rsqrt(5 + 3 * i)
                        rsqrt(6 + 3 * i)
                        pool.wait_ge(osc_done, i + 1)
                        nc.gpsimd.tensor_tensor(osb[:, :, :], osb[:, :, :], over_s(g_back[:, :]), ALU.mult)
                        pool.drain()
                        nc.gpsimd.tensor_tensor(xin[c][:, :, :], xin[c][:, :, :], osb[:, :, :], ALU.add).then_inc(x3_done, 1)

            @block.vector
            def _(dve):
                def variance(src):
                    for s in range(SUB):
                        nc.vector.bn_stats(st[:, s, :], src[:, s, :])
                    dve.drain()
                    for s in range(SUB):
                        nc.vector.bn_aggr(mv[:, s, :], st[:, s, :])
                    dve.drain()
                    nc.vector.tensor_scalar(ve[:, :], mv[:, :, 1], EPS, None, ALU.add).then_inc(var_done, 1)

                def scale_rows(dst, src, k):
                    dve.wait_ge(rstd_done, k + 1)
                    for s in range(SUB):
                        last = nc.vector.tensor_scalar(dst[:, s, :], src[:, s, :], mv[:, s, 0:1], rstd[:, s:s + 1], ALU.subtract, ALU.mult)
                    return last

                def first_variance(m, h):
                    dve.wait_ge(x_in[h], 16 * m + 16)
                    variance(xin[h])

                def first_norm(h, k):
                    scale_rows(xh, xin[h], k).then_inc(xh_done, 1)

                def second_variance(n):
                    dve.wait_ge(h_done, n + 1)
                    variance(xh)

                def second_norm(k):
                    scale_rows(uh, xh, k).then_inc(uh_done, 1)

                def convolve(i, n, h, grp, fresh):
                    if grp == 0:
                        if fresh:
                            nc.vector.memset(xc[h][:, :, 0:TAPS - 1], 0.0)
                        else:
                            nc.vector.tensor_copy(xc[h][:, :, 0:TAPS - 1], xc[1 - h][:, :, T:CW])
                        dve.drain()
                        dve.wait_ge(silu_done, 3 * n)
                    cts = CONV_GROUPS[grp]
                    for ct in cts:
                        dve.wait_ge(a_out, place(i, f"ct{ct}")[0] + 1)
                        nc.vector.tensor_scalar(cv[:, ct, :], xc[h][:, ct, 0:T], conv_w[:, ct, 0:1], conv_b[:, ct:ct + 1], ALU.mult, ALU.add)
                    for k in range(1, TAPS):
                        dve.drain()
                        for ct in cts:
                            last = nc.vector.scalar_tensor_tensor(cv[:, ct, :], xc[h][:, ct, k:k + T], conv_w[:, ct, k:k + 1], cv[:, ct, :], ALU.mult, ALU.add)
                    last.then_inc(conv_done, 1)

                def step_sizes(i, n):
                    dve.wait_ge(a_out, place(i, "dt")[0] + 1)
                    nc.vector.tensor_tensor(vraw[:, :, :], dtr[:, :, :], dtb[:, :].unsqueeze(1).to_broadcast([P, SUB, NH]), ALU.add)
                    dve.drain()
                    nc.vector.scalar_tensor_tensor(nabs[:, :, :], vraw[:, :, :], -1.0, vraw[:, :, :], ALU.mult, ALU.min).then_inc(nabs_done, 1)

                def softplus(n, h):
                    dve.wait_ge(ez_done, n + 1)
                    nc.vector.tensor_scalar(zp[:, :, :], ez[:, :, :], 2.0, None, ALU.add)
                    dve.drain()
                    nc.vector.reciprocal(zq[:, :, :], zp[:, :, :])
                    dve.drain()
                    nc.vector.tensor_tensor(zq[:, :, :], zq[:, :, :], ez[:, :, :], ALU.mult)
                    dve.drain()
                    nc.vector.tensor_tensor(zw[:, :, :], zq[:, :, :], zq[:, :, :], ALU.mult)
                    dve.drain()
                    nc.vector.tensor_scalar(zp[:, :, :], zw[:, :, :], 1.0 / 17, None, ALU.mult)
                    for k in range(15, 1, -2):
                        dve.drain()
                        nc.vector.scalar_tensor_tensor(zp[:, :, :], zp[:, :, :], 1.0 / k, zw[:, :, :], ALU.add, ALU.mult)
                    dve.drain()
                    nc.vector.scalar_tensor_tensor(zp[:, :, :], zp[:, :, :], 1.0, zq[:, :, :], ALU.add, ALU.mult)
                    nc.vector.tensor_scalar(vraw[:, :, :], vraw[:, :, :], 0.0, None, ALU.max)
                    dve.drain()
                    nc.vector.scalar_tensor_tensor(dts[h][:, :, :], zp[:, :, :], 2.0, vraw[:, :, :], ALU.mult, ALU.add)
                    dve.drain()
                    nc.vector.tensor_tensor(dA[h][:, :, :], dts[h][:, :, :], a_neg[:, :].unsqueeze(1).to_broadcast([P, SUB, NH]), ALU.mult).then_inc(dA_done, 1)

                def attention_weights(turn, i, h, s):
                    r = s % 2
                    dve.wait_ge(sc_done, i * SUB + s + 1)
                    nc.vector.tensor_tensor(sm[r][:, :], ps_sc[:, 0:P], upper[:, :], ALU.mult)
                    nc.vector.tensor_copy(btok[r][:, :], ps_sc[:, P:P + NS]).then_inc(sc_read, 1)
                    dve.wait_ge(a_out, place(turn, f"xT{s}")[0] + 1)
                    nc.vector.tensor_tensor(xdt[r][:, :, :], xtok[r][:, :, :], over_h(dts[h][:, s, :]), ALU.mult).then_inc(xdt_done, 1)
                    dve.drain()
                    nc.vector.tensor_tensor(att[r][:, :, :], decay[r][:, :, :], sm[r][:, :].unsqueeze(1).to_broadcast([P, NH, P]), ALU.mult).then_inc(att_done, 1)

                def outputs_and_state(i, s):
                    r = s % 2
                    heads = lambda t: t[:, :].rearrange("p (h c) -> p h c", h=NH)
                    dve.wait_ge(in_done, i * SUB + s + 1)
                    nc.vector.tensor_tensor(ysum[r][:, :, :], heads(ps_in), over_h(ex[r][:, 0, :]), ALU.mult).then_inc(in_read, 1)
                    dve.drain()
                    dve.wait_ge(y_done, i * SUB + s + 1)
                    nc.vector.tensor_tensor(ysum[r][:, :, :], ysum[r][:, :, :], heads(ps_y), ALU.add).then_inc(y_read, 1)
                    dve.wait_ge(st_done, i * SUB + s + 1)
                    for k in range(NH):
                        last = nc.vector.scalar_tensor_tensor(state[:, k, :], state[:, k, :], ex[r][0:NS, 2, k:k + 1], ps_st[0:NS, k * HP:(k + 1) * HP], ALU.mult, ALU.add)
                    last.then_inc(state_set, 1)

                dve.wait_ge(const_in, NCONST)
                nc.vector.memset(ss[:, :], 1.0)
                nc.vector.tensor_tensor(raw_sq, raw, raw, ALU.mult)
                nc.vector.tensor_tensor(raw_o_sq, raw_o, raw_o, ALU.mult)
                nc.vector.tensor_tensor(raw_dt_sq, raw_dt, raw_dt, ALU.mult)
                dve.drain()
                nc.vector.tensor_reduce(ss[:, 0:RT], raw_sq, AX.X, ALU.add)
                nc.vector.tensor_reduce(ss[:, RT:RT + KD], raw_o_sq, AX.X, ALU.add)
                nc.vector.tensor_reduce(ss[0:NH, RT + KD:RT + KD + 1], raw_dt_sq, AX.X, ALU.add)
                dve.drain()
                nc.vector.tensor_scalar(ss[:, :], ss[:, :], 1e-12, None, ALU.max).then_inc(setup_v, 1)
                dve.wait_ge(setup_p, 1)
                scale = float(D) ** -0.5
                nc.vector.scalar_tensor_tensor(raw, raw, scale, rs[:, 0:RT].unsqueeze(2).to_broadcast([P, RT, D]), ALU.mult, ALU.mult)
                nc.vector.tensor_tensor(raw_o, raw_o, rs[:, RT:RT + KD].unsqueeze(2).to_broadcast([P, KD, DI]), ALU.mult)
                nc.vector.tensor_scalar(raw_dt, raw_dt, rs[0:NH, RT + KD:RT + KD + 1], scale, ALU.mult, ALU.mult).then_inc(setup_v, 1)
                for r in range(RND):
                    dve.wait_ge(w_done, r + 1)
                    bank = wbank[r % 4]
                    if r < 4:
                        last = nc.vector.tensor_copy(win[:, :, 2 * r * P:(2 * r + 2) * P], bank[:, :].rearrange("p (k c) -> p k c", k=KD))
                    elif r == 4:
                        nc.vector.tensor_copy(win[:, :, 8 * P:9 * P], bank[:, 0:KD * P].rearrange("p (k c) -> p k c", k=KD))
                        last = nc.vector.tensor_copy(win[:, :, RT * P:ZX], bank[:, KD * P:KD * P + KD * NH].rearrange("p (k c) -> p k c", k=KD))
                    else:
                        for j in range(2):
                            ko = 2 * (r - 5) + j
                            last = nc.vector.tensor_scalar(wout[:, ko, :], bank[:, j * D:(j + 1) * D], rms[:, ko:ko + 1], None, ALU.mult)
                    last.then_inc(w_read, 1)
                dve.wait_ge(setup_a, 1)
                nc.vector.tensor_scalar(a_neg[:, :], a_neg[:, :], -1.0, None, ALU.mult)
                for n in range(2):
                    first_variance(0, n)
                    first_norm(n, 2 * n)
                    second_variance(n)
                    if n == 1:
                        dve.wait_ge(a_done, place(None, "uT1")[0] + 1)
                    second_norm(2 * n + 1)
                for grp in range(3):
                    convolve(None, 0, 0, grp, True)
                step_sizes(None, 0)
                softplus(0, 0)
                attention_weights(None, 0, 0, 0)
                with dve.Fori(0, B) as b:
                    dve.drain()
                    nc.vector.memset(state[:, :, :], 0.0).then_inc(state_set, 1)
                    for c in range(CPB):
                        i = b * CPB + c
                        h = c % 2
                        for s in range(SUB):
                            outputs_and_state(i, s)
                            if s == 2:
                                softplus(i + 1, 1 - h)
                            if s == 3:
                                second_norm(5 + 3 * i)
                            if s + 1 < SUB:
                                attention_weights(i, i, h, s + 1)
                            else:
                                attention_weights(i, i + 1, 1 - h, 0)
                            if s == 0:
                                first_variance(b + (c + 2) // 4, (c + 2) % 4)
                            if s < 3:
                                convolve(i, i + 1, 1 - h, s, c == CPB - 1)
                            if s == 0:
                                first_norm((c + 2) % 4, 4 + 3 * i)
                            if s == 1:
                                step_sizes(i, i + 1)
                            if s == 2:
                                second_variance(i + 2)
                        dve.wait_ge(ssq_done, i * SUB + SUB)
                        nc.vector.tensor_scalar(ve[:, :], ssq[:, :], 1.0 / DI, EPS, ALU.mult, ALU.add).then_inc(var_done, 1)
                        dve.wait_ge(rstd_done, 7 + 3 * i)
                        dve.wait_ge(a_out, place(i, "out3")[0] + 1)
                        for s in range(SUB):
                            last = nc.vector.tensor_scalar(osb[:, s, :], osb[:, s, :], rstd[:, s:s + 1], None, ALU.mult)
                        last.then_inc(osc_done, 1)

            @block.scalar
            def _(act):
                def take(i, name):
                    k, bank = place(i, name)
                    act.wait_ge(a_done, k + 1)
                    return ps_a[bank]

                def decays(i, s):
                    bank = take(i, f"cum{s}")
                    nc.scalar.activation(ex[s % 2][:, :, :], bank[:, 0:3 * NH].rearrange("p (a h) -> p a h", a=3), ACT.Exp).then_inc(a_out, 1)
                    bank = take(i, f"seg{s}")
                    nc.scalar.activation(decay[s % 2][:, :, :], bank[:, :].rearrange("p (h c) -> p h c", h=NH), ACT.Exp).then_inc(a_out, 1)

                def token_inputs(i, s):
                    bank = take(i, f"xT{s}")
                    nc.scalar.copy(xtok[s % 2][:, :, :], bank[:, :].rearrange("p (h c) -> p h c", h=NH)).then_inc(a_out, 1)

                def conv_inputs(i, h, ct):
                    bank = take(i, f"ct{ct}")
                    nc.scalar.copy(xc[h][:, ct, TAPS - 1:CW], bank[:, :]).then_inc(a_out, 1)

                def steps(i):
                    bank = take(i, "dt")
                    nc.scalar.copy(dtr[:, :, :], bank[:, 0:SUB * NH].rearrange("p (s h) -> p s h", s=SUB)).then_inc(a_out, 1)

                def gates(i, h, s):
                    bank = take(i, f"z{s}")
                    nc.scalar.activation(sz[h][:, s, :], bank[:, :], ACT.Silu).then_inc(a_out, 1)

                def conv_silu(n, h, grp):
                    act.wait_ge(conv_done, 3 * n + grp + 1)
                    for ct in CONV_GROUPS[grp]:
                        last = nc.scalar.activation(xs[h][:, ct, :], cv[:, ct, :], ACT.Silu)
                    last.then_inc(silu_done, 1)

                def step_exp(n):
                    act.wait_ge(nabs_done, n + 1)
                    nc.scalar.activation(ez[:, :, :], nabs[:, :, :], ACT.Exp).then_inc(ez_done, 1)

                def normed(i, h, names):
                    for k in range(KD):
                        bank = take(i, names[k])
                        nc.scalar.activation(uT[h][:, k, :], bank[:, :], ACT.Identity, scale=nw[:, k:k + 1], bias=nb[:, k:k + 1]).then_inc(a_out, 1)

                def gated_columns(i, s):
                    bank = take(i, f"gT{s}")
                    nc.scalar.copy(gT[s % 2][:, :, :], bank[:, :].rearrange("p (k c) -> p k c", k=KO)).then_inc(a_out, 1)
                    nc.scalar.activation(junk[:, :], g[s % 2][:, :], ACT.Square, accum_out=ssq[:, s:s + 1]).then_inc(ssq_done, 1)

                def projected(i, s):
                    bank = take(i, f"out{s}")
                    if s == 0:
                        act.wait_ge(x3_done, i)
                    nc.scalar.copy(osb[:, s, :], bank[:, 0:D]).then_inc(a_out, 1)

                act.wait_ge(const_in, NCONST)
                nc.scalar.activation(a_neg[:, :], a_neg[:, :], ACT.Exp).then_inc(setup_a, 1)
                normed(None, 0, ("uT0", "uT1"))
                act.wait_ge(w_read, RND)
                for ct in (4, 0, 1, 2, 3):
                    conv_inputs(None, 0, ct)
                steps(None)
                for s in range(SUB):
                    gates(None, 0, s)
                for grp in range(3):
                    conv_silu(0, 0, grp)
                step_exp(0)
                normed(None, 1, ("vT0", "vT1"))
                decays(None, 0)
                token_inputs(None, 0)
                with act.Fori(0, B) as b:
                    for c in range(CPB):
                        i = b * CPB + c
                        h = c % 2
                        decays(i, 1)
                        token_inputs(i, 1)
                        for ct in (4, 0, 1):
                            conv_inputs(i, 1 - h, ct)
                        gated_columns(i, 0)
                        decays(i, 2)
                        token_inputs(i, 2)
                        projected(i, 0)
                        conv_inputs(i, 1 - h, 2)
                        conv_inputs(i, 1 - h, 3)
                        steps(i)
                        step_exp(i + 1)
                        gated_columns(i, 1)
                        decays(i, 3)
                        token_inputs(i, 3)
                        projected(i, 1)
                        gates(i, 1 - h, 0)
                        gates(i, 1 - h, 1)
                        conv_silu(i + 1, 1 - h, 0)
                        conv_silu(i + 1, 1 - h, 1)
                        gated_columns(i, 2)
                        conv_silu(i + 1, 1 - h, 2)
                        decays(i, 0)
                        token_inputs(i, 0)
                        projected(i, 2)
                        gates(i, 1 - h, 2)
                        gates(i, 1 - h, 3)
                        gated_columns(i, 3)
                        normed(i, h, ("uT0", "uT1"))
                        projected(i, 3)

            @block.tensor
            def _(pe):
                def into(i, name):
                    k, bank = place(i, name)
                    if i is not None:
                        pe.wait_ge(a_out, k - A_BANKS + 1)
                    elif k >= A_BANKS:
                        pe.wait_ge(a_out, k - A_BANKS + 1)
                    return ps_a[bank]

                def normed(i, n, names):
                    pe.wait_ge(uh_done, n + 1)
                    for k in range(KD):
                        bank = into(i, names[k])
                        for s in range(SUB):
                            last = nc.tensor.transpose(bank[:, s * P:(s + 1) * P], uh[:, s, k * P:(k + 1) * P], keep["ident"][:, :])
                        last.then_inc(a_done, 1)

                def conv_inputs(i, h, ct):
                    bank = into(i, f"ct{ct}")
                    for k in range(KD):
                        last = nc.tensor.matmul(bank[:, :], win[:, k, DI + ct * P:DI + (ct + 1) * P], uT[h][:, k, :], start=(k == 0), stop=(k == KD - 1))
                    last.then_inc(a_done, 1)

                def gates(i, h, s):
                    bank = into(i, f"z{s}")
                    for k in range(KD):
                        last = nc.tensor.matmul(bank[:, :], uT[h][:, k, s * P:(s + 1) * P], win[:, k, 0:DI], start=(k == 0), stop=(k == KD - 1))
                    last.then_inc(a_done, 1)

                def steps(i, h):
                    bank = into(i, "dt")
                    for s in range(SUB):
                        for k in range(KD):
                            last = nc.tensor.matmul(bank[:, s * NH:(s + 1) * NH], uT[h][:, k, s * P:(s + 1) * P], win[:, k, RT * P:ZX], start=(k == 0), stop=(k == KD - 1))
                    last.then_inc(a_done, 1)

                def decays(turn, i, h, s):
                    bank = into(turn, f"cum{s}")
                    pe.wait_ge(dA_done, i + 1)
                    for k, m in enumerate((upper, lower, ones)):
                        last = nc.tensor.matmul(bank[:, k * NH:(k + 1) * NH], m[:, :], dA[h][:, s, :], start=True, stop=True)
                    last.then_inc(a_done, 1)
                    bank = into(turn, f"seg{s}")
                    pe.wait_ge(seg_set, i * SUB + s + 1)
                    for k in range(NH):
                        last = nc.tensor.matmul(bank[:, k * P:(k + 1) * P], segm[s % 2][:, k, :], upper[:, :], start=True, stop=True)
                    last.then_inc(a_done, 1)

                def scores(i, h, m, s):
                    cols = slice(s * P, (s + 1) * P)
                    if s == 0:
                        pe.wait_ge(cT_in[h], 16 * m + 16)
                    pe.wait_ge(sc_read, i * SUB + s)
                    nc.tensor.matmul(ps_sc[:, 0:P], xs[h][0:NS, CTL - 1, cols], cT[h][:, cols], start=True, stop=True)
                    nc.tensor.transpose(ps_sc[:, P:P + NS], xs[h][0:NS, CTL - 1, cols], keep["ident"][0:NS, 0:NS]).then_inc(sc_done, 1)

                def token_inputs(turn, i, h, s):
                    bank = into(turn, f"xT{s}")
                    if s == 0:
                        pe.wait_ge(silu_done, 3 * i + 3)
                    for k in range(NH):
                        last = nc.tensor.transpose(bank[:, k * P:(k + 1) * P], xs[h][:, k, s * P:(s + 1) * P], keep["ident"][:, :])
                    last.then_inc(a_done, 1)

                def outputs(i, b, c, h, s):
                    pe.wait_ge(state_set, b * (SUB * CPB + 1) + c * SUB + s + 1)
                    pe.wait_ge(in_read, i * SUB + s)
                    nc.tensor.matmul(ps_in[:, :], cT[h][:, s * P:(s + 1) * P], state[:, :, :].rearrange("n h c -> n (h c)"), start=True, stop=True).then_inc(in_done, 1)
                    pe.wait_ge(att_done, i * SUB + s + 1)
                    pe.wait_ge(y_read, i * SUB + s)
                    for k in range(NH):
                        last = nc.tensor.matmul(ps_y[:, k * HP:(k + 1) * HP], att[s % 2][:, k, :], xdt[s % 2][:, k, :], start=True, stop=True)
                    last.then_inc(y_done, 1)
                    pe.wait_ge(xde_done, i * SUB + s + 1)
                    nc.tensor.matmul(ps_st[0:NS, :], btok[s % 2][:, :], xde[s % 2][:, :, :].rearrange("p h c -> p (h c)"), start=True, stop=True).then_inc(st_done, 1)

                def gated_columns(i, s):
                    bank = into(i, f"gT{s}")
                    pe.wait_ge(g_done, i * SUB + s + 1)
                    for k in range(KO):
                        last = nc.tensor.transpose(bank[:, k * P:(k + 1) * P], g[s % 2][:, k * P:(k + 1) * P], keep["ident"][:, :])
                    last.then_inc(a_done, 1)

                def project(i, s):
                    bank = into(i, f"out{s}")
                    pe.wait_ge(a_out, place(i, f"gT{s}")[0] + 1)
                    for k in range(KO):
                        last = nc.tensor.matmul(bank[:, 0:D], gT[s % 2][:, k, :], wout[:, k, :], start=(k == 0), stop=(k == KO - 1))
                    last.then_inc(a_done, 1)

                pe.wait_ge(const_in, NCONST)
                pe.wait_ge(setup_v, 2)
                for r in range(RND):
                    if r >= 4:
                        pe.wait_ge(w_read, r - 3)
                    bank = wbank[r % 4]
                    if r < 4:
                        for k in range(KD):
                            for t in range(2):
                                last = nc.tensor.transpose(bank[:, (2 * k + t) * P:(2 * k + t + 1) * P], raw[:, 2 * r + t, k * P:(k + 1) * P], keep["ident"][:, :])
                    elif r == 4:
                        for k in range(KD):
                            nc.tensor.transpose(bank[:, k * P:(k + 1) * P], raw[:, 8, k * P:(k + 1) * P], keep["ident"][:, :])
                        for k in range(KD):
                            last = nc.tensor.transpose(bank[:, KD * P + k * NH:KD * P + (k + 1) * NH], raw_dt[:, k * P:(k + 1) * P], keep["ident"][0:NH, 0:NH])
                    else:
                        for j in range(2):
                            for o in range(KD):
                                ko = 2 * (r - 5) + j
                                last = nc.tensor.transpose(bank[:, (2 * j + o) * P:(2 * j + o + 1) * P], raw_o[:, o, ko * P:(ko + 1) * P], keep["ident"][:, :])
                    last.then_inc(w_done, 1)
                pe.wait_ge(w_read, RND)
                normed(None, 0, ("uT0", "uT1"))
                pe.wait_ge(a_out, place(None, "uT1")[0] + 1)
                for ct in (4, 0, 1, 2, 3):
                    conv_inputs(None, 0, ct)
                steps(None, 0)
                for s in range(SUB):
                    gates(None, 0, s)
                normed(None, 1, ("vT0", "vT1"))
                decays(None, 0, 0, 0)
                scores(0, 0, 0, 0)
                token_inputs(None, 0, 0, 0)
                with pe.Fori(0, B) as b:
                    for c in range(CPB):
                        i = b * CPB + c
                        h, m = c % 2, b * 2 + c // 2
                        fill = ("ct4", "ct0", "ct1"), ("ct2", "ct3", "dt"), ("z0", "z1"), ("z2", "z3")
                        for s in range(SUB):
                            outputs(i, b, c, h, s)
                            if s > 0:
                                gated_columns(i, s - 1)
                            nxt = (i, h, m, s + 1) if s + 1 < SUB else (i + 1, 1 - h, b * 2 + (c + 1) // 2, 0)
                            decays(i, nxt[0], nxt[1], nxt[3])
                            scores(*nxt)
                            token_inputs(i, nxt[0], nxt[1], nxt[3])
                            if s > 0:
                                project(i, s - 1)
                            for name in fill[s]:
                                if name[0] == "c":
                                    conv_inputs(i, 1 - h, int(name[2:]))
                                elif name[0] == "z":
                                    gates(i, 1 - h, int(name[1:]))
                                else:
                                    steps(i, 1 - h)
                        gated_columns(i, 3)
                        normed(i, i + 2, ("uT0", "uT1"))
                        project(i, 3)


def route_phase(nc, x, d, keep):
    ctx = ExitStack()
    with ctx:
        sb = lambda name, shape, dt=F32: ctx.enter_context(nc.sbuf_tensor("ro_" + name, shape, dt))
        wg, bg, iota = sb("wg", [P, KD, E1]), sb("bg", [P, E1]), sb("iota", [P, E1])
        upper, ones = sb("upper", [P, P]), sb("ones", [P, P])
        gvec, g_cur = sb("gvec", [P, 2, B, D]), sb("g_cur", [P, 2, D])
        mhalf = sb("mhalf", [P, SUB])
        xin = [sb(f"xin{h}", [P, SUB, D]) for h in range(2)]
        st, mv = sb("st", [P, SUB, 6]), sb("mv", [P, SUB, 2])
        ve, rstd = sb("ve", [P, SUB]), sb("rstd", [P, SUB])
        xh = sb("xh", [P, SUB, D])
        rows = [sb(f"rows{h}", [P, SUB, D]) for h in range(2)]
        rT = sb("rT", [P, KD, T])
        lg, mx8, ix = sb("lg", [P, SUB, E1]), sb("mx8", [P, SUB, 8]), sb("ix", [P, SUB, 8], U32)
        ixf, low, ex = sb("ixf", [P, SUB]), sb("low", [P, SUB, E1]), sb("ex", [P, SUB, E1])
        den, gate = sb("den", [P, SUB]), sb("gate", [P, SUB])
        pick, count = sb("pick", [P, SUB, E1]), sb("count", [P, E1])
        upto, pos, inside = sb("upto", [P, SUB, E1]), sb("pos", [P, SUB]), sb("inside", [P, SUB])
        place = sb("place", [P, SUB])
        slot = [sb(f"slot{h}", [P, SUB], U32) for h in range(2)]
        away = [sb(f"away{h}", [P, SUB], U32) for h in range(2)]
        target = [sb(f"target{h}", [P, SUB], U32) for h in range(2)]
        pb = lambda name, shape: ctx.enter_context(nc.psum_tensor("ro_" + name, shape, F32))
        ps_t = [pb(f"ps_t{k}", [P, T]) for k in range(KD)]
        ps_l, ps_c = pb("ps_l", [P, SUB, E1]), pb("ps_c", [P, SUB + 1, E1])
        sem = phase_semaphores(nc, ctx, "ro_")
        const_in, always = sem("const_in"), sem("always")
        x_in = [sem(f"x_in{h}") for h in range(2)]
        var_done, rstd_done, xh_done, rows_done = sem("var_done"), sem("rstd_done"), sem("xh_done"), sem("rows_done")
        tr_done, rT_done, lg_done, lg_read = sem("tr_done"), sem("rT_done"), sem("lg_done"), sem("lg_read")
        low_done, ex_done, pick_done, c_done, c_read = sem("low_done"), sem("ex_done"), sem("pick_done"), sem("c_done"), sem("c_read")
        slot_done = sem("slot_done")
        moved = [sem(f"moved{h}") for h in range(2)]
        over = lambda v: v.unsqueeze(1).to_broadcast([P, SUB, D])
        NCONST = 16 * (5 + 2 * B)

        with nc.Block() as block:
            @block.sync
            def _(sp):
                def load(n, h):
                    sp.dma_start(xin[h][:, :, :], d["x3"][ds(n * T, T), :].rearrange("(s p) f -> p s f", p=P)).then_inc(x_in[h], 16)

                load(0, 0)
                sp.dma_start(wg[:, :, :], x["wg"].rearrange("(k p) e -> p k e", p=P)).then_inc(const_in, 16)
                sp.dma_start(bg[:, :], x["bg"].partition_broadcast(P)).then_inc(const_in, 16)
                for t, name in ((iota, "iota"), (upper, "upper"), (ones, "ones_f")):
                    sp.dma_start(t[:, :], x[name]).then_inc(const_in, 16)
                for n, r in enumerate((R_CB1, R_SB1)):
                    for b in range(B):
                        sp.dma_start(gvec[:, n, b, :], d["rows"][r, b, :].partition_broadcast(P)).then_inc(const_in, 16)
                load(1, 1)
                with sp.Fori(0, NCH // 2 - 1) as m:
                    for h in range(2):
                        wait_alone(sp, xh_done, m * 2 + h + 1, always)
                        load(m * 2 + h + 2, h)

            @block.gpsimd
            def _(pool):
                nc.gpsimd.memset(mhalf[:, :], -0.5)
                pool.sem_inc(always, 1)
                pool.wait_ge(const_in, NCONST)

                def scatter(m, h):
                    pool.wait_ge(slot_done, m * 2 + h + 1)
                    nc.gpsimd.tensor_tensor(target[h][:, :], slot[h][:, :], away[h][:, :], ALU.add)
                    pool.drain()
                    for s in range(SUB):
                        nc.gpsimd.indirect_dma_start(d["buf"], bass.IndirectOffsetOnAxis(ap=target[h][:, s:s + 1], axis=0),
                                                     rows[h][:, s, :], None, bounds_check=N - 1, oob_is_err=False).then_inc(moved[h], 16)

                def make_rows(i, m, h):
                    pool.wait_ge(var_done, i + 1)
                    nc.gpsimd.tensor_tensor(rstd[:, :], ve[:, :], mhalf[:, :], ALU.pow).then_inc(rstd_done, 1)
                    pool.wait_ge(xh_done, i + 1)
                    wait_alone(pool, moved[h], 16 * SUB * m, always)
                    nc.gpsimd.tensor_tensor(rows[h][:, :, :], xh[:, :, :], over(g_cur[:, 0, :]), ALU.mult)
                    pool.drain()
                    nc.gpsimd.tensor_tensor(rows[h][:, :, :], rows[h][:, :, :], over(g_cur[:, 1, :]), ALU.add).then_inc(rows_done, 1)

                def batch_vectors(b):
                    pool.drain()
                    nc.gpsimd.tensor_copy(g_cur[:, :, :], gvec[:, :, ds(b, 1), :].rearrange("p n b f -> p (n b) f"))
                    pool.drain()

                def batch(b, last):
                    for c in range(CPB):
                        if c < CPB - 1 or not last:
                            if c == CPB - 1:
                                batch_vectors(b + 1)
                            make_rows(b * CPB + c + 1, b * 2 + (c + 1) // 2, (c + 1) % 2)
                        scatter(b * 2 + c // 2, c % 2)

                batch_vectors(0)
                make_rows(0, 0, 0)
                with pool.Fori(0, B - 1) as b:
                    batch(b, False)
                batch(B - 1, True)
                for h in range(2):
                    pool.wait_ge(moved[h], 16 * SUB * NCH // 2)

            @block.vector
            def _(dve):
                def norm(n, m, h):
                    dve.wait_ge(x_in[h], 16 * m + 16)
                    for s in range(SUB):
                        nc.vector.bn_stats(st[:, s, :], xin[h][:, s, :])
                    dve.drain()
                    for s in range(SUB):
                        nc.vector.bn_aggr(mv[:, s, :], st[:, s, :])
                    dve.drain()
                    nc.vector.tensor_scalar(ve[:, :], mv[:, :, 1], EPS, None, ALU.add).then_inc(var_done, 1)
                    dve.wait_ge(rows_done, n)
                    dve.wait_ge(rstd_done, n + 1)
                    for s in range(SUB):
                        last = nc.vector.tensor_scalar(xh[:, s, :], xin[h][:, s, :], mv[:, s, 0:1], rstd[:, s:s + 1], ALU.subtract, ALU.mult)
                    last.then_inc(xh_done, 1)

                def best(n):
                    dve.wait_ge(lg_done, n + 1)
                    nc.vector.tensor_tensor(lg[:, :, :], ps_l[:, :, :], bg[:, :].unsqueeze(1).to_broadcast([P, SUB, E1]), ALU.add).then_inc(lg_read, 1)
                    dve.drain()
                    for s in range(SUB):
                        nc.vector.max(mx8[:, s, :], lg[:, s, :])
                    dve.drain()
                    for s in range(SUB):
                        nc.vector.max_index(ix[:, s, :], mx8[:, s, :], lg[:, s, :])
                    nc.vector.tensor_tensor(low[:, :, :], lg[:, :, :], mx8[:, :, 0:1].to_broadcast([P, SUB, E1]), ALU.subtract).then_inc(low_done, 1)
                    dve.drain()
                    nc.vector.tensor_copy(ixf[:, :], ix[:, :, 0])
                    dve.drain()
                    dve.wait_ge(c_done, n)
                    nc.vector.tensor_tensor(pick[:, :, :], iota[:, :].unsqueeze(1).to_broadcast([P, SUB, E1]),
                                            ixf[:, :].unsqueeze(2).to_broadcast([P, SUB, E1]), ALU.is_equal).then_inc(pick_done, 1)

                def places(n, m, h):
                    dve.wait_ge(c_done, n + 1)
                    nc.vector.tensor_tensor(upto[:, :, :], ps_c[:, 0:SUB, :], count[:, :].unsqueeze(1).to_broadcast([P, SUB, E1]), ALU.add)
                    dve.drain()
                    nc.vector.tensor_tensor(count[:, :], count[:, :], ps_c[:, SUB, :], ALU.add).then_inc(c_read, 1)
                    nc.vector.tensor_tensor(upto[:, :, :], upto[:, :, :], pick[:, :, :], ALU.mult)
                    dve.drain()
                    nc.vector.tensor_reduce(pos[:, :], upto[:, :, :], AX.X, ALU.add)
                    dve.wait_ge(ex_done, n + 1)
                    nc.vector.tensor_reduce(den[:, :], ex[:, :, :], AX.X, ALU.add)
                    dve.drain()
                    nc.vector.reciprocal(gate[:, :], den[:, :])
                    nc.vector.tensor_scalar(inside[:, :], pos[:, :], float(CAP), None, ALU.is_le)
                    dve.wait_ge(moved[h], 16 * SUB * m)
                    nc.vector.tensor_scalar(place[:, :], pos[:, :], float(CAP), -1.0, ALU.min, ALU.add)
                    nc.vector.tensor_scalar(away[h][:, :], pos[:, :], float(CAP), float(2 * N), ALU.is_gt, ALU.mult)
                    dve.drain()
                    nc.vector.scalar_tensor_tensor(slot[h][:, :], ixf[:, :], float(CAP), place[:, :], ALU.mult, ALU.add).then_inc(slot_done, 1)
                    nc.vector.tensor_tensor(keep["gate"][:, ds(n * SUB, SUB)], gate[:, :], inside[:, :], ALU.mult)
                    dve.drain()
                    nc.vector.tensor_copy(keep["slot"][:, ds(n * SUB, SUB)], slot[h][:, :])

                nc.vector.memset(count[:, :], 0.0)
                dve.wait_ge(const_in, NCONST)
                norm(0, 0, 0)
                with dve.Fori(0, NCH // 2 - 1) as m:
                    for h in range(2):
                        best(m * 2 + h)
                        norm(m * 2 + h + 1, m + h, 1 - h)
                        places(m * 2 + h, m, h)
                best(NCH - 2)
                norm(NCH - 1, NCH // 2 - 1, 1)
                places(NCH - 2, NCH // 2 - 1, 0)
                best(NCH - 1)
                places(NCH - 1, NCH // 2 - 1, 1)

            @block.scalar
            def _(act):
                with act.Fori(0, NCH) as i:
                    act.wait_ge(tr_done, i + 1)
                    for k in range(KD):
                        last = nc.scalar.copy(rT[:, k, :], ps_t[k][:, :])
                    last.then_inc(rT_done, 1)
                    act.wait_ge(low_done, i + 1)
                    nc.scalar.activation(ex[:, :, :], low[:, :, :], ACT.Exp).then_inc(ex_done, 1)

            @block.tensor
            def _(pe):
                pe.wait_ge(const_in, NCONST)
                with pe.Fori(0, NCH // 2) as m:
                    for h in range(2):
                        i = m * 2 + h
                        pe.wait_ge(rows_done, i + 1)
                        for k in range(KD):
                            for s in range(SUB):
                                last = nc.tensor.transpose(ps_t[k][:, s * P:(s + 1) * P], rows[h][:, s, k * P:(k + 1) * P], keep["ident"][:, :])
                        last.then_inc(tr_done, 1)
                        pe.wait_ge(rT_done, i + 1)
                        pe.wait_ge(lg_read, i)
                        for s in range(SUB):
                            for k in range(KD):
                                last = nc.tensor.matmul(ps_l[:, s, :], rT[:, k, s * P:(s + 1) * P], wg[:, k, :], start=(k == 0), stop=(k == KD - 1))
                        last.then_inc(lg_done, 1)
                        pe.wait_ge(pick_done, i + 1)
                        pe.wait_ge(c_read, i)
                        for s in range(SUB + 1):
                            for s2 in range(min(s + 1, SUB)):
                                last = nc.tensor.matmul(ps_c[:, s, :], (upper if s2 == s else ones)[:, :], pick[:, s2, :],
                                                        start=(s2 == 0), stop=(s2 == min(s, SUB - 1)))
                        last.then_inc(c_done, 1)


def clear_phase(nc, x, d, keep):
    ctx = ExitStack()
    with ctx:
        zeros = ctx.enter_context(nc.sbuf_tensor("cl_zeros", [P, N // P // 4, D], F32))
        sem = phase_semaphores(nc, ctx, "cl_")
        zeros_set, cleared = sem("zeros_set"), sem("cleared")
        with nc.Block() as block:
            @block.vector
            def _(dve):
                nc.vector.memset(zeros[:, :, :], 0.0).then_inc(zeros_set, 1)

            @block.sync
            def _(sp):
                sp.wait_ge(zeros_set, 1)
                for k in range(4):
                    sp.dma_start(d["buf"][k * N // 4:(k + 1) * N // 4, :].rearrange("(p r) f -> p r f", p=P), zeros[:, :, :]).then_inc(cleared, 16)
                sp.wait_ge(cleared, 64)


def expert_phase(nc, x, d, keep):
    ctx = ExitStack()
    with ctx:
        sb = lambda name, shape, dt=F32: ctx.enter_context(nc.sbuf_tensor("ex_" + name, shape, dt))
        FT = F1 // P
        CS = CAP // P
        two = lambda name, shape: [sb(f"{name}{h}", shape) for h in range(2)]
        w1, w2, b1, b2 = two("w1", [P, KD, F1]), two("w2", [P, FT, D]), two("b1", [P, FT]), two("b2", [P, D])
        buf, bT = two("buf", [P, CS, D]), two("bT", [P, KD, CAP])
        hid = two("hid", [P, CAP])
        y = two("y", [P, CS, D])
        pb = lambda name, shape: ctx.enter_context(nc.psum_tensor("ex_" + name, shape, F32))
        ps_t = [pb(f"ps_t{k}", [P, CAP]) for k in range(KD)]
        ps_h = [pb(f"ps_h{k}", [P, CAP]) for k in range(2)]
        ps_y = [[pb(f"ps_y{h}{k}", [P, 2, D]) for k in range(2)] for h in range(2)]
        sem = phase_semaphores(nc, ctx, "ex_")
        always = sem("always")
        buf_in = [sem(f"buf_in{h}") for h in range(2)]
        w_in = [sem(f"w_in{h}") for h in range(2)]
        stored = [sem(f"stored{h}") for h in range(2)]
        tr_done, bT_done, h_done, hid_done, y_done, y_out = sem("tr_done"), sem("bT_done"), sem("h_done"), sem("hid_done"), sem("y_done"), sem("y_out")
        PAIRS = E1 // 2

        with nc.Block() as block:
            @block.sync
            def _(sp):
                def load(e, h):
                    sp.dma_start(buf[h][:, :, :], d["buf"][ds(e * CAP, CAP), :].rearrange("(s p) f -> p s f", p=P)).then_inc(buf_in[h], 16)
                    sp.dma_start(w1[h][:, :, :], x["fw1"][ds(e, 1), :, :].rearrange("e (k p) f -> p (e k) f", p=P)).then_inc(w_in[h], 16)
                    sp.dma_start(w2[h][:, :, :], x["fw2"][ds(e, 1), :, :].rearrange("e (k p) f -> p (e k) f", p=P)).then_inc(w_in[h], 16)
                    sp.dma_start(b1[h][:, :], x["fb1"][ds(e, 1), :, :].rearrange("e p k -> p (e k)")).then_inc(w_in[h], 16)
                    sp.dma_start(b2[h][:, :], x["fb2"][ds(e, 1), :].rearrange("e f -> (e f)").partition_broadcast(P)).then_inc(w_in[h], 16)

                def store(e, h):
                    wait_alone(sp, y_out, e + 1, always)
                    sp.dma_start(d["y"][ds(e * CAP, CAP), :].rearrange("(s p) f -> p s f", p=P), y[h][:, :, :]).then_inc(stored[h], 16)

                load(0, 0)
                load(1, 1)
                with sp.Fori(0, PAIRS - 1) as m:
                    for h in range(2):
                        store(m * 2 + h, h)
                        load(m * 2 + h + 2, h)
                for h in range(2):
                    store(E1 - 2 + h, h)
                for h in range(2):
                    sp.wait_ge(stored[h], 16 * PAIRS)

            @block.vector
            def _(dve):
                def columns(e, h):
                    dve.wait_ge(tr_done, e + 1)
                    for k in range(KD):
                        last = nc.vector.tensor_copy(bT[h][:, k, :], ps_t[k][:, :])
                    last.then_inc(bT_done, 1)

                def sums(e, m, h):
                    dve.wait_ge(y_done, e + 1)
                    dve.wait_ge(stored[h], 16 * m)
                    for k in range(2):
                        last = nc.vector.tensor_tensor(y[h][:, 2 * k:2 * k + 2, :], ps_y[h][k][:, :, :], b2[h][:, :].unsqueeze(1).to_broadcast([P, 2, D]), ALU.add)
                    last.then_inc(y_out, 1)

                dve.sem_inc(always, 1)
                columns(0, 0)
                with dve.Fori(0, PAIRS - 1) as m:
                    for h in range(2):
                        columns(m * 2 + h + 1, 1 - h)
                        sums(m * 2 + h, m, h)
                columns(E1 - 1, 1)
                sums(E1 - 2, PAIRS - 1, 0)
                sums(E1 - 1, PAIRS - 1, 1)

            @block.scalar
            def _(act):
                with act.Fori(0, PAIRS) as m:
                    for h in range(2):
                        act.wait_ge(w_in[h], 64 * m + 64)
                        for f in range(FT):
                            act.wait_ge(h_done, (m * 2 + h) * FT + f + 1)
                            nc.scalar.activation(hid[f % 2][:, :], ps_h[f % 2][:, :], ACT.Relu, bias=b1[h][:, f:f + 1]).then_inc(hid_done, 1)

            @block.tensor
            def _(pe):
                def columns(e, m, h):
                    pe.wait_ge(buf_in[h], 16 * m + 16)
                    for k in range(KD):
                        for s in range(CS):
                            last = nc.tensor.transpose(ps_t[k][:, s * P:(s + 1) * P], buf[h][:, s, k * P:(k + 1) * P], keep["ident"][:, :])
                    last.then_inc(tr_done, 1)

                def up(e, m, h, f):
                    if f == 0:
                        pe.wait_ge(bT_done, e + 1)
                        pe.wait_ge(w_in[h], 64 * m + 64)
                    for k in range(KD):
                        last = nc.tensor.matmul(ps_h[f % 2][:, :], w1[h][:, k, f * P:(f + 1) * P], bT[h][:, k, :], start=(k == 0), stop=(k == KD - 1))
                    last.then_inc(h_done, 1)

                def down(e, h, f):
                    if f == 0:
                        if isinstance(e, int):
                            pe.wait_ge(y_out, max(e - 1, 0))
                        else:
                            pe.wait_ge(y_out, e - 1 if h else e)
                    pe.wait_ge(hid_done, e * FT + f + 1)
                    for s in range(CS):
                        last = nc.tensor.matmul(ps_y[h][s // 2][:, s % 2, :], hid[f % 2][:, s * P:(s + 1) * P], w2[h][:, f, :],
                                                start=(f == 0 and s % 2 == 0), stop=(f == FT - 1 and s % 2 == 1), skip_group_check=True)
                    if f == FT - 1:
                        last.then_inc(y_done, 1)

                def expert(e, m, h, more):
                    for f in range(FT):
                        if f + 1 < FT:
                            up(e, m, h, f + 1)
                        elif more:
                            up(e + 1, m + h, 1 - h, 0)
                        if f == 3 and more:
                            columns(e + 1, m + h, 1 - h)
                        down(e, h, f)

                columns(0, 0, 0)
                up(0, 0, 0, 0)
                with pe.Fori(0, PAIRS - 1) as m:
                    for h in range(2):
                        expert(m * 2 + h, m, h, True)
                expert(E1 - 2, PAIRS - 1, 0, True)
                expert(E1 - 1, PAIRS - 1, 1, False)


def combine_phase(nc, x, d, keep):
    ctx = ExitStack()
    with ctx:
        sb = lambda name, shape, dt=F32: ctx.enter_context(nc.sbuf_tensor("co_" + name, shape, dt))
        DEEP = 4
        gvec, g_cur = sb("gvec", [P, B, D]), sb("g_cur", [P, D])
        slots = sb("slots", [P, DEEP * SUB], U32)
        xin = [sb(f"xin{h}", [P, SUB, D]) for h in range(DEEP)]
        yin = [sb(f"yin{h}", [P, SUB, D]) for h in range(DEEP)]
        res = [sb(f"res{h}", [P, SUB, D]) for h in range(DEEP)]
        sem = phase_semaphores(nc, ctx, "co_")
        const_in, always, res_done = sem("const_in"), sem("always"), sem("res_done")
        x_in = [sem(f"x_in{h}") for h in range(DEEP)]
        y_in = [sem(f"y_in{h}") for h in range(DEEP)]
        stored = [sem(f"stored{h}") for h in range(DEEP)]

        with nc.Block() as block:
            @block.sync
            def _(sp):
                def load(n, h):
                    sp.dma_start(xin[h][:, :, :], d["x3"][ds(n * T, T), :].rearrange("(s p) f -> p s f", p=P)).then_inc(x_in[h], 16)

                def store(n, h):
                    wait_alone(sp, res_done, n + 1, always)
                    sp.dma_start(x["out"][ds(n * T, T), :].rearrange("(s p) f -> p s f", p=P), res[h][:, :, :]).then_inc(stored[h], 16)

                for b in range(B):
                    sp.dma_start(gvec[:, b, :], d["rows"][R_GB1, b, :].partition_broadcast(P)).then_inc(const_in, 16)
                for n in range(DEEP):
                    load(n, n)
                with sp.Fori(0, NCH // DEEP - 1) as m:
                    for h in range(DEEP):
                        store(m * DEEP + h, h)
                        load(m * DEEP + h + DEEP, h)
                for h in range(DEEP):
                    store(NCH - DEEP + h, h)
                for h in range(DEEP):
                    sp.wait_ge(stored[h], 16 * (NCH // DEEP))

            @block.gpsimd
            def _(pool):
                pool.sem_inc(always, 1)
                with pool.Fori(0, NCH // DEEP) as m:
                    wait_alone(pool, res_done, m * DEEP, always)
                    nc.gpsimd.tensor_copy(slots[:, :], keep["slot"][:, ds(m * DEEP * SUB, DEEP * SUB)])
                    pool.drain()
                    for h in range(DEEP):
                        for s in range(SUB):
                            nc.gpsimd.indirect_dma_start(yin[h][:, s, :], None, d["y"],
                                                         bass.IndirectOffsetOnAxis(ap=slots[:, h * SUB + s:h * SUB + s + 1], axis=0)).then_inc(y_in[h], 16)

            @block.vector
            def _(dve):
                dve.wait_ge(const_in, 16 * B)
                with dve.Fori(0, B) as b:
                    dve.drain()
                    nc.vector.tensor_copy(g_cur[:, :], gvec[:, ds(b, 1), :].rearrange("p b f -> p (b f)"))
                    dve.drain()
                    for c in range(CPB):
                        i = b * CPB + c
                        dve.wait_ge(y_in[c], 16 * SUB * (b + 1))
                        dve.wait_ge(stored[c], 16 * b)
                        for s in range(SUB):
                            nc.vector.scalar_tensor_tensor(res[c][:, s, :], yin[c][:, s, :], keep["gate"][:, ds(i * SUB + s, 1)], g_cur[:, :], ALU.mult, ALU.mult)
                        dve.drain()
                        dve.wait_ge(x_in[c], 16 * (b + 1))
                        nc.vector.tensor_tensor(res[c][:, :, :], res[c][:, :, :], xin[c][:, :, :], ALU.add).then_inc(res_done, 1)


STAGES = [setup_phase, project_phase, attend_phase, mix_phase, scan_phase, clear_phase, route_phase, expert_phase, combine_phase]


def scratch(nc, kind="Internal"):
    shapes = {
        "rows": ([NROWS, B, D], F32),
        "parts": ([G, 3, P, N], BF16),
        "o": ([UNITS * (S // T) + 1, P, SUB, HPG * HD], F32),
        "x2": ([N, D], F32),
        "x3": ([N, D], F32),
        "buf": ([N, D], F32),
        "y": ([N, D], F32),
        "v": ([UNITS, P, KT, HPG * 32], F32),
    }
    return {n: nc.dram_tensor("t_" + n, s, t, kind=kind).ap() for n, (s, t) in shapes.items()}


def program(nc, x, d, stages):
    ctx = ExitStack()
    with ctx:
        sb = lambda name, shape, dt=F32: ctx.enter_context(nc.sbuf_tensor(name, shape, dt))
        keep = {
            "ident": sb("ident", [P, P]),
            "qscale": sb("qscale", [P, 1]),
            "bqk": sb("bqk", [P, G]),
            "bvT": sb("bvT", [P, KD]),
            "wqk": sb("wqk", [P, KD, G, P]),
            "wv": sb("wv", [P, KD, D]),
            "wo": sb("wo", [P, KD, D]),
            "gate": sb("gate", [P, N // P]),
            "slot": sb("slot", [P, N // P], U32),
            "mfm": sb("mfm", [P, 4 * KD, B + 1]),
        }
        for stage in stages:
            stage(nc, x, d, keep)


def host_layout(i):
    a = {n: np.asarray(v) for n, v in i.items()}
    o = {"x": a["L0_attn_x"].reshape(N, D)}
    for w in "qkvo":
        o["W" + w + "T"] = a[f"L0_attn_W{w}"].T
        o["A" + w] = a[f"L0_attn_A{w}"]
        o["B" + w + "T"] = a[f"L0_attn_B{w}"].T
    o["bqk"] = np.concatenate([a["L0_attn_bq"].reshape(G, 64).T, a["L0_attn_bk"].reshape(G, 64).T])
    o["bvT"], o["bo"], o["rezero"] = a["L0_attn_bv"].reshape(KD, P).T, a["L0_attn_bo"], a["L0_attn_rezero"]
    for l in range(2):
        o[f"c{l}T"], o[f"wmod{l}"] = a[f"L{l}_c"].T, a[f"L{l}_wmod"]
    o["rw"], o["rb"] = a["L0_ffn_router_w"], a["L0_ffn_router_b"]
    o["w1"], o["b1T"], o["w2"], o["b2"] = a["L0_ffn_W1"], a["L0_ffn_b1"].T, a["L0_ffn_W2"], a["L0_ffn_b2"]
    o["inw"], o["outw"] = a["L1_attn_in_proj_w"], a["L1_attn_out_proj_w"]
    o["conv_w"] = a["L1_attn_conv_w"].reshape(CTL, P, TAPS).transpose(1, 0, 2)
    o["conv_b"] = a["L1_attn_conv_b"].reshape(CTL, P).T
    o["dt_bias"], o["A_log"], o["Dskip"] = a["L1_attn_dt_bias"], a["L1_attn_A_log"], a["L1_attn_D"]
    o["xnw"], o["xnb"] = a["L1_attn_x_norm_w"].reshape(KD, P).T, a["L1_attn_x_norm_b"].reshape(KD, P).T
    o["rmsw"] = a["L1_attn_rms_w"].reshape(DI // P, P).T
    o["wg"], o["bg"] = a["L1_ffn_Wg"], a["L1_ffn_bg"]
    o["fw1"], o["fw2"], o["fb2"] = a["L1_ffn_W1"], a["L1_ffn_W2"], a["L1_ffn_b2"]
    o["fb1"] = a["L1_ffn_b1"].reshape(E1, F1 // P, P).transpose(0, 2, 1)
    o["upper"] = np.triu(np.ones((P, P), np.float32))
    o["lower"] = np.tril(np.ones((P, P), np.float32), -1)
    o["ones_f"] = np.ones((P, P), np.float32)
    o["mhalf"] = np.full((P, 16), -0.5, np.float32)
    o["iota"] = np.tile(np.arange(E1, dtype=np.float32), (P, 1))
    o["qscale"] = np.where(np.arange(P) < 64, np.float32(HD ** -0.5), np.float32(1)).astype(np.float32)[:, None]
    bias = (0.5 ** np.arange(H, dtype=np.float32))[:, None] * (np.arange(S, dtype=np.float32) - (S - 1))
    upper = bias.view(np.uint32) & 0xFFFF0000
    lower = (bias - upper.view(np.float32)).view(np.uint32)
    o["alibi"] = (np.stack([upper, lower]) >> 16).astype(np.uint16)
    o["ones"] = np.full((2, HPG, S), 0x3F80, np.uint16)
    o["ident"] = np.eye(P, dtype=np.float32)
    return {n: np.ascontiguousarray(v) for n, v in o.items()}


def kernel(**inputs):
    import concourse.bacc as bacc
    from concourse.bass_utils import run_bass_kernel_spmd

    arrays = {"in_" + n: v for n, v in host_layout(inputs).items()}
    nc = bacc.Bacc("TRN2", target_bir_lowering=False, num_devices=1)
    x = {n[3:]: nc.dram_tensor(n, a.shape, mybir.dt.from_np(a.dtype), kind="ExternalInput").ap() for n, a in arrays.items()}
    x["out"] = nc.dram_tensor("out", [N, D], F32, kind="ExternalOutput").ap()
    program(nc, x, scratch(nc), STAGES)
    r = run_bass_kernel_spmd(nc, [arrays], core_ids=[0])
    return r.results[0]["out"].reshape(B, S, D)
```

```python
from contextlib import ExitStack

import numpy as np

import concourse.bass as bass
from concourse import mybir

F32 = mybir.dt.float32
BF16 = mybir.dt.bfloat16
U32 = mybir.dt.uint32
I32 = mybir.dt.int32
ALU = mybir.AluOpType
ACT = mybir.ActivationFunctionType
AX = mybir.AxisListType
F32R = mybir.dt.float32r
ds = bass.ds

P = 128
B, S, D = 4, 2048, 256
N = B * S
KD = D // P
T = 512
SUB = T // P
CPB = S // T
NCH = N // T
EPS = 1e-5

H, HD = 16, 16
HPG = 4
G = H // HPG
UNITS = B * G
KT = S // P
LORA = 8
BANDS = [(0, 0), (0, 1), (1, 0), (1, 1), (0, 2), (2, 0)]
SROWS = 16 * len(BANDS)
ALI = SROWS
MXR = SROWS + 2
QROWS = SROWS + 4

E0, F0 = 8, 128
NH, HP, NS = 4, 128, 64
DI = NH * HP
CONV = DI + 2 * NS
CTL = CONV // P
TAPS = 4
E1, F1 = 16, 1024
CAP = N // E1
ROW = 3 * D + 1

R_GCA, R_GSA, R_GRZ, R_GB0, R_CA1, R_SA1, R_GA1, R_CB1, R_SB1, R_GB1 = range(10)
NROWS = 10


CUTS = [(0, 0), (0, 1), (1, 0)]


def upper_part(eng, out, src):
    return eng.tensor_copy(out, src)


def lower_part(eng, out, src, upper):
    return eng.tensor_tensor(out, src, upper.bitcast(F32), ALU.subtract)


def wait_alone(eng, sem, value, always):
    eng.wait_ge(always, 1)
    eng.wait_ge(sem, value)


def phase_semaphores(nc, ctx, prefix):
    mine = []

    def sem(name):
        mine.append(nc.alloc_semaphore(prefix + name))
        return mine[-1]

    def give_back():
        nc.clear_and_free_semaphores(mine)
        nc.all_engine_barrier()

    ctx.callback(give_back)
    return sem


def setup_phase(nc, x, d, keep):
    ctx = ExitStack()
    with ctx:
        sb = lambda name, shape, dt=F32: ctx.enter_context(nc.sbuf_tensor("su_" + name, shape, dt))
        cT = sb("cT", [P, KD, 2, B])
        silu_c = sb("silu_c", [P, KD, 2, B])
        wmod = sb("wmod", [P, 2, KD, 6 * D])
        lora_a = sb("lora_a", [LORA, 4, D])
        lora_b = sb("lora_b", [LORA, 4, D])
        wT = sb("wT", [P, 4, KD, D])
        modr = sb("modr", [B, 2, 6, D])
        rows = sb("rows", [B, NROWS, D])
        sgn = sb("sgn", [B, 4, D])
        mag = sb("mag", [B, 4, D])
        bo = sb("bo", [B, D])
        rz = sb("rz", [B, 1])
        bqk = sb("bqk", [P, G])
        ps = [ctx.enter_context(nc.psum_tensor(f"su_ps{i}", [P, 512], F32)) for i in range(8)]
        sem = phase_semaphores(nc, ctx, "su_")
        loaded, c_loaded = sem("loaded"), sem("c_loaded")
        silu_done, lora_done, mod0_done, mod1_done = sem("silu_done"), sem("lora_done"), sem("mod0_done"), sem("mod1_done")
        lora_read, rows_done, stored = sem("lora_read"), sem("rows_done"), sem("stored")
        nload = 0

        with nc.Block() as block:
            @block.sync
            def _(sp):
                sp.dma_start(cT[:, :, 0, :], x["c0T"].rearrange("(k p) b -> p k b", p=P)).then_inc(c_loaded, 16)
                sp.dma_start(cT[:, :, 1, :], x["c1T"].rearrange("(k p) b -> p k b", p=P)).then_inc(c_loaded, 16)
                for n, w in enumerate("qkvo"):
                    sp.dma_start(lora_a[:, n, :], x["A" + w]).then_inc(loaded, 16)
                    sp.dma_start(lora_b[:, n, :], x["B" + w + "T"]).then_inc(loaded, 16)
                    sp.dma_start(wT[:, n, :, :], x["W" + w + "T"].rearrange("(k p) n -> p k n", p=P)).then_inc(loaded, 16)
                for l in range(2):
                    sp.dma_start(wmod[:, l, :, :], x[f"wmod{l}"].rearrange("(k p) n -> p k n", p=P)).then_inc(loaded, 16)
                sp.dma_start(bo[:, :], x["bo"].partition_broadcast(B)).then_inc(loaded, 16)
                sp.dma_start(rz[:, :], x["rezero"].partition_broadcast(B)).then_inc(loaded, 16)
                sp.dma_start(bqk[:, :], x["bqk"]).then_inc(loaded, 16)
                sp.dma_start(keep["qscale"][:, :], x["qscale"]).then_inc(loaded, 16)
                sp.dma_start(keep["ident"][:, :], x["ident"]).then_inc(loaded, 16)
                sp.dma_start(keep["bvT"][:, :], x["bvT"]).then_inc(loaded, 16)
                sp.wait_ge(rows_done, 1)
                sp.dma_start(d["rows"].rearrange("r b f -> b r f"), rows[:, :, :]).then_inc(stored, 16)
                sp.wait_ge(stored, 16)

            NLOAD = 16 * (4 * 3 + 2 + 6)

            @block.scalar
            def _(act):
                act.wait_ge(c_loaded, 32)
                nc.scalar.activation(silu_c[:, :, :, :], cT[:, :, :, :], ACT.Silu).then_inc(silu_done, 1)

            @block.tensor
            def _(pe):
                pe.wait_ge(loaded, NLOAD)
                for n in range(4):
                    for k in range(KD):
                        last = nc.tensor.matmul(ps[n][:, k * D:(k + 1) * D], lora_a[:, n, k * P:(k + 1) * P],
                                                lora_b[:, n, :], start=True, stop=True)
                last.then_inc(lora_done, 1)
                pe.wait_ge(silu_done, 1)
                for j in range(3):
                    for k in range(KD):
                        nc.tensor.matmul(ps[4 + j][0:B, :], silu_c[:, k, 0, :], wmod[:, 0, k, j * 512:(j + 1) * 512],
                                         start=(k == 0), stop=(k == KD - 1))
                for w, part in enumerate((1, 0, 4, 3)):
                    for k2 in range(KD):
                        for k in range(KD):
                            col = part * D + k2 * P
                            last = nc.tensor.matmul(ps[7][:, (w * KD + k2) * B:(w * KD + k2 + 1) * B],
                                                    wmod[:, 0, k, col:col + P], silu_c[:, k, 0, :],
                                                    start=(k == 0), stop=(k == KD - 1))
                last.then_inc(mod0_done, 1)
                pe.wait_ge(lora_read, 1)
                for j in range(3):
                    for k in range(KD):
                        last = nc.tensor.matmul(ps[j][0:B, :], silu_c[:, k, 1, :], wmod[:, 1, k, j * 512:(j + 1) * 512],
                                                start=(k == 0), stop=(k == KD - 1))
                last.then_inc(mod1_done, 1)

            @block.vector
            def _(dve):
                dve.wait_ge(loaded, NLOAD)
                nc.vector.tensor_scalar(keep["bqk"][:, :], bqk[:, :], keep["qscale"][:, 0:1], None, ALU.mult)
                dve.wait_ge(lora_done, 1)
                for n in range(4):
                    for k in range(KD):
                        low = ps[n][:, k * D:(k + 1) * D]
                        if n < 2:
                            out = keep["wqk"][:, k, :, n * 64:(n + 1) * 64]
                            low, full = low.rearrange("p (g c) -> p g c", g=G), wT[:, n, k, :].rearrange("p (g c) -> p g c", g=G)
                        else:
                            out, full = keep["wv" if n == 2 else "wo"][:, k, :], wT[:, n, k, :]
                        last = nc.vector.scalar_tensor_tensor(out, low, 1.0 / LORA, full, ALU.mult, ALU.add)
                last.then_inc(lora_read, 1)
                dve.wait_ge(mod0_done, 1)
                for j in range(3):
                    nc.vector.tensor_copy(modr[:, 0, :, :].rearrange("b m f -> b (m f)")[:, j * 512:(j + 1) * 512], ps[4 + j][0:B, :])
                for w, add in enumerate((1.0, 0.0, 1.0, 0.0)):
                    src = ps[7][:, w * KD * B:(w + 1) * KD * B].rearrange("p (k b) -> p k b", b=B)
                    nc.vector.tensor_scalar(keep["mfm"][:, w * KD:(w + 1) * KD, 0:B], src, add, None, ALU.add)
                    nc.vector.tensor_scalar(keep["mfm"][:, w * KD:(w + 1) * KD, B:B + 1], src[:, :, B - 1:B], add, None, ALU.add)
                dve.wait_ge(mod1_done, 1)
                for j in range(3):
                    nc.vector.tensor_copy(modr[:, 1, :, :].rearrange("b m f -> b (m f)")[:, j * 512:(j + 1) * 512], ps[j][0:B, :])
                dve.drain()
                for l in range(2):
                    for n, m in enumerate((2, 5)):
                        nc.vector.tensor_scalar(sgn[:, 2 * l + n, :], modr[:, l, m, :], 0.0, 2.0, ALU.is_ge, ALU.mult)
                        nc.vector.tensor_scalar(mag[:, 2 * l + n, :], modr[:, l, m, :], -1.0, None, ALU.mult)
                dve.drain()
                for l in range(2):
                    for n, m in enumerate((2, 5)):
                        nc.vector.tensor_tensor(mag[:, 2 * l + n, :], mag[:, 2 * l + n, :], modr[:, l, m, :], ALU.max)
                dve.drain()
                nc.vector.tensor_scalar(mag[:, :, :], mag[:, :, :], 0.25, None, ALU.max)
                dve.drain()
                GA0, GB0, GA1, GB1 = range(4)
                for n in range(4):
                    nc.vector.scalar_tensor_tensor(sgn[:, n, :], sgn[:, n, :], -1.0, mag[:, n, :], ALU.add, ALU.mult)
                dve.drain()
                for r, n in ((R_GB0, GB0), (R_GA1, GA1), (R_GB1, GB1)):
                    nc.vector.tensor_copy(rows[:, r, :], sgn[:, n, :])
                for r, m, add in ((R_CA1, 1, 1.0), (R_SA1, 0, 0.0), (R_CB1, 4, 1.0), (R_SB1, 3, 0.0)):
                    nc.vector.tensor_scalar(rows[:, r, :], modr[:, 1, m, :], add, None, ALU.add)
                nc.vector.scalar_tensor_tensor(rows[:, R_GCA, :], modr[:, 0, 1, :], 1.0, sgn[:, GA0, :], ALU.add, ALU.mult)
                nc.vector.tensor_scalar(rows[:, R_GRZ, :], sgn[:, GA0, :], rz[:, 0:1], None, ALU.mult)
                nc.vector.tensor_tensor(rows[:, R_GSA, :], modr[:, 0, 0, :], sgn[:, GA0, :], ALU.mult)
                dve.drain()
                nc.vector.tensor_tensor(mag[:, 0, :], rows[:, R_GRZ, :], bo[:, :], ALU.mult)
                dve.drain()
                nc.vector.tensor_tensor(rows[:, R_GSA, :], rows[:, R_GSA, :], mag[:, 0, :], ALU.add).then_inc(rows_done, 1)


def project_phase(nc, x, d, keep):
    ctx = ExitStack()
    with ctx:
        sb = lambda name, shape, dt=F32: ctx.enter_context(nc.sbuf_tensor("pr_" + name, shape, dt))
        xin = [sb(f"xin{h}", [P, SUB, D]) for h in range(2)]
        xh = [sb(f"xh{h}", [P, SUB, D]) for h in range(2)]
        hT = [sb(f"hT{h}", [P, KD, T]) for h in range(2)]
        hTc = [[sb(f"hTc{h}{c}", [P, KD, T], F32R) for c in range(2)] for h in range(2)]
        wqkc = [sb(f"wqkc{c}", [P, KD, G, P], F32R) for c in range(2)]
        wvc = [sb(f"wvc{c}", [P, KD, D], F32R) for c in range(2)]
        mcur = sb("mcur", [P, 2 * KD])
        st, mv = sb("st", [P, SUB, 6]), sb("mv", [P, SUB, 2])
        ve, rstd, mhalf = sb("ve", [P, SUB]), sb("rstd", [P, SUB]), sb("mhalf", [P, SUB])
        qk = [sb(f"qk{g}", [P, T]) for g in range(G)]
        rest = [sb(f"rest{g}", [P, T]) for g in range(G)]
        parts = [sb(f"parts{g}", [P, 3, T], BF16) for g in range(G)]
        vaug = [sb(f"vaug{h}", [P, SUB, H, 32]) for h in range(2)]
        ps_t = [ctx.enter_context(nc.psum_tensor(f"pr_pst{k}", [P, T], F32)) for k in range(KD)]
        ps_qk = [ctx.enter_context(nc.psum_tensor(f"pr_psqk{k}", [P, T], F32)) for k in range(4)]
        ps_v = [ctx.enter_context(nc.psum_tensor(f"pr_psv{k}", [P, 2, D], F32)) for k in range(2)]
        sem = phase_semaphores(nc, ctx, "pr_")
        x_in = [sem(f"x_in{h}") for h in range(2)]
        var_done, rstd_done, xh_done = sem("var_done"), sem("rstd_done"), sem("xh_done")
        tr_done, hT_done, qk_done, qk_out = sem("tr_done"), sem("hT_done"), sem("qk_done"), sem("qk_out")
        w_cut, upper_done, hT_cut = sem("w_cut"), sem("upper_done"), sem("hT_cut")
        rest_done, p2_done, p3_done = sem("rest_done"), sem("p2_done"), sem("p3_done")
        v_done, v_out, always, const_done = sem("v_done"), sem("v_out"), sem("always"), sem("const_done")
        parts_stored = [sem(f"parts_stored{g}") for g in range(G)]
        v_stored = [sem(f"v_stored{h}") for h in range(2)]

        with nc.Block() as block:
            @block.sync
            def _(sp):
                with sp.Fori(0, B) as b:
                    for c in range(CPB):
                        i = b * CPB + c
                        for g in range(G):
                            sp.wait_ge(p3_done, i * G + g + 1)
                            sp.wait_ge(p2_done, i * G + g + 1)
                            sp.dma_start(d["parts"][g, :, :, ds(i * T, T)].rearrange("c p t -> p c t"), parts[g][:, :, :]).then_inc(parts_stored[g], 16)
                        sp.wait_ge(v_out, 2 * i + 2)
                        for g in range(G):
                            sp.dma_start(d["v"][ds(b * G + g, 1), :, c * SUB:(c + 1) * SUB, :].rearrange("u p s c -> p (u s) c"),
                                         vaug[c % 2][:, :, g * HPG:(g + 1) * HPG, :].rearrange("p s h c -> p s (h c)")).then_inc(v_stored[c % 2], 16)
                for g in range(G):
                    sp.wait_ge(parts_stored[g], 16 * NCH)
                for h in range(2):
                    sp.wait_ge(v_stored[h], 16 * G * NCH // 2)

            @block.gpsimd
            def _(pool):
                nc.gpsimd.memset(mhalf[:, :], -0.5)
                for h in range(2):
                    last = nc.gpsimd.memset(vaug[h][:, :, :, HD:32], 1.0)
                last.then_inc(const_done, 1)
                pool.sem_inc(always, 1)
                pool.drain()

                def load(chunk, h):
                    nc.gpsimd.dma_start(xin[h][:, :, :], x["x"][ds(chunk * T, T), :].rearrange("(s p) f -> p s f", p=P)).then_inc(x_in[h], 16)

                def rsqrt(n):
                    pool.wait_ge(var_done, n + 1)
                    nc.gpsimd.tensor_tensor(rstd[:, :], ve[:, :], mhalf[:, :], ALU.pow).then_inc(rstd_done, 1)

                def lower_rows(n, h):
                    pool.wait_ge(upper_done, n + 1)
                    lower_part(nc.gpsimd, hTc[h][1][:, :, :], hT[h][:, :, :], hTc[h][0][:, :, :]).then_inc(hT_cut, 1)

                for n in range(2):
                    load(n, n)
                for n in range(2):
                    rsqrt(n)
                    wait_alone(pool, xh_done, n + 1, always)
                    load(n + 2, n)
                lower_rows(0, 0)
                with pool.Fori(0, B) as b:
                    for c in range(CPB):
                        i = b * CPB + c
                        rsqrt(i + 2)
                        lower_rows(i + 1, (c + 1) % 2)
                        wait_alone(pool, xh_done, i + 3, always)
                        load((i + 4) % NCH, c % 2)
                        for g in range(G):
                            pool.wait_ge(p2_done, i * G + g + 1)
                            nc.gpsimd.tensor_tensor(parts[g][:, 2, :], rest[g][:, :], parts[g][:, 1, :], ALU.subtract).then_inc(p3_done, 1)
                for h in range(2):
                    pool.wait_ge(x_in[h], 16 * (NCH // 2 + 2))

            @block.vector
            def _(dve):
                def variance(n, m, h):
                    dve.wait_ge(x_in[h], 16 * m + 16)
                    for s in range(SUB):
                        nc.vector.bn_stats(st[:, s, :], xin[h][:, s, :])
                    dve.drain()
                    for s in range(SUB):
                        nc.vector.bn_aggr(mv[:, s, :], st[:, s, :])
                    dve.drain()
                    nc.vector.tensor_scalar(ve[:, :], mv[:, :, 1], EPS, None, ALU.add).then_inc(var_done, 1)

                def normalise(n, h):
                    dve.wait_ge(rstd_done, n + 1)
                    if not isinstance(n, int):
                        dve.wait_ge(tr_done, n - 1)
                    for s in range(SUB):
                        last = nc.vector.tensor_scalar(xh[h][:, s, :], xin[h][:, s, :], mv[:, s, 0:1], rstd[:, s:s + 1], ALU.subtract, ALU.mult)
                    last.then_inc(xh_done, 1)

                def upper_rows(n, h):
                    dve.wait_ge(hT_done, n + 1)
                    upper_part(nc.vector, hTc[h][0][:, :, :], hT[h][:, :, :]).then_inc(upper_done, 1)

                def v_columns(i, m, h, half):
                    dve.wait_ge(v_done, 2 * i + half + 1)
                    if half == 0:
                        dve.wait_ge(v_stored[h], m * G * 16)
                    nc.vector.tensor_copy(vaug[h][:, 2 * half:2 * half + 2, :, 0:HD],
                                          ps_v[half][:, :, :].rearrange("p s (h e) -> p s h e", e=HD)).then_inc(v_out, 1)

                def second_part(i, g):
                    dve.wait_ge(qk_out, i * G + g + 1)
                    dve.wait_ge(p3_done, i * G)
                    nc.vector.tensor_tensor(rest[g][:, :], qk[g][:, :], parts[g][:, 0, :], ALU.subtract).then_inc(rest_done, 1)
                    dve.drain()
                    nc.vector.tensor_copy(parts[g][:, 1, :], rest[g][:, :]).then_inc(p2_done, 1)

                variance(0, 0, 0)
                normalise(0, 0)
                for cut, w in ((wqkc, keep["wqk"][:, :, :, :].rearrange("p k g n -> p k (g n)")), (wvc, keep["wv"][:, :, :])):
                    flat = [t[:, :, :, :].rearrange("p k g n -> p k (g n)") if cut is wqkc else t[:, :, :] for t in cut]
                    upper_part(nc.vector, flat[0], w)
                    dve.drain()
                    lower_part(nc.vector, flat[1], w, flat[0]).then_inc(w_cut, 1)
                upper_rows(0, 0)
                variance(1, 0, 1)
                normalise(1, 1)
                dve.wait_ge(const_done, 1)
                with dve.Fori(0, B) as b:
                    for c in range(CPB):
                        i = b * CPB + c
                        variance(i + 2, b * 2 + (c + 2) // 2, c % 2)
                        upper_rows(i + 1, (c + 1) % 2)
                        second_part(i, 0)
                        normalise(i + 2, c % 2)
                        second_part(i, 1)
                        for half in range(2):
                            v_columns(i, b * 2 + c // 2, c % 2, half)
                        second_part(i, 2)
                        second_part(i, 3)

            @block.scalar
            def _(act):
                def modulate(n, h):
                    act.wait_ge(tr_done, n + 1)
                    for k in range(KD):
                        last = nc.scalar.activation(hT[h][:, k, :], ps_t[k][:, :], ACT.Identity,
                                                    scale=mcur[:, k:k + 1], bias=mcur[:, KD + k:KD + k + 1])
                    last.then_inc(hT_done, 1)

                def batch_vectors(b):
                    act.drain()
                    nc.scalar.copy(mcur[:, :], keep["mfm"][:, 0:2 * KD, ds(b, 1)].rearrange("p m b -> p (m b)"))
                    act.drain()

                batch_vectors(0)
                modulate(0, 0)
                with act.Fori(0, B) as b:
                    for c in range(CPB):
                        i = b * CPB + c
                        for g in range(G):
                            act.wait_ge(qk_done, i * G + g + 1)
                            act.wait_ge(rest_done, i * G)
                            act.wait_ge(parts_stored[g], 16 * i)
                            nc.scalar.activation(qk[g][:, :], ps_qk[g][:, :], ACT.Identity, scale=keep["qscale"][:, 0:1], bias=keep["bqk"][:, g:g + 1])
                            nc.scalar.activation(parts[g][:, 0, :], ps_qk[g][:, :], ACT.Identity, scale=keep["qscale"][:, 0:1],
                                                 bias=keep["bqk"][:, g:g + 1]).then_inc(qk_out, 1)
                            if g == 0:
                                if c == CPB - 1:
                                    batch_vectors(b + 1)
                                modulate(i + 1, (c + 1) % 2)

            @block.tensor
            def _(pe):
                def transposes(n, h):
                    pe.wait_ge(xh_done, n + 1)
                    pe.wait_ge(hT_done, n)
                    for k in range(KD):
                        for s in range(SUB):
                            last = nc.tensor.transpose(ps_t[k][:, s * P:(s + 1) * P], xh[h][:, s, k * P:(k + 1) * P], keep["ident"][:, :])
                    last.then_inc(tr_done, 1)

                def qk_products(i, c, g):
                    if g == 0:
                        pe.wait_ge(hT_cut, i + 1)
                    pe.wait_ge(qk_out, i * G)
                    for k in range(KD):
                        for n, (a, r) in enumerate(CUTS):
                            last = nc.tensor.matmul(ps_qk[g][:, :], wqkc[a][:, k, g, :], hTc[c % 2][r][:, k, :],
                                                    start=(k == 0 and n == 0), stop=(k == KD - 1 and n == 2))
                    last.then_inc(qk_done, 1)

                def v_products(i, c, half):
                    pe.wait_ge(v_out, 2 * i)
                    for s in range(2):
                        for k in range(KD):
                            for n, (a, r) in enumerate(CUTS):
                                last = nc.tensor.matmul(ps_v[half][:, s, :], hTc[c % 2][a][:, k, (2 * half + s) * P:(2 * half + s + 1) * P],
                                                        wvc[r][:, k, :], start=(k == 0 and n == 0), stop=(k == KD - 1 and n == 2))
                    last.then_inc(v_done, 1)

                transposes(0, 0)
                pe.wait_ge(w_cut, 2)
                with pe.Fori(0, B) as b:
                    for c in range(CPB):
                        i = b * CPB + c
                        qk_products(i, c, 0)
                        transposes(i + 1, (c + 1) % 2)
                        qk_products(i, c, 1)
                        v_products(i, c, 0)
                        v_products(i, c, 1)
                        qk_products(i, c, 2)
                        qk_products(i, c, 3)


def attend_phase(nc, x, d, keep):
    ctx = ExitStack()
    with ctx:
        sb = lambda name, shape, dt=F32: ctx.enter_context(nc.sbuf_tensor("at_" + name, shape, dt))
        qs = [sb(f"qs{s}", [QROWS, HPG, S], BF16) for s in range(2)]
        ks = [sb(f"ks{s}", [QROWS, HPG, S], BF16) for s in range(2)]
        vs = [sb(f"vs{s}", [P, KT, HPG * 32]) for s in range(2)]
        prob = [[sb(f"prob{r}{a}", [P, 2, T]) for a in range(2)] for r in range(2)]
        mxp = sb("mxp", [P, SUB * HPG, S // T])
        nmax = sb("nmax", [P, SUB * HPG])
        nparts = sb("nparts", [P, SUB, HPG, 2], BF16)
        nrows = sb("nrows", [2 * HPG, T], BF16)
        osum = sb("osum", [P, T])
        rec = sb("rec", [P, SUB, HPG])
        onorm = [sb(f"onorm{r}", [P, SUB, HPG * HD]) for r in range(2)]
        identb = sb("identb", [P, P], BF16)
        ps_s = [ctx.enter_context(nc.psum_tensor(f"at_ps_s{a}", [P, 2, T], F32)) for a in range(2)]
        ps_m = [ctx.enter_context(nc.psum_tensor(f"at_ps_m{a}", [P, T], F32)) for a in range(2)]
        ps_o = ctx.enter_context(nc.psum_tensor("at_ps_o", [P, T], F32))
        ps_x = ctx.enter_context(nc.psum_tensor("at_ps_x", [P, T], F32))
        x_bf = ps_x[:, :].bitcast(BF16)
        sem = phase_semaphores(nc, ctx, "at_")
        kq_in = [sem(f"kq_in{s}") for s in range(2)]
        s_done, p_done, o_done, o_out = sem("s_done"), sem("p_done"), sem("o_done"), sem("o_out")
        mx_done, mx_read, neg_done = sem("mx_done"), sem("mx_read"), sem("neg_done")
        xt_done, ot_done, x_read = sem("xt_done"), sem("ot_done"), sem("x_read")
        max_in, always = sem("max_in"), sem("always")
        o_stored = [sem(f"o_stored{r}") for r in range(2)]
        QC = S // T
        STEP = 2 * KT
        MXN = SUB * HPG * (S // T)
        NLD = 2 * len(BANDS) + 2

        CLR = 8
        blank = sb("blank", [P, CLR, ROW])
        cleared = sem("cleared")

        with nc.Block() as block:
            @block.gpsimd
            def _(pool):
                nc.gpsimd.memset(blank[:, :, :], 0.0)
                pool.drain()
                nc.gpsimd.memset(blank[:, :, 3 * D:ROW].bitcast(U32), 2 * N)
                pool.drain()
                for k in range(N // (P * CLR)):
                    nc.gpsimd.dma_start(d["buf"][k * P * CLR:(k + 1) * P * CLR, :].rearrange("(p r) f -> p r f", p=P), blank[:, :, :]).then_inc(cleared, 16)
                pool.wait_ge(cleared, 16 * (N // (P * CLR)))

            @block.sync
            def _(sp):
                def load(u, s):
                    b, g = u // G, u % G
                    for r, (qp, kp) in enumerate(BANDS):
                        for dst, part, row in ((qs, qp, 0), (ks, kp, HPG * HD)):
                            src = d["parts"][ds(g, 1), part, row:row + HPG * HD, ds(b * S, S)]
                            sp.dma_start(dst[s][r * HD:(r + 1) * HD, :, :], src.rearrange("g (j e) t -> e (g j) t", e=HD)).then_inc(kq_in[s], 16)
                    sp.dma_start(ks[s][ALI:ALI + 2, :, :], x["alibi"].bitcast(BF16)[:, ds(g * HPG, HPG), :]).then_inc(kq_in[s], 16)
                    sp.dma_start(vs[s][:, :, :], d["v"][ds(u, 1), :, :, :].rearrange("u p k c -> p (u k) c")).then_inc(kq_in[s], 16)

                for s in range(2):
                    sp.dma_start(qs[s][ALI:ALI + 2, :, :], x["ones"].bitcast(BF16)).then_inc(max_in, 16)
                    sp.dma_start(ks[s][MXR:MXR + 2, :, :], x["ones"].bitcast(BF16)).then_inc(max_in, 16)

                def store_max(s, c):
                    for j in range(HPG):
                        sp.dma_start(qs[s][MXR:MXR + 2, j, c * T:(c + 1) * T], nrows[2 * j:2 * j + 2, :]).then_inc(max_in, 16)

                load(0, 0)
                sp.wait_ge(x_read, 1)
                store_max(0, 0)
                with sp.Fori(0, UNITS // 2) as up:
                    for s in range(2):
                        u = up * 2 + s
                        wait_alone(sp, o_done, u * QC, always)
                        load((u + 1) % UNITS, 1 - s)
                        for c in range(QC):
                            n = u * QC + c
                            sp.wait_ge(x_read, 2 * n + 2)
                            store_max(s if c < QC - 1 else 1 - s, (c + 1) % QC)
                            wait_alone(sp, x_read, 2 * n + 3, always)
                            sp.dma_start(d["o"][ds(n, 1), :, :, :].rearrange("n p s c -> p (n s) c"), onorm[c % 2][:, :, :]).then_inc(o_stored[c % 2], 16)
                sp.wait_ge(x_read, 2 * UNITS * QC + 2)
                sp.dma_start(d["o"][UNITS * QC, :, :, :], onorm[0][:, :, :]).then_inc(o_stored[0], 16)
                sp.wait_ge(o_stored[0], 16 * (UNITS * QC // 2 + 1))
                sp.wait_ge(o_stored[1], 16 * (UNITS * QC // 2))
                sp.wait_ge(max_in, 64 + 64 * (UNITS * QC + 1))

            @block.scalar
            def _(act):
                def take_sums(n):
                    act.wait_ge(o_done, n)
                    act.wait_ge(ot_done, n)
                    nc.scalar.copy(osum[:, :], ps_o[:, :]).then_inc(o_out, 1)

                act.wait_ge(always, 1)
                with act.Fori(0, UNITS * QC) as n:
                    for t in range(KT):
                        for a in range(2):
                            act.wait_ge(s_done, n * STEP + 2 * t + a + 1)
                            nc.scalar.activation(prob[t % 2][a][:, :, :], ps_s[a][:, :, :], ACT.Exp).then_inc(p_done, 1)
                            if t == 0 and a == 0:
                                take_sums(n)
                take_sums(UNITS * QC)

            @block.vector
            def _(dve):
                def maxima(n, t):
                    for k in range(S // T):
                        dve.wait_ge(mx_done, n * MXN + t * (S // T) + k + 1)
                        nc.vector.tensor_reduce(mxp[:, t, k:k + 1], ps_m[k % 2][:, :], AX.X, ALU.max).then_inc(mx_read, 1)

                def negate():
                    dve.drain()
                    nc.vector.tensor_reduce(nmax[:, :], mxp[:, :, :], AX.X, ALU.max, negate=True)
                    dve.drain()
                    flat = nparts[:, :, :, :].rearrange("p s j c -> p (s j) c")
                    nc.vector.tensor_copy(flat[:, :, 0], nmax[:, :])
                    dve.drain()
                    nc.vector.tensor_tensor(flat[:, :, 1], nmax[:, :], flat[:, :, 0], ALU.subtract).then_inc(neg_done, 1)

                def take_rows(n):
                    dve.wait_ge(xt_done, n + 1)
                    dve.wait_ge(max_in, 64 + 64 * n)
                    nc.vector.tensor_copy(nrows[:, :], x_bf[0:2 * HPG, 0:T]).then_inc(x_read, 1)

                def normalise(n, r, m):
                    dve.wait_ge(ot_done, n + 1)
                    view = ps_x[:, :].rearrange("p (s j c) -> p s j c", s=SUB, j=HPG)
                    nc.vector.reciprocal(rec[:, :, :], view[:, :, :, HD])
                    dve.drain()
                    dve.wait_ge(o_stored[r], 16 * m)
                    nc.vector.tensor_tensor(onorm[r][:, :, :].rearrange("p s (j c) -> p s j c", j=HPG), view[:, :, :, 0:HD],
                                            rec[:, :, :].unsqueeze(3).to_broadcast([P, SUB, HPG, HD]), ALU.mult).then_inc(x_read, 1)

                nc.vector.memset(ps_o[:, :], 1.0)
                nc.vector.tensor_copy(identb[:, :], keep["ident"][:, :])
                dve.drain()
                dve.sem_inc(always, 1)
                for n in range(2):
                    for t in range(SUB * HPG):
                        maxima(n, t)
                    if n == 1:
                        dve.wait_ge(xt_done, 1)
                    negate()
                    if n == 0:
                        take_rows(0)
                with dve.Fori(0, UNITS * QC // 2) as m:
                    for r in range(2):
                        n = m * 2 + r
                        for t in range(SUB * HPG):
                            maxima(n + 2, t)
                            if t == 3:
                                take_rows(n + 1)
                            if t == 7:
                                normalise(n, r, m)
                        negate()
                normalise(UNITS * QC, 0, UNITS * QC // 2)

            @block.tensor
            def _(pe):
                def scores(s, c, t, a):
                    for j in range(2):
                        head = 2 * a + j
                        last = nc.tensor.matmul(ps_s[a][:, j, :], ks[s][0:QROWS, head, t * P:(t + 1) * P],
                                                qs[s][0:QROWS, head, c * T:(c + 1) * T], start=True, stop=True)
                    last.then_inc(s_done, 1)

                def max_scores(n, s, c, t, k):
                    if not (isinstance(n, int) and n * MXN + t * (S // T) + k < 2):
                        pe.wait_ge(mx_read, n * MXN + t * (S // T) + k - 1)
                    q0 = c * T + (t // HPG) * P
                    nc.tensor.matmul(ps_m[k % 2][:, :], qs[s][0:MXR, t % HPG, q0:q0 + P], ks[s][0:MXR, t % HPG, k * T:(k + 1) * T],
                                     start=True, stop=True).then_inc(mx_done, 1)

                def weighted(s, t, half):
                    cols = slice(half * (T // 2), (half + 1) * (T // 2))
                    for j in range(HPG):
                        last = nc.tensor.matmul(ps_o[32 * j:32 * j + 32, cols], vs[s][:, t, 32 * j:32 * j + 32], prob[t % 2][j // 2][:, j % 2, cols],
                                                start=(t == 0 and half == 0), stop=(t == KT - 1 and half == 1),
                                                tile_position=(0, 32 * j), skip_group_check=True)
                    return last

                def max_rows(n):
                    wait_alone(pe, neg_done, n + 1, always)
                    for s in range(SUB):
                        last = nc.tensor.transpose(x_bf[0:2 * HPG, s * P:(s + 1) * P], nparts[:, s, :, :].rearrange("p j c -> p (j c)"), identb[:, :])
                    last.then_inc(xt_done, 1)

                def sums_by_token(n):
                    pe.wait_ge(o_out, n + 1)
                    for s in range(SUB):
                        last = nc.tensor.transpose(ps_x[:, s * P:(s + 1) * P], osum[:, s * P:(s + 1) * P], keep["ident"][:, :])
                    last.then_inc(ot_done, 1)

                pe.wait_ge(max_in, 64)
                pe.wait_ge(kq_in[0], 16 * NLD)
                for t in range(SUB * HPG):
                    for k in range(S // T):
                        max_scores(0, 0, 0, t, k)
                max_rows(0)
                for t in range(SUB * HPG):
                    for k in range(S // T):
                        max_scores(1, 0, 1, t, k)
                pe.wait_ge(max_in, 128)
                for a in range(2):
                    scores(0, 0, 0, a)
                with pe.Fori(0, UNITS // 2) as up:
                    for s in range(2):
                        for c in range(QC):
                            n = (up * 2 + s) * QC + c
                            ms, mc = (s, c + 2) if c + 2 < QC else (1 - s, c + 2 - QC)
                            if c + 2 == QC:
                                pe.wait_ge(kq_in[1 - s], 16 * NLD * (up + 1 + s))
                            for t in range(KT):
                                nxt = (s, c, t + 1) if t + 1 < KT else ((s, c + 1, 0) if c + 1 < QC else (1 - s, 0, 0))
                                if t + 1 == KT:
                                    pe.wait_ge(max_in, 64 + 64 * (n + 2))
                                pe.wait_ge(p_done, n * STEP + 2 * t + 1)
                                scores(*nxt, 0)
                                max_scores(n + 2, ms, mc, t, 0)
                                if t == 0:
                                    pe.wait_ge(o_out, n + 1)
                                pe.wait_ge(p_done, n * STEP + 2 * t + 2)
                                weighted(s, t, 0)
                                max_scores(n + 2, ms, mc, t, 1)
                                scores(*nxt, 1)
                                max_scores(n + 2, ms, mc, t, 2)
                                last = weighted(s, t, 1)
                                if t + 1 == KT:
                                    last.then_inc(o_done, 1)
                                max_scores(n + 2, ms, mc, t, 3)
                                if t == 3:
                                    wait_alone(pe, x_read, 2 * n + 1, always)
                                    max_rows(n + 1)
                                if t == 7:
                                    pe.wait_ge(x_read, 2 * n + 2)
                                    sums_by_token(n)
                pe.wait_ge(x_read, 2 * UNITS * QC + 1)
                sums_by_token(UNITS * QC)


def mix_phase(nc, x, d, keep):
    ctx = ExitStack()
    with ctx:
        sb = lambda name, shape, dt=F32: ctx.enter_context(nc.sbuf_tensor("mi_" + name, shape, dt))
        w1 = sb("w1", [P, E0, KD, F0])
        w1c = [sb(f"w1c{c}", [P, E0, KD, F0], F32R) for c in range(2)]
        w2 = sb("w2", [P, E0, D])
        b1 = sb("b1", [F0, E0])
        b2 = sb("b2", [E0, D])
        rw = sb("rw", [P, KD, E0])
        rb = sb("rb", [P, E0])
        gvec = sb("gvec", [P, 4, B + 1, D])
        g_front = sb("g_front", [P, 2, D])
        g_back = sb("g_back", [P, D])
        wob = sb("wob", [P, KD, D])
        iota = sb("iota", [P, E0])
        xin = [sb(f"xin{h}", [P, SUB, D]) for h in range(2)]
        oin = [sb(f"oin{h}", [P, SUB, G, HPG * HD]) for h in range(2)]
        st, mv = sb("st", [P, SUB, 6]), sb("mv", [P, SUB, 2])
        ve, rstd, mhalf = sb("ve", [P, SUB]), sb("rstd", [P, SUB]), sb("mhalf", [P, SUB])
        xh1, base = sb("xh1", [P, SUB, D]), sb("base", [P, SUB, D])
        x1 = [sb(f"x1{h}", [P, SUB, D]) for h in range(2)]
        xh2 = sb("xh2", [P, SUB, D])
        oT = sb("oT", [P, KD, T])
        hT = [sb(f"hT{h}", [P, KD, T]) for h in range(2)]
        hTc = [[sb(f"hTc{h}{c}", [P, KD, T], F32R) for c in range(2)] for h in range(2)]
        mcur = sb("mcur", [P, 2 * KD])
        act_e = [sb(f"act{e}", [F0, T]) for e in range(E0)]
        acc = sb("acc", [P, SUB, D])
        scaled = sb("scaled", [P, SUB, D])
        x2 = [sb(f"x2{h}", [P, SUB, D]) for h in range(2)]
        lg, mx8, ix = sb("lg", [P, SUB, E0]), sb("mx8", [P, SUB, 8]), sb("ix", [P, SUB, 8], U32)
        ixf, gap, e2 = sb("ixf", [P, SUB, 2]), sb("gap", [P, SUB]), sb("e2", [P, SUB])
        den, wt = sb("den", [P, SUB]), sb("wt", [P, 2, SUB])
        pick = sb("pick", [P, 2, SUB, E0])
        mask = [sb(f"mask{h}", [P, SUB, E0]) for h in range(2)]
        maskT = sb("maskT", [E0, T])
        pb = lambda name, shape: ctx.enter_context(nc.psum_tensor("mi_" + name, shape, F32))
        ps_t = [pb(f"ps_t{k}", [P, T]) for k in range(KD)]
        ps_a = [pb(f"ps_a{k}", [P, 2, D]) for k in range(2)]
        ps_h = [pb(f"ps_h{k}", [P, T]) for k in range(2)]
        ps_f = [pb(f"ps_f{k}", [P, 2, D]) for k in range(2)]
        sem = phase_semaphores(nc, ctx, "mi_")
        const_in, always = sem("const_in"), sem("always")
        xo_in = [sem(f"xo_in{h}") for h in range(2)]
        var_done, rstd_done, xh1_done, base_done = sem("var_done"), sem("rstd_done"), sem("xh1_done"), sem("base_done")
        wob_done, x1_done, xh2_done, mask_done = sem("wob_done"), sem("x1_done"), sem("xh2_done"), sem("mask_done")
        tro_done, oT_done, proj_done, trx_done = sem("tro_done"), sem("oT_done"), sem("proj_done"), sem("trx_done")
        hT_done, lg_done, lg_read, gap_done, e2_done = sem("hT_done"), sem("lg_done"), sem("lg_read"), sem("gap_done"), sem("e2_done")
        mT_done, mT_out, b2_done, acc_set = sem("mT_done"), sem("mT_out"), sem("b2_done"), sem("acc_set")
        w1_cut, upper_done, hT_cut = sem("w1_cut"), sem("upper_done"), sem("hT_cut")
        h_done, act_done, f_done, f_read = sem("h_done"), sem("act_done"), sem("f_done"), sem("f_read")
        scaled_done, x2_done = sem("scaled_done"), sem("x2_done")
        x2_stored = [sem(f"x2_stored{h}") for h in range(2)]
        NCONST = 16 * (6 + 4 * B + 4 + 1)

        with nc.Block() as block:
            @block.sync
            def _(sp):
                sp.dma_start(iota[:, :], x["iota"][:, 0:E0]).then_inc(const_in, 16)
                sp.dma_start(rb[:, :], x["rb"].partition_broadcast(P)).then_inc(const_in, 16)
                sp.dma_start(rw[:, :, :], x["rw"].rearrange("(k p) e -> p k e", p=P)).then_inc(const_in, 16)
                sp.dma_start(b1[:, :], x["b1T"]).then_inc(const_in, 16)
                sp.dma_start(b2[:, :], x["b2"]).then_inc(const_in, 16)
                for n, r in enumerate((R_GCA, R_GSA, R_GRZ, R_GB0)):
                    for b in range(B + 1):
                        sp.dma_start(gvec[:, n, b, :], d["rows"][r, min(b, B - 1), :].partition_broadcast(P)).then_inc(const_in, 16)

                def load(n, b, c, h):
                    sp.dma_start(xin[h][:, :, :], x["x"][ds(n * T, T), :].rearrange("(s p) f -> p s f", p=P)).then_inc(xo_in[h], 16)
                    for g in range(G):
                        sp.dma_start(oin[h][:, :, g, :], d["o"][ds((b * G + g) * CPB + c + 1, 1), :, :, :].rearrange("n p s f -> p (n s) f")).then_inc(xo_in[h], 16)

                load(0, 0, 0, 0)
                sp.dma_start(w1[:, :, :, :], x["w1"].rearrange("e (k p) f -> p e k f", p=P)).then_inc(const_in, 16)
                load(1, 0, 1, 1)
                sp.dma_start(w2[:, :, :], x["w2"].rearrange("e f n -> f e n")).then_inc(const_in, 16)
                with sp.Fori(0, B) as b:
                    for c in range(CPB):
                        i = b * CPB + c
                        sp.wait_ge(base_done, i + 1)
                        wait_alone(sp, tro_done, i + 1, always)
                        load((i + 2) % NCH, (b + (c + 2) // CPB) % B, (c + 2) % CPB, c % 2)
                        wait_alone(sp, x2_done, i + 1, always)
                        sp.dma_start(d["x2"][ds(i * T, T), :].rearrange("(s p) f -> p s f", p=P), x2[c % 2][:, :, :]).then_inc(x2_stored[c % 2], 16)
                for h in range(2):
                    sp.wait_ge(x2_stored[h], 16 * NCH // 2)
                    sp.wait_ge(xo_in[h], 80 * (NCH // 2 + 1))

            @block.gpsimd
            def _(pool):
                def rsqrt(k):
                    pool.wait_ge(var_done, k + 1)
                    nc.gpsimd.tensor_tensor(rstd[:, :], ve[:, :], mhalf[:, :], ALU.pow).then_inc(rstd_done, 1)

                def residual_base(n, m, h):
                    over = lambda v: v.unsqueeze(1).to_broadcast([P, SUB, D])
                    pool.wait_ge(xh1_done, n + 1)
                    pool.wait_ge(x1_done, n)
                    nc.gpsimd.tensor_tensor(base[:, :, :], xh1[:, :, :], over(g_front[:, 0, :]), ALU.mult)
                    pool.drain()
                    nc.gpsimd.tensor_tensor(base[:, :, :], base[:, :, :], over(g_front[:, 1, :]), ALU.add)
                    pool.drain()
                    nc.gpsimd.tensor_tensor(base[:, :, :], base[:, :, :], xin[h][:, :, :], ALU.add).then_inc(base_done, 1)

                def front_vectors(b):
                    pool.drain()
                    nc.gpsimd.tensor_copy(g_front[:, :, :], gvec[:, 0:2, ds(b, 1), :].rearrange("p n b f -> p (n b) f"))
                    pool.drain()

                def lower_rows(n, h):
                    pool.wait_ge(upper_done, n + 1)
                    lower_part(nc.gpsimd, hTc[h][1][:, :, :], hT[h][:, :, :], hTc[h][0][:, :, :]).then_inc(hT_cut, 1)

                nc.gpsimd.memset(mhalf[:, :], -0.5)
                pool.sem_inc(always, 1)
                pool.wait_ge(const_in, NCONST)
                front_vectors(0)
                rsqrt(0)
                residual_base(0, 0, 0)
                rsqrt(1)
                lower_rows(0, 0)
                rsqrt(2)
                residual_base(1, 0, 1)
                with pool.Fori(0, B) as b:
                    for c in range(CPB):
                        i = b * CPB + c
                        rsqrt(2 * i + 3)
                        if c == CPB - 2:
                            front_vectors(b + 1)
                        rsqrt(2 * i + 4)
                        lower_rows(i + 1, (c + 1) % 2)
                        residual_base(i + 2, b * 2 + (c + 2) // 2, c % 2)
                        pool.wait_ge(scaled_done, i + 1)
                        pool.wait_ge(x2_stored[c % 2], 16 * (b * 2 + c // 2))
                        nc.gpsimd.tensor_tensor(x2[c % 2][:, :, :], scaled[:, :, :], x1[c % 2][:, :, :], ALU.add).then_inc(x2_done, 1)

            @block.vector
            def _(dve):
                def variance(src):
                    for s in range(SUB):
                        nc.vector.bn_stats(st[:, s, :], src[:, s, :])
                    dve.drain()
                    for s in range(SUB):
                        nc.vector.bn_aggr(mv[:, s, :], st[:, s, :])
                    dve.drain()
                    nc.vector.tensor_scalar(ve[:, :], mv[:, :, 1], EPS, None, ALU.add).then_inc(var_done, 1)

                def scale_rows(dst, src, k):
                    dve.wait_ge(rstd_done, k + 1)
                    for s in range(SUB):
                        last = nc.vector.tensor_scalar(dst[:, s, :], src[:, s, :], mv[:, s, 0:1], rstd[:, s:s + 1], ALU.subtract, ALU.mult)
                    return last

                def first_variance(m, h):
                    dve.wait_ge(xo_in[h], 80 * m + 80)
                    variance(xin[h])

                def first_norm(n, h):
                    dve.wait_ge(base_done, n)
                    scale_rows(xh1, xin[h], 2 * n).then_inc(xh1_done, 1)

                def output_weights(b):
                    dve.drain()
                    nc.vector.tensor_tensor(wob[:, :, :], keep["wo"][:, :, :], gvec[:, 2, ds(b, 1), :].to_broadcast([P, KD, D]), ALU.mult).then_inc(wob_done, 1)

                def first_residual(n, h):
                    dve.wait_ge(base_done, n + 1)
                    dve.wait_ge(proj_done, n + 1)
                    for k in range(2):
                        last = nc.vector.tensor_tensor(x1[h][:, 2 * k:2 * k + 2, :], base[:, 2 * k:2 * k + 2, :], ps_a[k][:, :, :], ALU.add)
                    last.then_inc(x1_done, 1)
                    dve.drain()
                    variance(x1[h])

                def second_norm(n, h):
                    dve.wait_ge(trx_done, n)
                    scale_rows(xh2, x1[h], 2 * n + 1).then_inc(xh2_done, 1)

                def best_two(n):
                    dve.wait_ge(lg_done, n + 1)
                    nc.vector.tensor_tensor(lg[:, :, :], ps_a[0][:, 0, 0:SUB * E0].rearrange("p (s e) -> p s e", s=SUB),
                                            rb[:, :].unsqueeze(1).to_broadcast([P, SUB, E0]), ALU.add).then_inc(lg_read, 1)
                    dve.drain()
                    for s in range(SUB):
                        nc.vector.max(mx8[:, s, :], lg[:, s, :])
                    dve.drain()
                    for s in range(SUB):
                        nc.vector.max_index(ix[:, s, :], mx8[:, s, :], lg[:, s, :])
                    nc.vector.tensor_tensor(gap[:, :], mx8[:, :, 1], mx8[:, :, 0], ALU.subtract).then_inc(gap_done, 1)
                    dve.drain()
                    nc.vector.tensor_copy(ixf[:, :, :], ix[:, :, 0:2])

                def routing(n, h):
                    dve.wait_ge(e2_done, n + 1)
                    nc.vector.tensor_scalar(den[:, :], e2[:, :], 1.0, None, ALU.add)
                    dve.drain()
                    nc.vector.reciprocal(wt[:, 0, :], den[:, :])
                    dve.drain()
                    nc.vector.tensor_tensor(wt[:, 1, :], e2[:, :], wt[:, 0, :], ALU.mult)
                    dve.drain()
                    for k in range(2):
                        for s in range(SUB):
                            nc.vector.tensor_scalar(pick[:, k, s, :], iota[:, :], ixf[:, s, k:k + 1], wt[:, k, s:s + 1], ALU.is_equal, ALU.mult)
                    dve.drain()
                    nc.vector.tensor_tensor(mask[h][:, :, :], pick[:, 0, :, :], pick[:, 1, :, :], ALU.add).then_inc(mask_done, 1)

                def upper_rows(n, h):
                    dve.wait_ge(hT_done, n + 1)
                    upper_part(nc.vector, hTc[h][0][:, :, :], hT[h][:, :, :]).then_inc(upper_done, 1)

                def add_expert(i, h, e):
                    for pair in range(2):
                        dve.wait_ge(f_done, (i * E0 + e) * 2 + pair + 1)
                        for j in range(2):
                            s = 2 * pair + j
                            last = nc.vector.scalar_tensor_tensor(acc[:, s, :], ps_f[pair][:, j, :], mask[h][:, s, e:e + 1], acc[:, s, :], ALU.mult, ALU.add)
                        last.then_inc(f_read, 1)
                    dve.drain()

                dve.wait_ge(const_in, NCONST)
                output_weights(0)
                first_variance(0, 0)
                first_norm(0, 0)
                first_residual(0, 0)
                second_norm(0, 0)
                best_two(0)
                routing(0, 0)
                upper_rows(0, 0)
                w1f, w1u, w1l = (t[:, :, :, :].rearrange("p e k f -> p (e k f)") for t in (w1, *w1c))
                upper_part(nc.vector, w1u, w1f)
                dve.drain()
                lower_part(nc.vector, w1l, w1f, w1u).then_inc(w1_cut, 1)
                first_variance(0, 1)
                first_norm(1, 1)
                with dve.Fori(0, B) as b:
                    dve.drain()
                    nc.vector.tensor_copy(g_back[:, :], gvec[:, 3, ds(b, 1), :].rearrange("p b f -> p (b f)"))
                    for c in range(CPB):
                        i = b * CPB + c
                        h, h1 = c % 2, (c + 1) % 2
                        if c == CPB - 1:
                            output_weights(b + 1)
                        dve.wait_ge(acc_set, i + 1)
                        add_expert(i, h, 0)
                        first_residual(i + 1, h1)
                        add_expert(i, h, 1)
                        second_norm(i + 1, h1)
                        add_expert(i, h, 2)
                        add_expert(i, h, 3)
                        first_variance(b * 2 + (c + 2) // 2, h)
                        add_expert(i, h, 4)
                        upper_rows(i + 1, h1)
                        first_norm(i + 2, h)
                        add_expert(i, h, 5)
                        best_two(i + 1)
                        add_expert(i, h, 6)
                        routing(i + 1, h1)
                        add_expert(i, h, 7)
                        dve.wait_ge(x2_done, i)
                        nc.vector.tensor_tensor(scaled[:, :, :], acc[:, :, :], g_back[:, :].unsqueeze(1).to_broadcast([P, SUB, D]), ALU.mult).then_inc(scaled_done, 1)

            @block.scalar
            def _(act):
                def attention_rows(n):
                    act.wait_ge(tro_done, n + 1)
                    for k in range(KD):
                        last = nc.scalar.activation(oT[:, k, :], ps_t[k][:, :], ACT.Identity, bias=keep["bvT"][:, k:k + 1])
                    last.then_inc(oT_done, 1)

                def modulate(n, h):
                    act.wait_ge(trx_done, n + 1)
                    for k in range(KD):
                        last = nc.scalar.activation(hT[h][:, k, :], ps_t[k][:, :], ACT.Identity, scale=mcur[:, k:k + 1], bias=mcur[:, KD + k:KD + k + 1])
                    last.then_inc(hT_done, 1)

                def batch_vectors(b):
                    act.drain()
                    nc.scalar.copy(mcur[:, :], keep["mfm"][:, 2 * KD:4 * KD, ds(b, 1)].rearrange("p m b -> p (m b)"))
                    act.drain()

                def second_weight(n):
                    act.wait_ge(gap_done, n + 1)
                    nc.scalar.activation(e2[:, :], gap[:, :], ACT.Exp).then_inc(e2_done, 1)

                def hidden(i, e):
                    act.wait_ge(h_done, i * E0 + e + 1)
                    nc.scalar.activation(act_e[e][:, :], ps_h[e % 2][:, :], ACT.Gelu, bias=b1[:, e:e + 1]).then_inc(act_done, 1)

                act.wait_ge(const_in, NCONST)
                batch_vectors(0)
                attention_rows(0)
                modulate(0, 0)
                second_weight(0)
                hidden(0, 0)
                hidden(0, 1)
                with act.Fori(0, B) as b:
                    for c in range(CPB):
                        i = b * CPB + c
                        act.wait_ge(mT_done, i + 1)
                        nc.scalar.copy(maskT[:, :], ps_a[1][0:E0, :, :].rearrange("p a f -> p (a f)")).then_inc(mT_out, 1)
                        attention_rows(i + 1)
                        act.wait_ge(x2_done, i)
                        act.wait_ge(b2_done, i + 1)
                        for k in range(2):
                            last = nc.scalar.copy(acc[:, 2 * k:2 * k + 2, :], ps_a[k][:, :, :])
                        last.then_inc(acc_set, 1)
                        for e in range(2, 6):
                            hidden(i, e)
                        if c == CPB - 1:
                            batch_vectors(b + 1)
                        modulate(i + 1, (c + 1) % 2)
                        hidden(i, 6)
                        hidden(i, 7)
                        second_weight(i + 1)
                        hidden(i + 1, 0)
                        hidden(i + 1, 1)

            @block.tensor
            def _(pe):
                def attention_rows(n, m, h):
                    pe.wait_ge(xo_in[h], 80 * m + 80)
                    pe.wait_ge(hT_done, n)
                    for k in range(KD):
                        for s in range(SUB):
                            o_tok = oin[h][:, s, :, :].rearrange("p g c -> p (g c)")[:, k * P:(k + 1) * P]
                            last = nc.tensor.transpose(ps_t[k][:, s * P:(s + 1) * P], o_tok, keep["ident"][:, :])
                    last.then_inc(tro_done, 1)

                def project(n, b1st):
                    pe.wait_ge(oT_done, n + 1)
                    pe.wait_ge(wob_done, b1st + 1)
                    pe.wait_ge(acc_set, n)
                    for s in range(SUB):
                        for k in range(KD):
                            last = nc.tensor.matmul(ps_a[s // 2][:, s % 2, :], oT[:, k, s * P:(s + 1) * P], wob[:, k, :], start=(k == 0), stop=(k == KD - 1))
                    last.then_inc(proj_done, 1)

                def normed_rows(n):
                    pe.wait_ge(xh2_done, n + 1)
                    for k in range(KD):
                        for s in range(SUB):
                            last = nc.tensor.transpose(ps_t[k][:, s * P:(s + 1) * P], xh2[:, s, k * P:(k + 1) * P], keep["ident"][:, :])
                    last.then_inc(trx_done, 1)

                def router(n, h):
                    pe.wait_ge(hT_done, n + 1)
                    for s in range(SUB):
                        for k in range(KD):
                            last = nc.tensor.matmul(ps_a[0][:, 0, s * E0:(s + 1) * E0], hT[h][:, k, s * P:(s + 1) * P], rw[:, k, :], start=(k == 0), stop=(k == KD - 1))
                    last.then_inc(lg_done, 1)

                def up(i, h, e):
                    if e > 0:
                        pe.wait_ge(act_done, i * E0 + e - 1)
                    elif not isinstance(i, int):
                        pe.wait_ge(act_done, i * E0 - 1)
                    if e == 0:
                        pe.wait_ge(hT_cut, i + 1)
                    for k in range(KD):
                        for n, (a, r) in enumerate(CUTS):
                            last = nc.tensor.matmul(ps_h[e % 2][:, :], w1c[a][:, e, k, :], hTc[h][r][:, k, :],
                                                    start=(k == 0 and n == 0), stop=(k == KD - 1 and n == 2))
                    last.then_inc(h_done, 1)

                def down(i, e):
                    pe.wait_ge(act_done, i * E0 + e + 1)
                    for pair in range(2):
                        pe.wait_ge(f_read, (i * E0 + e) * 2 + (pair - 1 if e else 0))
                        for j in range(2):
                            s = 2 * pair + j
                            last = nc.tensor.matmul(ps_f[pair][:, j, :], act_e[e][:, s * P:(s + 1) * P], w2[:, e, :], start=True, stop=True)
                        last.then_inc(f_done, 1)

                pe.wait_ge(const_in, NCONST)
                attention_rows(0, 0, 0)
                project(0, 0)
                normed_rows(0)
                router(0, 0)
                pe.wait_ge(w1_cut, 1)
                up(0, 0, 0)
                up(0, 0, 1)
                with pe.Fori(0, B) as b:
                    for c in range(CPB):
                        i = b * CPB + c
                        h, h1, m1 = c % 2, (c + 1) % 2, b * 2 + (c + 1) // 2
                        pe.wait_ge(mask_done, i + 1)
                        for s in range(SUB):
                            last = nc.tensor.transpose(ps_a[1][0:E0, s // 2, (s % 2) * P:(s % 2 + 1) * P], mask[h][:, s, :], keep["ident"][:, :])
                        last.then_inc(mT_done, 1)
                        attention_rows(i + 1, m1, h1)
                        pe.wait_ge(mT_out, i + 1)
                        for s in range(SUB):
                            last = nc.tensor.matmul(ps_a[s // 2][:, s % 2, :], maskT[:, s * P:(s + 1) * P], b2[:, :], start=True, stop=True)
                        last.then_inc(b2_done, 1)
                        up(i, h, 2)
                        down(i, 0)
                        up(i, h, 3)
                        project(i + 1, b + (c + 1) // CPB)
                        down(i, 1)
                        up(i, h, 4)
                        down(i, 2)
                        up(i, h, 5)
                        normed_rows(i + 1)
                        down(i, 3)
                        up(i, h, 6)
                        down(i, 4)
                        up(i, h, 7)
                        pe.wait_ge(x1_done, i + 2)
                        router(i + 1, h1)
                        down(i, 5)
                        up(i + 1, h1, 0)
                        down(i, 6)
                        up(i + 1, h1, 1)
                        down(i, 7)


A_TURN = (["cum1", "seg1", "xT1", "ct4", "ct0", "ct1"]
          + ["gT0", "cum2", "seg2", "xT2", "out0", "ct2", "ct3", "dt"]
          + ["gT1", "cum3", "seg3", "xT3", "out1", "z0", "z1"]
          + ["gT2", "cum0", "seg0", "xT0", "out2", "z2", "z3", "gT3", "uT0", "uT1", "out3"])
A_FIRST = ["uT0", "uT1", "ct4", "ct0", "ct1", "ct2", "ct3", "dt", "z0", "z1", "z2", "z3", "vT0", "vT1", "cum0", "seg0", "xT0"]
A_BANKS = 4
A_POS = {n: len(A_FIRST) + k for k, n in enumerate(A_TURN)}
A_PRE = {n: k for k, n in enumerate(A_FIRST)}
CONV_GROUPS = [(4, 0), (1, 2), (3,)]


def scan_phase(nc, x, d, keep):
    ctx = ExitStack()
    with ctx:
        sb = lambda name, shape, dt=F32: ctx.enter_context(nc.sbuf_tensor("sc_" + name, shape, dt))
        ZX = 2 * DI + 2 * NS + NH
        RT = (2 * DI + 2 * NS) // P
        KO = DI // P
        win = sb("win", [P, KD, ZX])
        wout = sb("wout", [P, KO, D])
        upper, lower, ones = sb("upper", [P, P]), sb("lower", [P, P]), sb("ones", [P, P])
        dtb, a_neg, dvec = sb("dtb", [P, NH]), sb("a_neg", [P, NH]), sb("dvec", [P, NH])
        conv_w, conv_b = sb("conv_w", [P, CTL, TAPS]), sb("conv_b", [P, CTL])
        nw, nb, rms = sb("nw", [P, KD]), sb("nb", [P, KD]), sb("rms", [P, KO])
        gvec = sb("gvec", [P, 3, B + 1, D])
        g_front, g_back = sb("g_front", [P, 2, D]), sb("g_back", [P, D])
        ss, rs = sb("ss", [P, 16]), sb("rs", [P, 16])
        mhalf = sb("mhalf", [P, 16])
        xin = [sb(f"xin{h}", [P, SUB, D]) for h in range(4)]
        xh, uh = sb("xh", [P, SUB, D]), sb("uh", [P, SUB, D])
        st, mv = sb("st", [P, SUB, 6]), sb("mv", [P, SUB, 2])
        ve, rstd = sb("ve", [P, SUB]), sb("rstd", [P, SUB])
        uT = [sb(f"uT{h}", [P, KD, T]) for h in range(2)]
        CW = T + TAPS - 1
        xc_flat = [sb(f"xc{h}", [P, CTL * CW]) for h in range(2)]
        xc = [t[:, :].rearrange("p (c w) -> p c w", w=CW) for t in xc_flat]
        cv = sb("cv", [P, CTL, T])
        xs = [sb(f"xs{h}", [P, CTL, T]) for h in range(2)]
        cT = [sb(f"cT{h}", [NS, T]) for h in range(2)]
        sz = [sb(f"sz{h}", [P, SUB, DI]) for h in range(2)]
        dtr = sb("dtr", [P, SUB, NH])
        vraw, nabs, ez = sb("vraw", [P, SUB, NH]), sb("nabs", [P, SUB, NH]), sb("ez", [P, SUB, NH])
        zq, zw, zp = sb("zq", [P, SUB, NH]), sb("zw", [P, SUB, NH]), sb("zp", [P, SUB, NH])
        dts = [sb(f"dts{h}", [P, SUB, NH]) for h in range(2)]
        dA = [sb(f"dA{h}", [P, SUB, NH]) for h in range(2)]
        two = lambda name, shape: [sb(f"{name}{h}", shape) for h in range(2)]
        segm, decay, att = two("segm", [P, NH, P]), two("decay", [P, NH, P]), two("att", [P, NH, P])
        sm, btok, ex = two("sm", [P, P]), two("btok", [P, NS]), two("ex", [P, 3, NH])
        xtok, xdt, xde, xd = two("xtok", [P, NH, HP]), two("xdt", [P, NH, HP]), two("xde", [P, NH, HP]), two("xd", [P, NH, HP])
        ysum, g, gT = two("ysum", [P, NH, HP]), two("g", [P, DI]), two("gT", [P, KO, P])
        junk, ssq, osb = sb("junk", [P, DI]), sb("ssq", [P, SUB]), sb("osb", [P, SUB, D])
        state = sb("state", [NS, NH, HP])
        pb = lambda name: ctx.enter_context(nc.psum_tensor("sc_" + name, [P, 512], F32))
        ps_a = [pb(f"ps_a{k}") for k in range(A_BANKS)]
        ps_sc, ps_in, ps_y, ps_st = pb("ps_sc"), pb("ps_in"), pb("ps_y"), pb("ps_st")
        wbank = [ps_sc, ps_in, ps_y, ps_st]
        raw = xc_flat[0][:, 0:RT * D].rearrange("p (t f) -> p t f", f=D)
        raw_sq = xc_flat[1][:, 0:RT * D].rearrange("p (t f) -> p t f", f=D)
        cvf = cv[:, :, :].rearrange("p c t -> p (c t)")
        raw_o = cvf[:, 0:KD * DI].rearrange("p (o f) -> p o f", f=DI)
        raw_dt = cvf[0:NH, KD * DI:KD * DI + D]
        uhf = uh[:, :, :].rearrange("p s f -> p (s f)")
        raw_o_sq = uhf[:, 0:KD * DI].rearrange("p (o f) -> p o f", f=DI)
        raw_dt_sq = xh[0:NH, 0, :]

        sem = phase_semaphores(nc, ctx, "sc_")
        const_in, always, setup_v, setup_p, setup_a = sem("const_in"), sem("always"), sem("setup_v"), sem("setup_p"), sem("setup_a")
        w_done, w_read = sem("w_done"), sem("w_read")
        x_in = [sem(f"x_in{h}") for h in range(4)]
        x_stored = [sem(f"x_stored{h}") for h in range(4)]
        cT_in = [sem(f"cT_in{h}") for h in range(2)]
        a_done, a_out = sem("a_done"), sem("a_out")
        var_done, rstd_done, xh_done, h_done, uh_done = sem("var_done"), sem("rstd_done"), sem("xh_done"), sem("h_done"), sem("uh_done")
        conv_done, silu_done, nabs_done, ez_done, dA_done = sem("conv_done"), sem("silu_done"), sem("nabs_done"), sem("ez_done"), sem("dA_done")
        seg_set, xdt_done, att_done, xde_done, g_done = sem("seg_set"), sem("xdt_done"), sem("att_done"), sem("xde_done"), sem("g_done")
        sc_done, sc_read, in_done, in_read = sem("sc_done"), sem("sc_read"), sem("in_done"), sem("in_read")
        y_done, y_read, st_done, state_set = sem("y_done"), sem("y_read"), sem("st_done"), sem("state_set")
        ssq_done, osc_done, x3_done = sem("ssq_done"), sem("osc_done"), sem("x3_done")

        NCONST = 16 * (15 + 3 * (B + 1))
        TURN = len(A_TURN)
        RND = 7
        over_h = lambda v: v.unsqueeze(2).to_broadcast([P, NH, P])
        over_s = lambda v: v.unsqueeze(1).to_broadcast([P, SUB, D])

        def place(i, name):
            pos = A_PRE[name] if i is None else A_POS[name]
            return (pos if i is None else i * TURN + pos), pos % A_BANKS

        with nc.Block() as block:
            @block.sync
            def _(sp):
                sp.dma_start(raw, x["inw"][0:RT * P, :].rearrange("(t p) f -> p t f", p=P)).then_inc(const_in, 16)
                sp.dma_start(raw_dt, x["inw"][RT * P:ZX, :]).then_inc(const_in, 16)
                sp.dma_start(raw_o, x["outw"].rearrange("(o p) f -> p o f", p=P)).then_inc(const_in, 16)
                for t, name in ((upper, "upper"), (lower, "lower"), (ones, "ones_f"), (conv_b, "conv_b"), (nw, "xnw"), (nb, "xnb"), (rms, "rmsw")):
                    sp.dma_start(t[:, :], x[name]).then_inc(const_in, 16)
                sp.dma_start(conv_w[:, :, :], x["conv_w"]).then_inc(const_in, 16)
                for t, name in ((dtb, "dt_bias"), (a_neg, "A_log"), (dvec, "Dskip")):
                    sp.dma_start(t[:, :], x[name].partition_broadcast(P)).then_inc(const_in, 16)
                sp.dma_start(mhalf[:, :], x["mhalf"]).then_inc(const_in, 16)
                for n, r in enumerate((R_CA1, R_SA1, R_GA1)):
                    for b in range(B + 1):
                        sp.dma_start(gvec[:, n, b, :], d["rows"][r, min(b, B - 1), :].partition_broadcast(P)).then_inc(const_in, 16)

                def load(n, h):
                    sp.dma_start(xin[h][:, :, :], d["x2"][ds(n * T, T), :].rearrange("(s p) f -> p s f", p=P)).then_inc(x_in[h], 16)

                def move_c(n, m, h):
                    wait_alone(sp, silu_done, 3 * n + 1, always)
                    sp.dma_start(cT[h][:, :], xs[h][NS:2 * NS, CTL - 1, :]).then_inc(cT_in[h], 16)

                for n in range(3):
                    load(n, n)
                move_c(0, 0, 0)
                with sp.Fori(0, B) as b:
                    for c in range(CPB):
                        i = b * CPB + c
                        if c == 0:
                            wait_alone(sp, x_stored[3], 16 * b, always)
                        else:
                            wait_alone(sp, x_stored[c - 1], 16 * (b + 1), always)
                        load((i + 3) % NCH, (c + 3) % 4)
                        move_c(i + 1, b * 2 + (c + 1) // 2, (c + 1) % 2)
                        wait_alone(sp, x3_done, i + 1, always)
                        sp.dma_start(d["x3"][ds(i * T, T), :].rearrange("(s p) f -> p s f", p=P), xin[c][:, :, :]).then_inc(x_stored[c], 16)
                for h in range(4):
                    sp.wait_ge(x_stored[h], 16 * B)
                    sp.wait_ge(x_in[h], 16 * (B + (h < 3)))
                sp.wait_ge(cT_in[0], 16 * (NCH // 2 + 1))
                sp.wait_ge(cT_in[1], 16 * NCH // 2)

            @block.gpsimd
            def _(pool):
                def rsqrt(k):
                    pool.wait_ge(var_done, k + 1)
                    nc.gpsimd.tensor_tensor(rstd[:, :], ve[:, :], mhalf[:, 0:SUB], ALU.pow).then_inc(rstd_done, 1)

                def scale_shift(n):
                    pool.wait_ge(xh_done, n + 1)
                    nc.gpsimd.tensor_tensor(xh[:, :, :], xh[:, :, :], over_s(g_front[:, 0, :]), ALU.mult)
                    pool.drain()
                    nc.gpsimd.tensor_tensor(xh[:, :, :], xh[:, :, :], over_s(g_front[:, 1, :]), ALU.add).then_inc(h_done, 1)

                def front_vectors(b):
                    pool.drain()
                    nc.gpsimd.tensor_copy(g_front[:, :, :], gvec[:, 0:2, ds(b, 1), :].rearrange("p n b f -> p (n b) f"))
                    pool.drain()

                def segment_mask(n, h, s):
                    pool.wait_ge(dA_done, n + 1)
                    nc.gpsimd.tensor_tensor(segm[s % 2][:, :, :], lower[:, :].unsqueeze(1).to_broadcast([P, NH, P]),
                                            over_h(dA[h][:, s, :]), ALU.mult).then_inc(seg_set, 1)

                def weigh_inputs(i, s):
                    pool.wait_ge(xdt_done, i * SUB + s + 1)
                    nc.gpsimd.tensor_tensor(xde[s % 2][:, :, :], xdt[s % 2][:, :, :], over_h(ex[s % 2][:, 1, :]), ALU.mult).then_inc(xde_done, 1)
                    nc.gpsimd.tensor_tensor(xd[s % 2][:, :, :], xtok[s % 2][:, :, :], over_h(dvec[:, :]), ALU.mult)

                def gate(i, h, s):
                    pool.drain()
                    pool.wait_ge(y_read, i * SUB + s + 1)
                    nc.gpsimd.tensor_tensor(xd[s % 2][:, :, :], xd[s % 2][:, :, :], ysum[s % 2][:, :, :], ALU.add)
                    pool.drain()
                    nc.gpsimd.tensor_tensor(g[s % 2][:, :], xd[s % 2][:, :, :].rearrange("p h c -> p (h c)"), sz[h][:, s, :], ALU.mult).then_inc(g_done, 1)

                pool.sem_inc(always, 1)
                pool.wait_ge(const_in, NCONST)
                pool.wait_ge(setup_v, 1)
                nc.gpsimd.tensor_tensor(rs[:, :], ss[:, :], mhalf[:, :], ALU.pow).then_inc(setup_p, 1)
                front_vectors(0)
                for n in range(2):
                    rsqrt(2 * n)
                    scale_shift(n)
                    rsqrt(2 * n + 1)
                segment_mask(0, 0, 0)
                segment_mask(0, 0, 1)
                weigh_inputs(0, 0)
                with pool.Fori(0, B) as b:
                    for c in range(CPB):
                        i = b * CPB + c
                        h = c % 2
                        for s in range(SUB):
                            gate(i, h, s)
                            if s < 2:
                                segment_mask(i, h, s + 2)
                            elif s == 3:
                                segment_mask(i + 1, 1 - h, 1)
                            weigh_inputs(i + (s + 1) // SUB, (s + 1) % SUB)
                            if s == 0:
                                if c == 2:
                                    front_vectors(b + 1)
                                rsqrt(4 + 3 * i)
                                scale_shift(i + 2)
                            if s == 2:
                                segment_mask(i + 1, 1 - h, 0)
                                rsqrt(5 + 3 * i)
                        rsqrt(6 + 3 * i)
                        pool.wait_ge(osc_done, i + 1)
                        nc.gpsimd.tensor_tensor(xin[c][:, :, :], xin[c][:, :, :], osb[:, :, :], ALU.add).then_inc(x3_done, 1)

            @block.vector
            def _(dve):
                def variance(src):
                    for s in range(SUB):
                        nc.vector.bn_stats(st[:, s, :], src[:, s, :])
                    dve.drain()
                    for s in range(SUB):
                        nc.vector.bn_aggr(mv[:, s, :], st[:, s, :])
                    dve.drain()
                    nc.vector.tensor_scalar(ve[:, :], mv[:, :, 1], EPS, None, ALU.add).then_inc(var_done, 1)

                def scale_rows(dst, src, k):
                    dve.wait_ge(rstd_done, k + 1)
                    for s in range(SUB):
                        last = nc.vector.tensor_scalar(dst[:, s, :], src[:, s, :], mv[:, s, 0:1], rstd[:, s:s + 1], ALU.subtract, ALU.mult)
                    return last

                def first_variance(m, h):
                    dve.wait_ge(x_in[h], 16 * m + 16)
                    variance(xin[h])

                def first_norm(h, k):
                    scale_rows(xh, xin[h], k).then_inc(xh_done, 1)

                def second_variance(n):
                    dve.wait_ge(h_done, n + 1)
                    variance(xh)

                def second_norm(k):
                    scale_rows(uh, xh, k).then_inc(uh_done, 1)

                def convolve(i, h, grp, fresh):
                    if grp == 0:
                        if fresh:
                            nc.vector.memset(xc[h][:, :, 0:TAPS - 1], 0.0)
                        else:
                            nc.vector.tensor_copy(xc[h][:, :, 0:TAPS - 1], xc[1 - h][:, :, T:CW])
                    cts = CONV_GROUPS[grp]
                    for k in range(TAPS - 1):
                        dve.drain()
                        for ct in cts:
                            if k == 0:
                                dve.wait_ge(a_out, place(i, f"ct{ct}")[0] + 1)
                            last = nc.vector.scalar_tensor_tensor(cv[:, ct, :], xc[h][:, ct, k:k + T], conv_w[:, ct, k:k + 1], cv[:, ct, :], ALU.mult, ALU.add)
                    last.then_inc(conv_done, 1)

                def step_sizes(i, n):
                    dve.wait_ge(a_out, place(i, "dt")[0] + 1)
                    nc.vector.tensor_tensor(vraw[:, :, :], dtr[:, :, :], dtb[:, :].unsqueeze(1).to_broadcast([P, SUB, NH]), ALU.add)
                    dve.drain()
                    nc.vector.scalar_tensor_tensor(nabs[:, :, :], vraw[:, :, :], -1.0, vraw[:, :, :], ALU.mult, ALU.min).then_inc(nabs_done, 1)

                def softplus(n, h):
                    dve.wait_ge(ez_done, n + 1)
                    nc.vector.tensor_scalar(zp[:, :, :], ez[:, :, :], 2.0, None, ALU.add)
                    dve.drain()
                    nc.vector.reciprocal(zq[:, :, :], zp[:, :, :])
                    dve.drain()
                    nc.vector.tensor_tensor(zq[:, :, :], zq[:, :, :], ez[:, :, :], ALU.mult)
                    dve.drain()
                    nc.vector.tensor_tensor(zw[:, :, :], zq[:, :, :], zq[:, :, :], ALU.mult)
                    dve.drain()
                    nc.vector.tensor_scalar(zp[:, :, :], zw[:, :, :], 1.0 / 17, None, ALU.mult)
                    for k in range(15, 1, -2):
                        dve.drain()
                        nc.vector.scalar_tensor_tensor(zp[:, :, :], zp[:, :, :], 1.0 / k, zw[:, :, :], ALU.add, ALU.mult)
                    dve.drain()
                    nc.vector.scalar_tensor_tensor(zp[:, :, :], zp[:, :, :], 1.0, zq[:, :, :], ALU.add, ALU.mult)
                    nc.vector.tensor_scalar(vraw[:, :, :], vraw[:, :, :], 0.0, None, ALU.max)
                    dve.drain()
                    nc.vector.scalar_tensor_tensor(dts[h][:, :, :], zp[:, :, :], 2.0, vraw[:, :, :], ALU.mult, ALU.add)
                    dve.drain()
                    nc.vector.tensor_tensor(dA[h][:, :, :], dts[h][:, :, :], a_neg[:, :].unsqueeze(1).to_broadcast([P, SUB, NH]), ALU.mult).then_inc(dA_done, 1)

                def attention_weights(turn, i, h, s):
                    r = s % 2
                    dve.wait_ge(sc_done, i * SUB + s + 1)
                    nc.vector.tensor_tensor(sm[r][:, :], ps_sc[:, 0:P], upper[:, :], ALU.mult)
                    nc.vector.tensor_copy(btok[r][:, :], ps_sc[:, P:P + NS]).then_inc(sc_read, 1)
                    dve.wait_ge(a_out, place(turn, f"xT{s}")[0] + 1)
                    nc.vector.tensor_tensor(xdt[r][:, :, :], xtok[r][:, :, :], over_h(dts[h][:, s, :]), ALU.mult).then_inc(xdt_done, 1)
                    dve.drain()
                    nc.vector.tensor_tensor(att[r][:, :, :], decay[r][:, :, :], sm[r][:, :].unsqueeze(1).to_broadcast([P, NH, P]), ALU.mult).then_inc(att_done, 1)

                def outputs_and_state(i, s):
                    r = s % 2
                    heads = lambda t: t[:, :].rearrange("p (h c) -> p h c", h=NH)
                    dve.wait_ge(in_done, i * SUB + s + 1)
                    nc.vector.tensor_tensor(ysum[r][:, :, :], heads(ps_in), over_h(ex[r][:, 0, :]), ALU.mult).then_inc(in_read, 1)
                    dve.drain()
                    dve.wait_ge(y_done, i * SUB + s + 1)
                    nc.vector.tensor_tensor(ysum[r][:, :, :], ysum[r][:, :, :], heads(ps_y), ALU.add).then_inc(y_read, 1)
                    dve.wait_ge(st_done, i * SUB + s + 1)
                    for k in range(NH):
                        last = nc.vector.scalar_tensor_tensor(state[:, k, :], state[:, k, :], ex[r][0:NS, 2, k:k + 1], ps_st[0:NS, k * HP:(k + 1) * HP], ALU.mult, ALU.add)
                    last.then_inc(state_set, 1)

                dve.wait_ge(const_in, NCONST)
                nc.vector.memset(ss[:, :], 1.0)
                nc.vector.tensor_tensor(raw_sq, raw, raw, ALU.mult)
                nc.vector.tensor_tensor(raw_o_sq, raw_o, raw_o, ALU.mult)
                nc.vector.tensor_tensor(raw_dt_sq, raw_dt, raw_dt, ALU.mult)
                dve.drain()
                nc.vector.tensor_reduce(ss[:, 0:RT], raw_sq, AX.X, ALU.add)
                nc.vector.tensor_reduce(ss[:, RT:RT + KD], raw_o_sq, AX.X, ALU.add)
                nc.vector.tensor_reduce(ss[0:NH, RT + KD:RT + KD + 1], raw_dt_sq, AX.X, ALU.add)
                dve.drain()
                nc.vector.tensor_scalar(ss[:, :], ss[:, :], 1e-12, None, ALU.max).then_inc(setup_v, 1)
                dve.wait_ge(setup_p, 1)
                scale = float(D) ** -0.5
                nc.vector.scalar_tensor_tensor(raw, raw, scale, rs[:, 0:RT].unsqueeze(2).to_broadcast([P, RT, D]), ALU.mult, ALU.mult)
                nc.vector.tensor_tensor(raw_o, raw_o, rs[:, RT:RT + KD].unsqueeze(2).to_broadcast([P, KD, DI]), ALU.mult)
                nc.vector.tensor_scalar(raw_dt, raw_dt, rs[0:NH, RT + KD:RT + KD + 1], scale, ALU.mult, ALU.mult).then_inc(setup_v, 1)
                for r in range(RND):
                    dve.wait_ge(w_done, r + 1)
                    bank = wbank[r % 4]
                    if r < 4:
                        last = nc.vector.tensor_copy(win[:, :, 2 * r * P:(2 * r + 2) * P], bank[:, :].rearrange("p (k c) -> p k c", k=KD))
                    elif r == 4:
                        nc.vector.tensor_copy(win[:, :, 8 * P:9 * P], bank[:, 0:KD * P].rearrange("p (k c) -> p k c", k=KD))
                        last = nc.vector.tensor_copy(win[:, :, RT * P:ZX], bank[:, KD * P:KD * P + KD * NH].rearrange("p (k c) -> p k c", k=KD))
                    else:
                        for j in range(2):
                            ko = 2 * (r - 5) + j
                            last = nc.vector.tensor_scalar(wout[:, ko, :], bank[:, j * D:(j + 1) * D], rms[:, ko:ko + 1], None, ALU.mult)
                    last.then_inc(w_read, 1)
                dve.wait_ge(setup_a, 1)
                nc.vector.tensor_scalar(a_neg[:, :], a_neg[:, :], -1.0, None, ALU.mult)
                for n in range(2):
                    first_variance(0, n)
                    first_norm(n, 2 * n)
                    second_variance(n)
                    if n == 1:
                        dve.wait_ge(a_done, place(None, "uT1")[0] + 1)
                    second_norm(2 * n + 1)
                for grp in range(3):
                    convolve(None, 0, grp, True)
                step_sizes(None, 0)
                softplus(0, 0)
                attention_weights(None, 0, 0, 0)
                with dve.Fori(0, B) as b:
                    dve.drain()
                    nc.vector.memset(state[:, :, :], 0.0).then_inc(state_set, 1)
                    nc.vector.tensor_copy(g_back[:, :], gvec[:, 2, ds(b, 1), :].rearrange("p b f -> p (b f)"))
                    for c in range(CPB):
                        i = b * CPB + c
                        h = c % 2
                        for s in range(SUB):
                            outputs_and_state(i, s)
                            if s == 2:
                                softplus(i + 1, 1 - h)
                            if s == 3:
                                second_norm(5 + 3 * i)
                            if s + 1 < SUB:
                                attention_weights(i, i, h, s + 1)
                            else:
                                attention_weights(i, i + 1, 1 - h, 0)
                            if s == 0:
                                first_variance(b + (c + 2) // 4, (c + 2) % 4)
                            if s < 3:
                                convolve(i, 1 - h, s, c == CPB - 1)
                            if s == 0:
                                first_norm((c + 2) % 4, 4 + 3 * i)
                            if s == 1:
                                step_sizes(i, i + 1)
                            if s == 2:
                                second_variance(i + 2)
                        dve.wait_ge(ssq_done, i * SUB + SUB)
                        nc.vector.tensor_scalar(ve[:, :], ssq[:, :], 1.0 / DI, EPS, ALU.mult, ALU.add).then_inc(var_done, 1)
                        dve.wait_ge(rstd_done, 7 + 3 * i)
                        dve.wait_ge(a_out, place(i, "out3")[0] + 1)
                        for s in range(SUB):
                            last = nc.vector.scalar_tensor_tensor(osb[:, s, :], osb[:, s, :], rstd[:, s:s + 1], g_back[:, :], ALU.mult, ALU.mult)
                        last.then_inc(osc_done, 1)

            @block.scalar
            def _(act):
                def take(i, name):
                    k, bank = place(i, name)
                    act.wait_ge(a_done, k + 1)
                    return ps_a[bank]

                def decays(i, s):
                    bank = take(i, f"cum{s}")
                    nc.scalar.activation(ex[s % 2][:, :, :], bank[:, 0:3 * NH].rearrange("p (a h) -> p a h", a=3), ACT.Exp).then_inc(a_out, 1)
                    bank = take(i, f"seg{s}")
                    nc.scalar.activation(decay[s % 2][:, :, :], bank[:, :].rearrange("p (h c) -> p h c", h=NH), ACT.Exp).then_inc(a_out, 1)

                def token_inputs(i, s):
                    bank = take(i, f"xT{s}")
                    nc.scalar.copy(xtok[s % 2][:, :, :], bank[:, :].rearrange("p (h c) -> p h c", h=NH)).then_inc(a_out, 1)

                def conv_inputs(i, h, ct):
                    bank = take(i, f"ct{ct}")
                    nc.scalar.activation(cv[:, ct, :], bank[:, :], ACT.Identity, scale=conv_w[:, ct, TAPS - 1:TAPS], bias=conv_b[:, ct:ct + 1])
                    nc.scalar.copy(xc[h][:, ct, TAPS - 1:CW], bank[:, :]).then_inc(a_out, 1)

                def steps(i):
                    bank = take(i, "dt")
                    nc.scalar.copy(dtr[:, :, :], bank[:, 0:SUB * NH].rearrange("p (s h) -> p s h", s=SUB)).then_inc(a_out, 1)

                def gates(i, h, s):
                    bank = take(i, f"z{s}")
                    nc.scalar.activation(sz[h][:, s, :], bank[:, :], ACT.Silu).then_inc(a_out, 1)

                def conv_silu(n, h, grp):
                    act.wait_ge(conv_done, 3 * n + grp + 1)
                    for ct in CONV_GROUPS[grp]:
                        last = nc.scalar.activation(xs[h][:, ct, :], cv[:, ct, :], ACT.Silu)
                    last.then_inc(silu_done, 1)

                def step_exp(n):
                    act.wait_ge(nabs_done, n + 1)
                    nc.scalar.activation(ez[:, :, :], nabs[:, :, :], ACT.Exp).then_inc(ez_done, 1)

                def normed(i, h, names):
                    for k in range(KD):
                        bank = take(i, names[k])
                        nc.scalar.activation(uT[h][:, k, :], bank[:, :], ACT.Identity, scale=nw[:, k:k + 1], bias=nb[:, k:k + 1]).then_inc(a_out, 1)

                def gated_columns(i, s):
                    bank = take(i, f"gT{s}")
                    nc.scalar.copy(gT[s % 2][:, :, :], bank[:, :].rearrange("p (k c) -> p k c", k=KO)).then_inc(a_out, 1)
                    nc.scalar.activation(junk[:, :], g[s % 2][:, :], ACT.Square, accum_out=ssq[:, s:s + 1]).then_inc(ssq_done, 1)

                def projected(i, s):
                    bank = take(i, f"out{s}")
                    if s == 0:
                        act.wait_ge(x3_done, i)
                    nc.scalar.copy(osb[:, s, :], bank[:, 0:D]).then_inc(a_out, 1)

                act.wait_ge(const_in, NCONST)
                nc.scalar.activation(a_neg[:, :], a_neg[:, :], ACT.Exp).then_inc(setup_a, 1)
                normed(None, 0, ("uT0", "uT1"))
                act.wait_ge(w_read, RND)
                for ct in (4, 0, 1, 2, 3):
                    conv_inputs(None, 0, ct)
                steps(None)
                for s in range(SUB):
                    gates(None, 0, s)
                for grp in range(3):
                    conv_silu(0, 0, grp)
                step_exp(0)
                normed(None, 1, ("vT0", "vT1"))
                decays(None, 0)
                token_inputs(None, 0)
                with act.Fori(0, B) as b:
                    for c in range(CPB):
                        i = b * CPB + c
                        h = c % 2
                        decays(i, 1)
                        token_inputs(i, 1)
                        for ct in (4, 0, 1):
                            conv_inputs(i, 1 - h, ct)
                        gated_columns(i, 0)
                        decays(i, 2)
                        token_inputs(i, 2)
                        projected(i, 0)
                        conv_inputs(i, 1 - h, 2)
                        conv_inputs(i, 1 - h, 3)
                        steps(i)
                        step_exp(i + 1)
                        gated_columns(i, 1)
                        decays(i, 3)
                        token_inputs(i, 3)
                        projected(i, 1)
                        gates(i, 1 - h, 0)
                        gates(i, 1 - h, 1)
                        conv_silu(i + 1, 1 - h, 0)
                        conv_silu(i + 1, 1 - h, 1)
                        gated_columns(i, 2)
                        conv_silu(i + 1, 1 - h, 2)
                        decays(i, 0)
                        token_inputs(i, 0)
                        projected(i, 2)
                        gates(i, 1 - h, 2)
                        gates(i, 1 - h, 3)
                        gated_columns(i, 3)
                        normed(i, h, ("uT0", "uT1"))
                        projected(i, 3)

            @block.tensor
            def _(pe):
                def into(i, name):
                    k, bank = place(i, name)
                    if i is not None:
                        pe.wait_ge(a_out, k - A_BANKS + 1)
                    elif k >= A_BANKS:
                        pe.wait_ge(a_out, k - A_BANKS + 1)
                    return ps_a[bank]

                def normed(i, n, names):
                    pe.wait_ge(uh_done, n + 1)
                    for k in range(KD):
                        bank = into(i, names[k])
                        for s in range(SUB):
                            last = nc.tensor.transpose(bank[:, s * P:(s + 1) * P], uh[:, s, k * P:(k + 1) * P], keep["ident"][:, :])
                        last.then_inc(a_done, 1)

                def conv_inputs(i, h, ct):
                    bank = into(i, f"ct{ct}")
                    for k in range(KD):
                        last = nc.tensor.matmul(bank[:, :], win[:, k, DI + ct * P:DI + (ct + 1) * P], uT[h][:, k, :], start=(k == 0), stop=(k == KD - 1))
                    last.then_inc(a_done, 1)

                def gates(i, h, s):
                    bank = into(i, f"z{s}")
                    for k in range(KD):
                        last = nc.tensor.matmul(bank[:, :], uT[h][:, k, s * P:(s + 1) * P], win[:, k, 0:DI], start=(k == 0), stop=(k == KD - 1))
                    last.then_inc(a_done, 1)

                def steps(i, h):
                    bank = into(i, "dt")
                    for s in range(SUB):
                        for k in range(KD):
                            last = nc.tensor.matmul(bank[:, s * NH:(s + 1) * NH], uT[h][:, k, s * P:(s + 1) * P], win[:, k, RT * P:ZX], start=(k == 0), stop=(k == KD - 1))
                    last.then_inc(a_done, 1)

                def decays(turn, i, h, s):
                    bank = into(turn, f"cum{s}")
                    pe.wait_ge(dA_done, i + 1)
                    for k, m in enumerate((upper, lower, ones)):
                        last = nc.tensor.matmul(bank[:, k * NH:(k + 1) * NH], m[:, :], dA[h][:, s, :], start=True, stop=True)
                    last.then_inc(a_done, 1)
                    bank = into(turn, f"seg{s}")
                    pe.wait_ge(seg_set, i * SUB + s + 1)
                    for k in range(NH):
                        last = nc.tensor.matmul(bank[:, k * P:(k + 1) * P], segm[s % 2][:, k, :], upper[:, :], start=True, stop=True)
                    last.then_inc(a_done, 1)

                def scores(i, h, m, s):
                    cols = slice(s * P, (s + 1) * P)
                    if s == 0:
                        pe.wait_ge(cT_in[h], 16 * m + 16)
                    pe.wait_ge(sc_read, i * SUB + s)
                    nc.tensor.matmul(ps_sc[:, 0:P], xs[h][0:NS, CTL - 1, cols], cT[h][:, cols], start=True, stop=True)
                    nc.tensor.transpose(ps_sc[:, P:P + NS], xs[h][0:NS, CTL - 1, cols], keep["ident"][0:NS, 0:NS]).then_inc(sc_done, 1)

                def token_inputs(turn, i, h, s):
                    bank = into(turn, f"xT{s}")
                    if s == 0:
                        pe.wait_ge(silu_done, 3 * i + 3)
                    for k in range(NH):
                        last = nc.tensor.transpose(bank[:, k * P:(k + 1) * P], xs[h][:, k, s * P:(s + 1) * P], keep["ident"][:, :])
                    last.then_inc(a_done, 1)

                def outputs(i, b, c, h, s):
                    pe.wait_ge(state_set, b * (SUB * CPB + 1) + c * SUB + s + 1)
                    pe.wait_ge(in_read, i * SUB + s)
                    nc.tensor.matmul(ps_in[:, :], cT[h][:, s * P:(s + 1) * P], state[:, :, :].rearrange("n h c -> n (h c)"), start=True, stop=True).then_inc(in_done, 1)
                    pe.wait_ge(att_done, i * SUB + s + 1)
                    pe.wait_ge(y_read, i * SUB + s)
                    for k in range(NH):
                        last = nc.tensor.matmul(ps_y[:, k * HP:(k + 1) * HP], att[s % 2][:, k, :], xdt[s % 2][:, k, :], start=True, stop=True)
                    last.then_inc(y_done, 1)
                    pe.wait_ge(xde_done, i * SUB + s + 1)
                    nc.tensor.matmul(ps_st[0:NS, :], btok[s % 2][:, :], xde[s % 2][:, :, :].rearrange("p h c -> p (h c)"), start=True, stop=True).then_inc(st_done, 1)

                def gated_columns(i, s):
                    bank = into(i, f"gT{s}")
                    pe.wait_ge(g_done, i * SUB + s + 1)
                    for k in range(KO):
                        last = nc.tensor.transpose(bank[:, k * P:(k + 1) * P], g[s % 2][:, k * P:(k + 1) * P], keep["ident"][:, :])
                    last.then_inc(a_done, 1)

                def project(i, s):
                    bank = into(i, f"out{s}")
                    pe.wait_ge(a_out, place(i, f"gT{s}")[0] + 1)
                    for k in range(KO):
                        last = nc.tensor.matmul(bank[:, 0:D], gT[s % 2][:, k, :], wout[:, k, :], start=(k == 0), stop=(k == KO - 1))
                    last.then_inc(a_done, 1)

                pe.wait_ge(const_in, NCONST)
                pe.wait_ge(setup_v, 2)
                for r in range(RND):
                    if r >= 4:
                        pe.wait_ge(w_read, r - 3)
                    bank = wbank[r % 4]
                    if r < 4:
                        for k in range(KD):
                            for t in range(2):
                                last = nc.tensor.transpose(bank[:, (2 * k + t) * P:(2 * k + t + 1) * P], raw[:, 2 * r + t, k * P:(k + 1) * P], keep["ident"][:, :])
                    elif r == 4:
                        for k in range(KD):
                            nc.tensor.transpose(bank[:, k * P:(k + 1) * P], raw[:, 8, k * P:(k + 1) * P], keep["ident"][:, :])
                        for k in range(KD):
                            last = nc.tensor.transpose(bank[:, KD * P + k * NH:KD * P + (k + 1) * NH], raw_dt[:, k * P:(k + 1) * P], keep["ident"][0:NH, 0:NH])
                    else:
                        for j in range(2):
                            for o in range(KD):
                                ko = 2 * (r - 5) + j
                                last = nc.tensor.transpose(bank[:, (2 * j + o) * P:(2 * j + o + 1) * P], raw_o[:, o, ko * P:(ko + 1) * P], keep["ident"][:, :])
                    last.then_inc(w_done, 1)
                pe.wait_ge(w_read, RND)
                normed(None, 0, ("uT0", "uT1"))
                pe.wait_ge(a_out, place(None, "uT1")[0] + 1)
                for ct in (4, 0, 1, 2, 3):
                    conv_inputs(None, 0, ct)
                steps(None, 0)
                for s in range(SUB):
                    gates(None, 0, s)
                normed(None, 1, ("vT0", "vT1"))
                decays(None, 0, 0, 0)
                scores(0, 0, 0, 0)
                token_inputs(None, 0, 0, 0)
                with pe.Fori(0, B) as b:
                    for c in range(CPB):
                        i = b * CPB + c
                        h, m = c % 2, b * 2 + c // 2
                        fill = ("ct4", "ct0", "ct1"), ("ct2", "ct3", "dt"), ("z0", "z1"), ("z2", "z3")
                        for s in range(SUB):
                            outputs(i, b, c, h, s)
                            if s > 0:
                                gated_columns(i, s - 1)
                            nxt = (i, h, m, s + 1) if s + 1 < SUB else (i + 1, 1 - h, b * 2 + (c + 1) // 2, 0)
                            decays(i, nxt[0], nxt[1], nxt[3])
                            scores(*nxt)
                            token_inputs(i, nxt[0], nxt[1], nxt[3])
                            if s > 0:
                                project(i, s - 1)
                            for name in fill[s]:
                                if name[0] == "c":
                                    conv_inputs(i, 1 - h, int(name[2:]))
                                elif name[0] == "z":
                                    gates(i, 1 - h, int(name[1:]))
                                else:
                                    steps(i, 1 - h)
                        gated_columns(i, 3)
                        normed(i, i + 2, ("uT0", "uT1"))
                        project(i, 3)


def route_phase(nc, x, d, keep):
    ctx = ExitStack()
    with ctx:
        sb = lambda name, shape, dt=F32: ctx.enter_context(nc.sbuf_tensor("ro_" + name, shape, dt))
        wg, bg, iota = sb("wg", [P, KD, E1]), sb("bg", [P, E1]), sb("iota", [P, E1])
        upper_in, ones_in = sb("upper_in", [P, P]), sb("ones_in", [P, P])
        upper, ones = sb("upper", [P, P], BF16), sb("ones", [P, P], BF16)
        gvec, g_cur, g_res = sb("gvec", [P, 3, B, D]), sb("g_cur", [P, 2, D]), sb("g_res", [P, D])
        token = sb("token", [P, N // P], U32)
        mhalf = sb("mhalf", [P, SUB])
        xin = [sb(f"xin{c}", [P, SUB, D]) for c in range(CPB)]
        row = [sb(f"row{c}", [P, SUB, ROW]) for c in range(CPB)]
        rows, residual, factor = ([t[:, :, k * D:(k + 1) * D] for t in row] for k in range(3))
        gate = [sb(f"gate{c}", [P, SUB]) for c in range(CPB)]
        slot, away, target = ([sb(f"{name}{c}", [P, SUB], U32) for c in range(CPB)] for name in ("slot", "away", "target"))
        st, mv = sb("st", [P, SUB, 6]), sb("mv", [P, SUB, 2])
        ve, rstd = sb("ve", [P, SUB]), sb("rstd", [P, SUB])
        xg = sb("xg", [P, SUB, D])
        rT = sb("rT", [P, KD, T])
        lg, mx8, ix = sb("lg", [P, SUB, E1]), sb("mx8", [P, SUB, 8]), sb("ix", [P, SUB, 8], U32)
        ixf, low, ex = sb("ixf", [P, SUB]), sb("low", [P, SUB, E1]), sb("ex", [P, SUB, E1])
        den = sb("den", [P, SUB])
        pick, count = sb("pick", [P, SUB, E1], BF16), sb("count", [P, E1])
        upto, pos = sb("upto", [P, SUB, E1]), sb("pos", [P, SUB])
        pb = lambda name, shape: ctx.enter_context(nc.psum_tensor("ro_" + name, shape, F32))
        ps_t = [pb(f"ps_t{k}", [P, T]) for k in range(KD)]
        ps_l, ps_c = pb("ps_l", [P, SUB, E1]), pb("ps_c", [P, SUB + 1, E1])
        sem = phase_semaphores(nc, ctx, "ro_")
        const_in, always, cast_done = sem("const_in"), sem("always"), sem("cast_done")
        x_in = [sem(f"x_in{c}") for c in range(CPB)]
        var_done, rstd_done, rows_done = sem("var_done"), sem("rstd_done"), sem("rows_done")
        tr_done, rT_done, lg_done = sem("tr_done"), sem("rT_done"), sem("lg_done")
        low_done, ex_done, pick_done, c_done = sem("low_done"), sem("ex_done"), sem("pick_done"), sem("c_done")
        gate_done, slot_done, rest_done = sem("gate_done"), sem("slot_done"), sem("rest_done")
        moved = [sem(f"moved{c}") for c in range(CPB)]
        NCONST = 16 * (6 + 3 * B)
        AHEAD = 2

        def ahead(b, c):
            return b + (c + AHEAD) // CPB, (c + AHEAD) % CPB

        with nc.Block() as block:
            @block.sync
            def _(sp):
                def load(n, c):
                    sp.dma_start(xin[c][:, :, :], d["x3"][ds(n * T, T), :].rearrange("(s p) f -> p s f", p=P)).then_inc(x_in[c], 16)

                load(0, 0)
                for n, r in enumerate((R_CB1, R_SB1, R_GB1)):
                    for b in range(B):
                        sp.dma_start(gvec[:, n, b, :], d["rows"][r, b, :].partition_broadcast(P)).then_inc(const_in, 16)
                    if n == 1:
                        load(1, 1)
                sp.dma_start(wg[:, :, :], x["wg"].rearrange("(k p) e -> p k e", p=P)).then_inc(const_in, 16)
                sp.dma_start(bg[:, :], x["bg"].partition_broadcast(P)).then_inc(const_in, 16)
                for t, name in ((iota, "iota"), (upper_in, "upper"), (ones_in, "ones_f")):
                    sp.dma_start(t[:, :], x[name]).then_inc(const_in, 16)
                sp.dma_start(token[:, :], x["token"].bitcast(U32)).then_inc(const_in, 16)
                for c in range(2, CPB):
                    load(c, c)
                with sp.Fori(0, B - 1) as b:
                    for c in range(CPB):
                        wait_alone(sp, rest_done, b * CPB + c + 1, always)
                        load((b + 1) * CPB + c, c)

            @block.gpsimd
            def _(pool):
                def inverse(n):
                    pool.wait_ge(var_done, n + 1)
                    nc.gpsimd.tensor_tensor(rstd[:, :], ve[:, :], mhalf[:, :], ALU.pow).then_inc(rstd_done, 1)

                def scatter(n, c):
                    pool.wait_ge(rest_done, n + 1)
                    nc.gpsimd.tensor_tensor(target[c][:, :], slot[c][:, :], away[c][:, :], ALU.add)
                    pool.drain()
                    for s in range(SUB):
                        nc.gpsimd.indirect_dma_start(d["buf"], bass.IndirectOffsetOnAxis(ap=target[c][:, s:s + 1], axis=0),
                                                     row[c][:, s, :], None, bounds_check=N - 1, oob_is_err=False).then_inc(moved[c], 16)

                def batch(b, last):
                    for c in range(CPB):
                        if c + AHEAD < CPB or not last:
                            inverse(b * CPB + c + AHEAD)
                        scatter(b * CPB + c, c)

                nc.gpsimd.memset(mhalf[:, :], -0.5)
                pool.sem_inc(always, 1)
                pool.drain()
                for n in range(AHEAD):
                    inverse(n)
                with pool.Fori(0, B - 1) as b:
                    batch(b, False)
                batch(B - 1, True)
                for c in range(CPB):
                    pool.wait_ge(moved[c], 16 * SUB * B)

            @block.vector
            def _(dve):
                def batch_vectors(b):
                    nc.vector.tensor_copy(g_cur[:, :, :], gvec[:, 0:2, ds(b, 1), :].rearrange("p n b f -> p (n b) f"))

                def variance(b, c):
                    dve.wait_ge(x_in[c], 16 * b + 16)
                    for s in range(SUB):
                        nc.vector.bn_stats(st[:, s, :], xin[c][:, s, :])
                    dve.drain()
                    for s in range(SUB):
                        nc.vector.bn_aggr(mv[:, s, :], st[:, s, :])
                    dve.drain()
                    nc.vector.tensor_scalar(ve[:, :], mv[:, :, 1], EPS, None, ALU.add).then_inc(var_done, 1)

                def normalise(n, b, c):
                    for s in range(SUB):
                        nc.vector.scalar_tensor_tensor(xg[:, s, :], xin[c][:, s, :], mv[:, s, 0:1], g_cur[:, 0, :], ALU.subtract, ALU.mult)
                    dve.drain()
                    dve.wait_ge(rstd_done, n + 1)
                    dve.wait_ge(moved[c], 16 * SUB * b)
                    for s in range(SUB):
                        last = nc.vector.scalar_tensor_tensor(rows[c][:, s, :], xg[:, s, :], rstd[:, s:s + 1], g_cur[:, 1, :], ALU.mult, ALU.add)
                    last.then_inc(rows_done, 1)

                def best(n):
                    dve.wait_ge(lg_done, n + 1)
                    nc.vector.tensor_tensor(lg[:, :, :], ps_l[:, :, :], bg[:, :].unsqueeze(1).to_broadcast([P, SUB, E1]), ALU.add)
                    dve.drain()
                    for s in range(SUB):
                        nc.vector.max(mx8[:, s, :], lg[:, s, :])
                    dve.drain()
                    for s in range(SUB):
                        nc.vector.max_index(ix[:, s, :], mx8[:, s, :], lg[:, s, :])
                    nc.vector.tensor_tensor(low[:, :, :], lg[:, :, :], mx8[:, :, 0:1].to_broadcast([P, SUB, E1]), ALU.subtract).then_inc(low_done, 1)
                    dve.drain()
                    nc.vector.tensor_copy(ixf[:, :], ix[:, :, 0])
                    dve.drain()
                    nc.vector.tensor_tensor(pick[:, :, :], iota[:, :].unsqueeze(1).to_broadcast([P, SUB, E1]),
                                            ixf[:, :].unsqueeze(2).to_broadcast([P, SUB, E1]), ALU.is_equal).then_inc(pick_done, 1)

                def places(n, c):
                    dve.wait_ge(ex_done, n + 1)
                    nc.vector.tensor_reduce(den[:, :], ex[:, :, :], AX.X, ALU.add)
                    dve.drain()
                    nc.vector.reciprocal(gate[c][:, :], den[:, :]).then_inc(gate_done, 1)
                    dve.wait_ge(c_done, n + 1)
                    nc.vector.tensor_tensor(upto[:, :, :], ps_c[:, 0:SUB, :], count[:, :].unsqueeze(1).to_broadcast([P, SUB, E1]), ALU.add)
                    dve.drain()
                    nc.vector.tensor_tensor(count[:, :], count[:, :], ps_c[:, SUB, :], ALU.add)
                    nc.vector.tensor_tensor(upto[:, :, :], upto[:, :, :], pick[:, :, :], ALU.mult)
                    dve.drain()
                    nc.vector.tensor_reduce(pos[:, :], upto[:, :, :], AX.X, ALU.add)
                    dve.drain()
                    nc.vector.tensor_copy(row[c][:, :, 3 * D:ROW].bitcast(U32).rearrange("p s o -> p (s o)"), token[:, ds(n * SUB, SUB)])
                    nc.vector.tensor_scalar(away[c][:, :], pos[:, :], float(CAP), float(2 * N), ALU.is_ge, ALU.mult)
                    nc.vector.scalar_tensor_tensor(slot[c][:, :], ixf[:, :], float(CAP), pos[:, :], ALU.mult, ALU.add).then_inc(slot_done, 1)

                def batch(b, last):
                    for c in range(CPB):
                        n = b * CPB + c
                        more = c + AHEAD < CPB or not last
                        if c + AHEAD == CPB and more:
                            batch_vectors(b + 1)
                        if more:
                            variance(*ahead(b, c))
                        best(n)
                        if more:
                            normalise(n + AHEAD, *ahead(b, c))
                        places(n, c)

                nc.vector.memset(count[:, :], -1.0)
                variance(0, 0)
                dve.wait_ge(const_in, NCONST)
                batch_vectors(0)
                nc.vector.tensor_copy(upper[:, :], upper_in[:, :])
                nc.vector.tensor_copy(ones[:, :], ones_in[:, :]).then_inc(cast_done, 1)
                dve.drain()
                normalise(0, 0, 0)
                for n in range(1, AHEAD):
                    dve.drain()
                    variance(0, n)
                    dve.drain()
                    normalise(n, 0, n)
                with dve.Fori(0, B - 1) as b:
                    batch(b, False)
                batch(B - 1, True)

            @block.scalar
            def _(act):
                def columns(n):
                    act.wait_ge(tr_done, n + 1)
                    for k in range(KD):
                        last = nc.scalar.copy(rT[:, k, :], ps_t[k][:, :])
                    last.then_inc(rT_done, 1)

                def rest(n, c):
                    act.wait_ge(gate_done, n + 1)
                    for s in range(SUB):
                        nc.scalar.activation(factor[c][:, s, :], g_res[:, :], ACT.Copy, scale=gate[c][:, s:s + 1])
                    act.wait_ge(slot_done, n + 1)
                    nc.scalar.copy(residual[c], xin[c][:, :, :]).then_inc(rest_done, 1)

                def batch(b, last):
                    act.drain()
                    nc.scalar.copy(g_res[:, :], gvec[:, 2, ds(b, 1), :].rearrange("p b f -> p (b f)"))
                    act.drain()
                    for c in range(CPB):
                        n = b * CPB + c
                        act.wait_ge(low_done, n + 1)
                        nc.scalar.activation(ex[:, :, :], low[:, :, :], ACT.Exp).then_inc(ex_done, 1)
                        if c < CPB - 1 or not last:
                            columns(n + 1)
                        rest(n, c)

                act.wait_ge(const_in, NCONST)
                columns(0)
                with act.Fori(0, B - 1) as b:
                    batch(b, False)
                batch(B - 1, True)

            @block.tensor
            def _(pe):
                def columns(n, c):
                    pe.wait_ge(rows_done, n + 1)
                    for k in range(KD):
                        for s in range(SUB):
                            last = nc.tensor.transpose(ps_t[k][:, s * P:(s + 1) * P], rows[c][:, s, k * P:(k + 1) * P], keep["ident"][:, :])
                    last.then_inc(tr_done, 1)

                def logits(n):
                    pe.wait_ge(rT_done, n + 1)
                    for s in range(SUB):
                        for k in range(KD):
                            last = nc.tensor.matmul(ps_l[:, s, :], rT[:, k, s * P:(s + 1) * P], wg[:, k, :], start=(k == 0), stop=(k == KD - 1))
                    last.then_inc(lg_done, 1)

                def counts(n):
                    pe.wait_ge(pick_done, n + 1)
                    for s in range(SUB + 1):
                        for s2 in range(min(s + 1, SUB)):
                            last = nc.tensor.matmul(ps_c[:, s, :], (upper if s2 == s else ones)[:, :], pick[:, s2, :],
                                                    start=(s2 == 0), stop=(s2 == min(s, SUB - 1)))
                    last.then_inc(c_done, 1)

                def batch(b, last):
                    for c in range(CPB):
                        logits(b * CPB + c)
                        if c < CPB - 1 or not last:
                            columns(b * CPB + c + 1, (c + 1) % CPB)
                        counts(b * CPB + c)

                pe.wait_ge(const_in, NCONST)
                pe.wait_ge(cast_done, 1)
                columns(0, 0)
                with pe.Fori(0, B - 1) as b:
                    batch(b, False)
                batch(B - 1, True)


def expert_phase(nc, x, d, keep):
    ctx = ExitStack()
    with ctx:
        sb = lambda name, shape, dt=F32: ctx.enter_context(nc.sbuf_tensor("ex_" + name, shape, dt))
        FT = F1 // P
        CS = CAP // P
        HB = 4
        two = lambda name, shape: [sb(f"{name}{h}", shape) for h in range(2)]
        cut = lambda name, shape, n=2: [[sb(f"{name}{h}{c}", shape, F32R) for c in range(2)] for h in range(n)]
        w1, w2 = two("w1", [P, KD, F1]), two("w2", [P, FT, D])
        w1c, w2c = cut("w1c", [P, KD, F1]), cut("w2c", [P, FT, D])
        b1, b2 = two("b1", [P, FT]), two("b2", [P, D])
        buf, rest, bTc = two("buf", [P, CS, D]), two("rest", [P, CS, ROW - D]), cut("bTc", [P, KD, CAP])
        hid, hidc = [sb(f"hid{f}", [P, CAP]) for f in range(HB)], cut("hidc", [P, CAP], HB)
        y = two("y", [P, CS, D])
        pb = lambda name, shape: ctx.enter_context(nc.psum_tensor("ex_" + name, shape, F32))
        ps_t = [pb(f"ps_t{k}", [P, CAP]) for k in range(KD)]
        ps_h = [pb(f"ps_h{k}", [P, CAP]) for k in range(2)]
        ps_y = [[pb(f"ps_y{h}{k}", [P, 2, D]) for k in range(2)] for h in range(2)]
        sem = phase_semaphores(nc, ctx, "ex_")
        always = sem("always")
        buf_in = [sem(f"buf_in{h}") for h in range(2)]
        w_in = [sem(f"w_in{h}") for h in range(2)]
        b_in = [sem(f"b_in{h}") for h in range(2)]
        stored = [sem(f"stored{h}") for h in range(2)]
        upper_done, w_cut, tr_done, bT_cut = sem("upper_done"), sem("w_cut"), sem("tr_done"), sem("bT_cut")
        h_done, hid_done, hid_cut, y_done, y_out = sem("h_done"), sem("hid_done"), sem("hid_cut"), sem("y_done"), sem("y_out")
        PAIRS = E1 // 2

        with nc.Block() as block:
            @block.sync
            def _(sp):
                def load_weights(e, h):
                    sp.dma_start(w1[h][:, :, :], x["fw1"][ds(e, 1), :, :].rearrange("e (k p) f -> p (e k) f", p=P)).then_inc(w_in[h], 16)
                    sp.dma_start(w2[h][:, :, :], x["fw2"][ds(e, 1), :, :].rearrange("e (k p) f -> p (e k) f", p=P)).then_inc(w_in[h], 16)

                def load_inputs(e, h):
                    sp.dma_start(buf[h][:, :, :], d["buf"][ds(e * CAP, CAP), 0:D].rearrange("(s p) f -> p s f", p=P)).then_inc(buf_in[h], 16)

                def load_rest(e, h):
                    sp.dma_start(rest[h][:, :, :], d["buf"][ds(e * CAP, CAP), D:ROW].rearrange("(s p) f -> p s f", p=P)).then_inc(b_in[h], 16)
                    sp.dma_start(b1[h][:, :], x["fb1"][ds(e, 1), :, :].rearrange("e p k -> p (e k)")).then_inc(b_in[h], 16)
                    sp.dma_start(b2[h][:, :], x["fb2"][ds(e, 1), :].rearrange("e f -> (e f)").partition_broadcast(P)).then_inc(b_in[h], 16)

                for h in range(2):
                    load_inputs(h, h)
                    load_weights(h, h)
                    load_rest(h, h)
                with sp.Fori(0, PAIRS - 1) as m:
                    for h in range(2):
                        e = m * 2 + h
                        wait_alone(sp, w_cut, e + 1, always)
                        load_weights(e + 2, h)
                        wait_alone(sp, tr_done, e + 1, always)
                        load_inputs(e + 2, h)
                        wait_alone(sp, stored[h], 16 * CS * (m + 1), always)
                        load_rest(e + 2, h)

            @block.gpsimd
            def _(pool):
                def lower_weights(e, h):
                    pool.wait_ge(upper_done, e + 1)
                    lower_part(nc.gpsimd, w1c[h][1][:, :, :], w1[h][:, :, :], w1c[h][0][:, :, :])
                    lower_part(nc.gpsimd, w2c[h][1][:, :, :], w2[h][:, :, :], w2c[h][0][:, :, :]).then_inc(w_cut, 1)

                def results(e, h):
                    pool.wait_ge(y_out, e + 1)
                    nc.gpsimd.tensor_tensor(y[h][:, :, :], y[h][:, :, :], rest[h][:, :, D:2 * D], ALU.mult)
                    pool.drain()
                    nc.gpsimd.tensor_tensor(y[h][:, :, :], y[h][:, :, :], rest[h][:, :, 0:D], ALU.add)
                    pool.drain()
                    for s in range(CS):
                        nc.gpsimd.indirect_dma_start(d["x3"], bass.IndirectOffsetOnAxis(ap=rest[h][:, s, 2 * D:ROW - D].bitcast(U32), axis=0),
                                                     y[h][:, s, :], None, bounds_check=N - 1, oob_is_err=False).then_inc(stored[h], 16)

                lower_weights(0, 0)
                lower_weights(1, 1)
                with pool.Fori(0, PAIRS - 1) as m:
                    for h in range(2):
                        results(m * 2 + h, h)
                        lower_weights(m * 2 + h + 2, h)
                for h in range(2):
                    results(E1 - 2 + h, h)
                for h in range(2):
                    pool.wait_ge(stored[h], 16 * CS * PAIRS)

            @block.vector
            def _(dve):
                def weights(m, h):
                    dve.wait_ge(w_in[h], 32 * m + 32)
                    upper_part(nc.vector, w1c[h][0][:, :, :], w1[h][:, :, :])
                    upper_part(nc.vector, w2c[h][0][:, :, :], w2[h][:, :, :]).then_inc(upper_done, 1)

                def columns(e, h):
                    dve.wait_ge(tr_done, e + 1)
                    for k in range(KD):
                        upper_part(nc.vector, bTc[h][0][:, k, :], ps_t[k][:, :])
                    dve.drain()
                    for k in range(KD):
                        last = lower_part(nc.vector, bTc[h][1][:, k, :], ps_t[k][:, :], bTc[h][0][:, k, :])
                    last.then_inc(bT_cut, 1)

                def hidden(e, f):
                    r = f % HB
                    dve.wait_ge(hid_done, e * FT + f + 1)
                    upper_part(nc.vector, hidc[r][0][:, :], hid[r][:, :])
                    dve.drain()
                    lower_part(nc.vector, hidc[r][1][:, :], hid[r][:, :], hidc[r][0][:, :]).then_inc(hid_cut, 1)

                def sums(e, m, h):
                    dve.wait_ge(y_done, e + 1)
                    dve.wait_ge(b_in[h], 48 * m + 48)
                    dve.wait_ge(stored[h], 16 * CS * m)
                    for k in range(2):
                        last = nc.vector.tensor_tensor(y[h][:, 2 * k:2 * k + 2, :], ps_y[h][k][:, :, :], b2[h][:, :].unsqueeze(1).to_broadcast([P, 2, D]), ALU.add)
                    last.then_inc(y_out, 1)

                def expert(e, m, h, first, last):
                    for f in range(FT):
                        hidden(e, f)
                        if f == 1 and not first:
                            sums(e - 1, m - 1 + h, 1 - h)
                        if f == 2 and not last:
                            weights(m + h, 1 - h)
                        if f == 4 and not last:
                            columns(e + 1, 1 - h)

                dve.sem_inc(always, 1)
                weights(0, 0)
                columns(0, 0)
                expert(0, 0, 0, True, False)
                with dve.Fori(0, PAIRS - 1) as m:
                    expert(m * 2 + 1, m, 1, False, False)
                    expert(m * 2 + 2, m + 1, 0, False, False)
                expert(E1 - 1, PAIRS - 1, 1, False, True)
                sums(E1 - 1, PAIRS - 1, 1)

            @block.scalar
            def _(act):
                with act.Fori(0, PAIRS) as m:
                    for h in range(2):
                        act.wait_ge(b_in[h], 48 * m + 48)
                        for f in range(FT):
                            act.wait_ge(h_done, (m * 2 + h) * FT + f + 1)
                            nc.scalar.activation(hid[f % HB][:, :], ps_h[f % 2][:, :], ACT.Relu, bias=b1[h][:, f:f + 1]).then_inc(hid_done, 1)

            @block.tensor
            def _(pe):
                def columns(e, m, h):
                    pe.wait_ge(buf_in[h], 16 * m + 16)
                    for k in range(KD):
                        for s in range(CS):
                            last = nc.tensor.transpose(ps_t[k][:, s * P:(s + 1) * P], buf[h][:, s, k * P:(k + 1) * P], keep["ident"][:, :])
                    last.then_inc(tr_done, 1)

                def up(e, h, f):
                    if f == 0:
                        pe.wait_ge(bT_cut, e + 1)
                        pe.wait_ge(w_cut, e + 1)
                    for k in range(KD):
                        for n, (a, c) in enumerate(CUTS):
                            last = nc.tensor.matmul(ps_h[f % 2][:, :], w1c[h][a][:, k, f * P:(f + 1) * P], bTc[h][c][:, k, :],
                                                    start=(k == 0 and n == 0), stop=(k == KD - 1 and n == 2))
                    last.then_inc(h_done, 1)

                def down(e, h, f):
                    if f == 0 and not (isinstance(e, int) and e < 2):
                        pe.wait_ge(y_out, e - 1)
                    pe.wait_ge(hid_cut, e * FT + f + 1)
                    for s in range(CS):
                        for n, (a, c) in enumerate(CUTS):
                            last = nc.tensor.matmul(ps_y[h][s // 2][:, s % 2, :], hidc[f % HB][a][:, s * P:(s + 1) * P], w2c[h][c][:, f, :],
                                                    start=(f == 0 and s % 2 == 0 and n == 0), stop=(f == FT - 1 and s % 2 == 1 and n == 2),
                                                    skip_group_check=True)
                    if f == FT - 1:
                        last.then_inc(y_done, 1)

                def expert(e, m, h, last):
                    for f in range(FT):
                        pe.wait_ge(hid_done, e * FT + f + 1)
                        if f + 2 < FT:
                            up(e, h, f + 2)
                        elif not last:
                            up(e + 1, 1 - h, f + 2 - FT)
                        if f == 3 and not last:
                            columns(e + 1, m + h, 1 - h)
                        down(e, h, f)

                columns(0, 0, 0)
                up(0, 0, 0)
                up(0, 0, 1)
                expert(0, 0, 0, False)
                with pe.Fori(0, PAIRS - 1) as m:
                    expert(m * 2 + 1, m, 1, False)
                    expert(m * 2 + 2, m + 1, 0, False)
                expert(E1 - 1, PAIRS - 1, 1, True)


STAGES = [setup_phase, project_phase, attend_phase, mix_phase, scan_phase, route_phase, expert_phase]


def scratch(nc, kind="Internal"):
    shapes = {
        "rows": ([NROWS, B, D], F32),
        "parts": ([G, 3, P, N], BF16),
        "o": ([UNITS * (S // T) + 1, P, SUB, HPG * HD], F32),
        "x2": ([N, D], F32),
        "buf": ([N, ROW], F32),
        "v": ([UNITS, P, KT, HPG * 32], F32),
    }
    return {n: nc.dram_tensor("t_" + n, s, t, kind=kind).ap() for n, (s, t) in shapes.items()}


def program(nc, x, d, stages):
    with ExitStack() as whole, ExitStack() as until_mix, ExitStack() as until_project:
        keep = {}

        def hold(stack, **shapes):
            for n, (shape, dt) in shapes.items():
                keep[n] = stack.enter_context(nc.sbuf_tensor(n, shape, dt))

        hold(whole, ident=([P, P], F32))
        hold(until_mix, wo=([P, KD, D], F32), bvT=([P, KD], F32), mfm=([P, 4 * KD, B + 1], F32))
        hold(until_project, wqk=([P, KD, G, P], F32), wv=([P, KD, D], F32), bqk=([P, G], F32), qscale=([P, 1], F32))
        for stage in stages:
            if stage not in (setup_phase, project_phase):
                until_project.close()
                if stage not in (attend_phase, mix_phase):
                    until_mix.close()
            stage(nc, x, d, keep)


def host_layout(i):
    a = {n: np.asarray(v) for n, v in i.items()}
    o = {"x": a["L0_attn_x"].reshape(N, D)}
    for w in "qkvo":
        o["W" + w + "T"] = a[f"L0_attn_W{w}"].T
        o["A" + w] = a[f"L0_attn_A{w}"]
        o["B" + w + "T"] = a[f"L0_attn_B{w}"].T
    o["bqk"] = np.concatenate([a["L0_attn_bq"].reshape(G, 64).T, a["L0_attn_bk"].reshape(G, 64).T])
    o["bvT"], o["bo"], o["rezero"] = a["L0_attn_bv"].reshape(KD, P).T, a["L0_attn_bo"], a["L0_attn_rezero"]
    for l in range(2):
        o[f"c{l}T"], o[f"wmod{l}"] = a[f"L{l}_c"].T, a[f"L{l}_wmod"]
    o["rw"], o["rb"] = a["L0_ffn_router_w"], a["L0_ffn_router_b"]
    o["w1"], o["b1T"], o["w2"], o["b2"] = a["L0_ffn_W1"], a["L0_ffn_b1"].T, a["L0_ffn_W2"], a["L0_ffn_b2"]
    o["inw"], o["outw"] = a["L1_attn_in_proj_w"], a["L1_attn_out_proj_w"]
    o["conv_w"] = a["L1_attn_conv_w"].reshape(CTL, P, TAPS).transpose(1, 0, 2)
    o["conv_b"] = a["L1_attn_conv_b"].reshape(CTL, P).T
    o["dt_bias"], o["A_log"], o["Dskip"] = a["L1_attn_dt_bias"], a["L1_attn_A_log"], a["L1_attn_D"]
    o["xnw"], o["xnb"] = a["L1_attn_x_norm_w"].reshape(KD, P).T, a["L1_attn_x_norm_b"].reshape(KD, P).T
    o["rmsw"] = a["L1_attn_rms_w"].reshape(DI // P, P).T
    o["wg"], o["bg"] = a["L1_ffn_Wg"], a["L1_ffn_bg"]
    o["fw1"], o["fw2"], o["fb2"] = a["L1_ffn_W1"], a["L1_ffn_W2"], a["L1_ffn_b2"]
    o["fb1"] = a["L1_ffn_b1"].reshape(E1, F1 // P, P).transpose(0, 2, 1)
    o["upper"] = np.triu(np.ones((P, P), np.float32))
    o["lower"] = np.tril(np.ones((P, P), np.float32), -1)
    o["ones_f"] = np.ones((P, P), np.float32)
    o["mhalf"] = np.full((P, 16), -0.5, np.float32)
    o["iota"] = np.tile(np.arange(E1, dtype=np.float32), (P, 1))
    o["token"] = (np.arange(N // P, dtype=np.int32)[None, :] * P + np.arange(P, dtype=np.int32)[:, None])
    o["qscale"] = np.where(np.arange(P) < 64, np.float32(HD ** -0.5), np.float32(1)).astype(np.float32)[:, None]
    bias = (0.5 ** np.arange(H, dtype=np.float32))[:, None] * (np.arange(S, dtype=np.float32) - (S - 1))
    upper = bias.view(np.uint32) & 0xFFFF0000
    lower = (bias - upper.view(np.float32)).view(np.uint32)
    o["alibi"] = (np.stack([upper, lower]) >> 16).astype(np.uint16)
    o["ones"] = np.full((2, HPG, S), 0x3F80, np.uint16)
    o["ident"] = np.eye(P, dtype=np.float32)
    return {n: np.ascontiguousarray(v) for n, v in o.items()}


def kernel(**inputs):
    import concourse.bacc as bacc
    from concourse.bass_utils import run_bass_kernel_spmd

    arrays = {"in_" + n: v for n, v in host_layout(inputs).items()}
    nc = bacc.Bacc("TRN2", target_bir_lowering=False, num_devices=1)
    x = {n[3:]: nc.dram_tensor(n, a.shape, mybir.dt.from_np(a.dtype), kind="ExternalInput").ap() for n, a in arrays.items()}
    out = nc.dram_tensor("out", [N, D], F32, kind="ExternalOutput").ap()
    program(nc, x, {**scratch(nc), "x3": out}, STAGES)
    r = run_bass_kernel_spmd(nc, [arrays], core_ids=[0])
    return r.results[0]["out"].reshape(B, S, D)
```
